# Optimizing a Trainium2 kernel written in Bass

```python
import numpy as np
import jax
import jax.numpy as jnp

def _softmax(x, axis=-1):
    return jax.nn.softmax(x, axis=axis)

def _gelu(x):
    return jax.nn.gelu(x, approximate=True)

def _silu(x):
    return jax.nn.silu(x)

def _sigmoid(x):
    return jax.nn.sigmoid(x)

def _layernorm(x, axis=-1, eps=1e-05):
    m = jnp.mean(x, axis=axis, keepdims=True)
    v = jnp.var(x, axis=axis, keepdims=True)
    return (x - m) / jnp.sqrt(v + eps)

def _scatter_add(tgt, idx, src, axis=0):
    return tgt.at[idx].add(src)

def _segment_sum(src, seg, n):
    return jax.ops.segment_sum(src, seg, n)
kernel_name = 'mk_conv_attn_hybrid_d2_conv_nhwc256_r2_b9772a'

def setup_inputs(seed: int=0):
    np.random.seed(seed)
    _w = jnp.asarray

    def _rec_inputs():
        import jax
        import jax.numpy as jnp
        _gk = jax.random.key(seed)
        x = 7.22e-05 + 1 * jax.random.normal(jax.random.fold_in(_gk, 1), (8, 32, 32, 128), jnp.float32)
        return x
    x = _rec_inputs()

    def _L0_conv_setup():
        import jax, jax.numpy as jnp
        import numpy as np
        B, H, W, C = (8, 32, 32, 128)
        key = jax.random.key(seed)
        ks = jax.random.split(key, 5)
        s = 1.0 / np.sqrt(C)
        return {'inputs': jax.random.normal(ks[0], (B, H, W, C), dtype=jnp.float32), 'dw1': jax.random.normal(ks[1], (C,), dtype=jnp.float32) * s, 'pw1': jax.random.normal(ks[2], (C, C), dtype=jnp.float32) * s, 'b1': jnp.zeros((C,), dtype=jnp.float32), 'dw2': jax.random.normal(ks[3], (C,), dtype=jnp.float32) * s, 'pw2': jax.random.normal(ks[4], (C, C), dtype=jnp.float32) * s, 'b2': jnp.zeros((C,), dtype=jnp.float32), 'gamma': jnp.ones((1,), dtype=jnp.float32)}
    _L0_conv_all = _L0_conv_setup()
    _L0_conv_in = {k: v for k, v in _L0_conv_all.items() if k in ('dw1', 'pw1', 'b1', 'dw2', 'pw2', 'b2', 'gamma')}
    del _L0_conv_all

    def _L1_attn_setup():
        import jax, jax.numpy as jnp
        import numpy as np
        D_MODEL = 128
        D_STATE = 32
        D_CONV = 4
        EXPAND = 2
        HEADDIM = 32
        D_INNER = EXPAND * D_MODEL
        NHEADS = D_INNER // HEADDIM
        CONV_DIM = D_INNER + 2 * D_STATE
        BATCH = 8
        SEQ = 2048

        def _rmsnorm(x, w, eps):
            return x * jax.lax.rsqrt(jnp.mean(x * x, axis=-1, keepdims=True) + eps) * w
        key = jax.random.key(seed)
        ks = jax.random.split(key, 6)
        x = jax.random.normal(ks[0], (BATCH, SEQ, D_MODEL), jnp.float32)
        d_in_proj = 2 * D_INNER + 2 * D_STATE + NHEADS
        W_in = jax.random.normal(ks[1], (d_in_proj, D_MODEL), jnp.float32) / np.sqrt(D_MODEL)
        conv_w = jax.random.normal(ks[2], (CONV_DIM, D_CONV), jnp.float32) / np.sqrt(D_CONV)
        conv_b = jnp.zeros((CONV_DIM,), jnp.float32)
        dt = jnp.exp(jax.random.uniform(ks[3], (NHEADS,), jnp.float32, np.log(0.001), np.log(0.1)))
        dt_bias = dt + jnp.log(-jnp.expm1(-dt))
        A_log = jnp.log(jax.random.uniform(ks[4], (NHEADS,), jnp.float32, 1.0, 16.0))
        Dp = jnp.ones((NHEADS,), jnp.float32)
        gnorm_w = jnp.ones((D_INNER,), jnp.float32)
        norm_w = jnp.ones((D_MODEL,), jnp.float32)
        W_out = jax.random.normal(ks[5], (D_MODEL, D_INNER), jnp.float32) / np.sqrt(D_INNER)
        return {'x': x, 'W_in': W_in, 'conv_w': conv_w, 'conv_b': conv_b, 'dt_bias': dt_bias, 'A_log': A_log, 'Dp': Dp, 'gnorm_w': gnorm_w, 'norm_w': norm_w, 'W_out': W_out}
    _L1_attn_all = _L1_attn_setup()
    _L1_attn_in = {k: v for k, v in _L1_attn_all.items() if k in ('W_in', 'conv_w', 'conv_b', 'dt_bias', 'A_log', 'Dp', 'gnorm_w', 'norm_w', 'W_out')}
    del _L1_attn_all

    def _L1_ffn_setup():
        import jax, jax.numpy as jnp
        import numpy as np
        N_EXPERTS = 8
        TOP_K = 2
        key = jax.random.key(seed)
        ks = jax.random.split(key, 5)
        B, T, C, E, H = (8, 1024, 128, 8, 341)
        scale = 1.0 / np.sqrt(C)
        return {'x': jax.random.normal(ks[0], (B, T, C), dtype=jnp.float32), 'router_w': jax.random.normal(ks[1], (E, C), dtype=jnp.float32) * scale, 'w1': jax.random.normal(ks[2], (E, H, C), dtype=jnp.float32) * scale, 'w2': jax.random.normal(ks[3], (E, C, H), dtype=jnp.float32) * (1.0 / np.sqrt(H)), 'w3': jax.random.normal(ks[4], (E, H, C), dtype=jnp.float32) * scale}
    _L1_ffn_all = _L1_ffn_setup()
    _L1_ffn_in = {k: v for k, v in _L1_ffn_all.items() if k in ('router_w', 'w1', 'w2', 'w3')}
    del _L1_ffn_all
    return {'x': x, 'L0_conv_dw1': _L0_conv_in['dw1'], 'L0_conv_pw1': _L0_conv_in['pw1'], 'L0_conv_b1': _L0_conv_in['b1'], 'L0_conv_dw2': _L0_conv_in['dw2'], 'L0_conv_pw2': _L0_conv_in['pw2'], 'L0_conv_b2': _L0_conv_in['b2'], 'L0_conv_gamma': _L0_conv_in['gamma'], 'L1_attn_W_in': _L1_attn_in['W_in'], 'L1_attn_conv_w': _L1_attn_in['conv_w'], 'L1_attn_conv_b': _L1_attn_in['conv_b'], 'L1_attn_dt_bias': _L1_attn_in['dt_bias'], 'L1_attn_A_log': _L1_attn_in['A_log'], 'L1_attn_Dp': _L1_attn_in['Dp'], 'L1_attn_gnorm_w': _L1_attn_in['gnorm_w'], 'L1_attn_norm_w': _L1_attn_in['norm_w'], 'L1_attn_W_out': _L1_attn_in['W_out'], 'L1_ffn_router_w': _L1_ffn_in['router_w'], 'L1_ffn_w1': _L1_ffn_in['w1'], 'L1_ffn_w2': _L1_ffn_in['w2'], 'L1_ffn_w3': _L1_ffn_in['w3']}

def reference(x, L0_conv_dw1, L0_conv_pw1, L0_conv_b1, L0_conv_dw2, L0_conv_pw2, L0_conv_b2, L0_conv_gamma, L1_attn_W_in, L1_attn_conv_w, L1_attn_conv_b, L1_attn_dt_bias, L1_attn_A_log, L1_attn_Dp, L1_attn_gnorm_w, L1_attn_norm_w, L1_attn_W_out, L1_ffn_router_w, L1_ffn_w1, L1_ffn_w2, L1_ffn_w3):
    import jax
    import jax.numpy as jnp

    def _L0_conv_ref(inputs, dw1, pw1, b1, dw2, pw2, b2, gamma):
        import jax, jax.numpy as jnp
        import numpy as np
        B, H, W, C = (8, 32, 32, 128)
        b, h, w, c = inputs.shape
        hw = h * w
        x1 = inputs * dw1 @ pw1 + b1
        x2 = inputs * dw2 @ pw2 + b2
        q = x1.reshape(b, hw, c)
        v = x2.reshape(b, hw, c)
        scores = jnp.einsum('bic,bjc->bij', q, q)
        attn = jax.nn.softmax(scores, axis=-1)
        out = jnp.einsum('bij,bjc->bic', attn, v)
        out = out.reshape(b, h, w, c) * gamma + inputs
        return out

    def _L1_attn_ref(x, W_in, conv_w, conv_b, dt_bias, A_log, Dp, gnorm_w, norm_w, W_out):
        import jax, jax.numpy as jnp
        import numpy as np
        D_MODEL = 128
        D_STATE = 32
        D_CONV = 4
        EXPAND = 2
        HEADDIM = 32
        D_INNER = EXPAND * D_MODEL
        NHEADS = D_INNER // HEADDIM
        CONV_DIM = D_INNER + 2 * D_STATE
        BATCH = 8
        SEQ = 2048

        def _rmsnorm(x, w, eps):
            return x * jax.lax.rsqrt(jnp.mean(x * x, axis=-1, keepdims=True) + eps) * w
        Bsz, L, _ = x.shape
        xn = _rmsnorm(x, norm_w, jnp.finfo(x.dtype).eps)
        zxbcdt = jnp.einsum('bld,ed->ble', xn, W_in)
        z = zxbcdt[..., :D_INNER]
        xBC = zxbcdt[..., D_INNER:D_INNER + CONV_DIM]
        dt = zxbcdt[..., -NHEADS:]
        xpad = jnp.pad(xBC, ((0, 0), (D_CONV - 1, 0), (0, 0)))
        conv = sum((xpad[:, k:k + L, :] * conv_w[:, k] for k in range(D_CONV))) + conv_b
        xBC = jax.nn.silu(conv)
        xs = xBC[..., :D_INNER].reshape(Bsz, L, NHEADS, HEADDIM)
        Bm = xBC[..., D_INNER:D_INNER + D_STATE]
        Cm = xBC[..., D_INNER + D_STATE:]
        dt = jax.nn.softplus(dt + dt_bias)
        dA = jnp.exp(dt * -jnp.exp(A_log))

        def step(state, inp):
            dA_t, dt_t, B_t, C_t, x_t = inp
            state = state * dA_t[:, :, None, None] + (dt_t[:, :, None] * x_t)[..., None] * B_t[:, None, None, :]
            y = jnp.einsum('bhpn,bn->bhp', state, C_t)
            return (state, y)
        init = jnp.zeros((Bsz, NHEADS, HEADDIM, D_STATE), x.dtype)
        tm = lambda a: jnp.moveaxis(a, 1, 0)
        _, ys = jax.lax.scan(step, init, (tm(dA), tm(dt), tm(Bm), tm(Cm), tm(xs)))
        y = jnp.moveaxis(ys, 0, 1) + Dp[None, None, :, None] * xs
        y = y.reshape(Bsz, L, D_INNER)
        y = _rmsnorm(y * jax.nn.silu(z), gnorm_w, 1e-05)
        return x + jnp.einsum('ble,de->bld', y, W_out)

    def _L1_ffn_ref(x, router_w, w1, w2, w3):
        import jax, jax.numpy as jnp
        import numpy as np
        N_EXPERTS = 8
        TOP_K = 2
        B, T, C = x.shape
        flat = x.reshape(-1, C)
        logits = flat @ router_w.T
        probs = jax.nn.softmax(logits, axis=-1)
        topk_probs, topk_idx = jax.lax.top_k(probs, TOP_K)
        topk_probs = topk_probs / (jnp.sum(topk_probs, axis=-1, keepdims=True) + 1e-09)
        onehot = jax.nn.one_hot(topk_idx, N_EXPERTS, dtype=flat.dtype)
        gates = jnp.einsum('nk,nke->ne', topk_probs, onehot)
        h1 = jnp.einsum('nc,ehc->neh', flat, w1)
        h3 = jnp.einsum('nc,ehc->neh', flat, w3)
        h = jax.nn.silu(h1) * h3
        y = jnp.einsum('neh,ech->nec', h, w2)
        out = jnp.einsum('ne,nec->nc', gates, y)
        return out.reshape(B, T, C)

    def _gn(v, G=32, eps=1e-05):
        B_, H_, W_, C_ = v.shape
        g = v.reshape(B_, H_, W_, G, C_ // G)
        m = jnp.mean(g, axis=(1, 2, 4), keepdims=True)
        s = jnp.var(g, axis=(1, 2, 4), keepdims=True)
        return ((g - m) / jnp.sqrt(s + eps)).reshape(v.shape)

    def _ln_c(v, eps=1e-06):
        m = jnp.mean(v, axis=-1, keepdims=True)
        s = jnp.var(v, axis=-1, keepdims=True)
        return (v - m) / jnp.sqrt(s + eps)

    def _ln_t(v, eps=1e-05):
        m = jnp.mean(v, axis=-1, keepdims=True)
        s = jnp.var(v, axis=-1, keepdims=True)
        return (v - m) / jnp.sqrt(s + eps)

    def _to_tokens(v):
        B_, H_, W_, C_ = v.shape
        return v.reshape(B_, H_ * W_, C_)

    def _from_tokens(t, like):
        return t.reshape(like.shape)
    x = _L0_conv_ref(x, L0_conv_dw1, L0_conv_pw1, L0_conv_b1, L0_conv_dw2, L0_conv_pw2, L0_conv_b2, L0_conv_gamma)
    t = _to_tokens(x)
    t = t + _L1_attn_ref(_ln_t(t), L1_attn_W_in, L1_attn_conv_w, L1_attn_conv_b, L1_attn_dt_bias, L1_attn_A_log, L1_attn_Dp, L1_attn_gnorm_w, L1_attn_norm_w, L1_attn_W_out)
    t = t + _L1_ffn_ref(_ln_t(t), L1_ffn_router_w, L1_ffn_w1, L1_ffn_w2, L1_ffn_w3)
    x = _from_tokens(t, x)
    return x

_drawn_inputs = setup_inputs


def setup_inputs(seed=0):
    import zlib

    import numpy as np

    out = dict(_drawn_inputs(seed))
    spreads = {'L0_conv_b1': (0.0, 0.8),
     'L0_conv_b2': (0.0, 0.1),
     'L1_attn_conv_b': (0.0, 0.308),
     'L1_attn_Dp': (1.0, 0.2),
     'L1_attn_gnorm_w': (1.0, 0.2),
     'L1_attn_norm_w': (1.0, 0.2)}
    factors = {'L0_conv_dw1': 8.0, 'L0_conv_pw1': 32.734, 'L0_conv_dw2': 6.112, 'L0_conv_pw2': 6.485}
    for name, (base, spread) in spreads.items():
        noise = np.random.default_rng([zlib.crc32(name.encode()), seed]).standard_normal(out[name].shape)
        drawn = base * np.exp(spread * noise) if base else spread * noise
        out[name] = jnp.asarray(drawn.astype(out[name].dtype))
    for name, factor in factors.items():
        out[name] = (out[name] * factor).astype(out[name].dtype)
    return out
```

```python
import concourse.bass as bass
from concourse import mybir
from contextlib import ExitStack


def conv_attn_ssm_moe(nc, x, xT, dw1, pw1, b1, dw2, pw2, b2, gamma, w_zdt, w_xbc, conv_w, conv_b,
                      dt_bias, a_log, d_skip, gnorm_w, norm_w, w_outT, routerT, w1T, w3T, w2T, out):
    fp32, bf16, f32r = mybir.dt.float32, mybir.dt.bfloat16, mybir.dt.float32r
    ALU, ACT, AX = mybir.AluOpType, mybir.ActivationFunctionType, mybir.AxisListType
    P = 128
    TILES = x.shape[0] // P
    NT = 8
    SEQ = NT * P
    C = x.shape[1]
    H, HD, NS = 8, 32, 32
    DI = H * HD
    TAPS = 4
    LAG = 4
    ATANH = [1.0, 0.33333157962211934, 0.20012429465084794, 0.1398064909942622, 0.14087686162896493]
    E, TOP = 8, 2
    HID = w1T.shape[2]
    HC = [(P * k, min(P, HID - P * k)) for k in range(-(-HID // P))]
    TOKENS = TILES * P
    REGION = TOKENS + P
    SLOTS = TOP * TILES + E
    ROW = C + 2
    PAD = TOP * TOKENS
    LN_EPS, RMS_EPS, FLT_EPS = 1e-5, 1e-5, 1.1920928955078125e-07

    ctx = ExitStack()
    with ctx:
        def sb(name, shape, dt=fp32):
            return ctx.enter_context(nc.sbuf_tensor(name, shape, dt))

        def ps(name, shape, dt=fp32):
            return ctx.enter_context(nc.psum_tensor(name, shape, dt))

        def sem(name):
            return ctx.enter_context(nc.semaphore(name))

        ident = sb("ident", [P, P])
        identb = sb("identb", [P, P], bf16)
        tri = sb("tri", [P, P])
        ones = sb("ones", [P, P])
        later = sb("later", [P, P], bf16)
        pick = sb("pick", [P, 16, P], bf16)
        mhalf = sb("mhalf", [P, 2])
        pw1s, pw2s = sb("pw1s", [P, C]), sb("pw2s", [P, C])
        pcol = sb("pcol", [P, 8])
        b2b = sb("b2b", [P, C])
        wz, wx = sb("wz", [P, DI + H]), sb("wx", [P, 3 * P])
        cw, cb = sb("cw", [P, 3, TAPS]), sb("cb", [P, 3])
        hrow = sb("hrow", [P, 3, H])
        gw = sb("gw", [P, 2])
        wo = sb("wo", [P, 2, C])
        XT, X = sb("XT", [P, SEQ]), sb("X", [P, NT, C])
        QH, QL = sb("QH", [P, SEQ], f32r), sb("QL", [P, SEQ], f32r)
        V = sb("V", [P, NT, C])
        PR, PT = sb("PR", [P, SEQ]), sb("PT", [P, SEQ])
        NM, RS, RG = sb("NM", [P, NT]), sb("RS", [P, NT]), sb("RG", [P, NT])
        TA = sb("TA", [P, NT, C])
        BN = sb("BN", [P, NT, 6])
        MV = sb("MV", [P, NT, 2])
        st = sb("st", [P, 12, 2])
        XN = sb("XN", [P, 2, C])
        TR = sb("TR", [P, NT, C])
        XNT = sb("XNT", [P, 2 * P])
        XBC = sb("XBC", [P, 3, TAPS - 1 + SEQ])
        CV, TH = sb("CV", [P, 3, 2 * P]), sb("TH", [P, 3, 2 * P])
        SX = sb("SX", [P, 2, 3, 2 * P])
        CTP = sb("CTP", [P, 2, 2 * P])
        TZ = sb("TZ", [P, 2, DI])
        SZ = sb("SZ", [P, 2, 2, DI])
        dts = sb("dts", [P, 10, 2, H])
        DT = sb("DT", [P, 2, 2, H])
        AD = sb("AD", [P, 64])
        CT = sb("CT", [P, P])
        ECUM, ETOT, DEC = (sb(n, [P, 2, 2, H]) for n in ("ECUM", "ETOT", "DEC"))
        R1 = sb("R1", [P, 2, H])
        C3 = sb("C3", [P, 3, 2, H], bf16)
        R1b = sb("R1b", [P, 2, H])
        CT3, NCT3 = sb("CT3", [P, 2, P], bf16), sb("NCT3", [P, 2, P], bf16)
        XDT = sb("XDT", [P, DI + HD])
        DX, XW, YO, YD, Y2 = (sb(n, [P, DI]) for n in ("DX", "XW", "YO", "YD", "Y2"))
        YG = sb("YG", [P, DI])
        BNAT, GT = sb("BNAT", [P, P]), sb("GT", [P, P])
        ED, M = sb("ED", [P, H, P]), sb("M", [P, H, P])
        ST, STE = sb("ST", [P, DI]), sb("STE", [P, DI])
        SQ, SS = sb("SQ", [P, DI]), sb("SS", [P, 1])
        RY = sb("RY", [P, 2, 2])
        YT = sb("YT", [P, 2, P])
        T2 = sb("T2", [P, TILES, C])
        BN2, MV2 = sb("BN2", [P, NT, 6]), sb("MV2", [P, NT, 2])
        rs2 = sb("rs2", [P, 3, NT])
        XA = sb("XA", [P, TOP, NT, ROW])
        VT = sb("VT", [P, 4 * P])
        rT = sb("rT", [P, 64])
        LG, PB, OHS, SA, PM = (sb(n, [P, NT, E]) for n in ("LG", "PB", "OHS", "SA", "PM"))
        OH = sb("OH", [P, TOP, NT, E])
        M8 = sb("M8", [P, NT, 8])
        IX = sb("IX", [P, NT, 8], mybir.dt.uint32)
        IXF = sb("IXF", [P, NT, TOP])
        r8 = sb("r8", [P, 6, NT])
        PCT = sb("PCT", [P, 2, NT, E])
        OFF = sb("OFF", [P, NT + 1, E])
        iota8, ebase = sb("iota8", [P, E]), sb("ebase", [P, E])
        TOK = sb("TOK", [P, NT])
        SLF = sb("SLF", [P, TOP, NT])
        SL = sb("SL", [P, TOP, NT], mybir.dt.uint32)
        ZT = sb("ZT", [P, 2 * E, ROW])
        ZI = sb("ZI", [P, E], mybir.dt.uint32)
        pidx = sb("pidx", [P, 1])
        NTE, CTE = sb("NTE", [P, E]), sb("CTE", [P, E])
        NTI = sb("NTI", [P, E], mybir.dt.int32)
        itile = sb("itile", [P, SLOTS])
        GE = XBC[:].rearrange("p m t -> p (m t)")[:, 0:SLOTS * E].rearrange("p (t e) -> p t e", e=E)
        TB = sb("TB", [P, 3, SLOTS])
        TBI = sb("TBI", [P, 2, SLOTS], mybir.dt.int32)
        W1, W3 = sb("W1", [P, E * HID]), sb("W3", [P, E * HID])
        W2 = sb("W2", [P, E, len(HC), C])
        GX = sb("GX", [P, 2, ROW])
        GXT = TA[:, 0:2, :]
        SH = XT[:, 0:2 * HID].rearrange("p (a h) -> p a h", a=2)
        HH = X[:].rearrange("p t c -> p (t c)")[:, 0:2 * HID].rearrange("p (a h) -> p a h", a=2)
        HT = V[:].rearrange("p t c -> p (t c)")[:, 0:2 * len(HC) * P].rearrange("p (a k t) -> p a k t", a=2, t=P)
        YE = sb("YE", [P, 2, C])
        DIX = sb("DIX", [P, 2, 1], mybir.dt.uint32)
        xg = nc.dram_tensor("rows_by_expert", [E * REGION + E * P, ROW], fp32, kind="Internal").ap()
        yg = nc.dram_tensor("results_by_choice", [PAD + 2 * E * P, C], fp32, kind="Internal").ap()

        pX, pY = ps("pX", [P, 2 * 512]), ps("pY", [P, 2 * 512])
        pa, pb, pc, pd = (ps(n, [P, 512]) for n in ("pa", "pb", "pc", "pd"))

        S = {}
        Y01 = [[PR, PT], [ED, M]]
        tokens = lambda a: a[:].rearrange("p a b -> p (a b)") if a in (ED, M) else a[:]
        Y01 = [[tokens(a).rearrange("p (t c) -> p t c", c=C) for a in two] for two in Y01]

        def s(name):
            if name not in S:
                S[name] = sem(name)
            return S[name]

        def upto(eng, name, base, c):
            if not isinstance(base, int):
                eng.wait_ge(s(name), base + c)
            elif base + c > 0:
                eng.wait_ge(s(name), min(base + c, TILES))

        def apart(eng):
            eng.sem_inc(s("apart"), 1)

        class Steps:
            def __init__(self, eng, name, base, c, tiles, per_tile):
                self.eng, self.sem, self.n = eng, s(name), 0
                self.start, self.total = base * per_tile + c * per_tile, tiles * per_tile

            def then(self, ins, last=False):
                self.n += 1
                assert self.n < self.total
                if last:
                    ins.then_inc(self.sem, self.total - self.n + 1)
                    self.n = self.total
                else:
                    ins.then_inc(self.sem, 1)
                self.eng.wait_ge(self.sem, self.start + self.n)

        def there(base, c):
            return not isinstance(base, int) or 0 <= base + c < TILES

        block = ctx.enter_context(nc.Block())

        def batches(eng, step):
            for i in range(NT):
                step(0, i)
            with eng.Fori(NT, TILES - 2 * NT + 1, NT) as base:
                for i in range(NT):
                    step(base, i)
            for i in range(NT):
                step(TILES - NT, i)
            for i in range(NT):
                step(TILES, i)

        NLOAD = 5 + 5 + 2 + 3 + 3 + 2 + 1 + 1

        @block.sync
        def _(sp):
            def load(dst, src):
                sp.dma_start(dst, src).then_inc(s("loaded"), 16)
            row = lambda v, n: v.rearrange("(a n) -> a n", a=1).broadcast_to([P, n])
            sp.dma_start(XT[:], xT[0:P, :]).then_inc(s("xT_loaded"), 16)
            xtok = x.rearrange("(t p) c -> p t c", p=P)
            sp.dma_start(X[:], xtok[:, 0:NT, :]).then_inc(s("x_loaded"), 16)
            col = lambda v: v.rearrange("(p a) -> p a", a=1)
            for k, v in enumerate((dw1, dw2, b1, norm_w)):
                load(pcol[:, k:k + 1], col(v))
            load(pcol[:, 4:5], row(gamma, 1))
            load(pw1s[:], pw1)
            load(pw2s[:], pw2)
            load(b2b[:], row(b2, C))
            load(wz[:], w_zdt)
            load(wx[:, 0:DI + 2 * NS], w_xbc)
            sp.wait_ge(s("zeroed"), 1)
            load(cw[:, 0:2, :], conv_w[0:2 * P, :].rearrange("(m p) k -> p m k", p=P))
            load(cw[0:2 * NS, 2, :], conv_w[2 * P:, :])
            for m in range(3):
                part = conv_b[m * P:min((m + 1) * P, DI + 2 * NS)]
                load(cb[0:part.shape[0], m:m + 1], col(part))
            for k, v in enumerate((dt_bias, a_log, d_skip)):
                load(hrow[:, k, :], row(v, H))
            for m in range(2):
                load(gw[:, m:m + 1], col(gnorm_w[m * P:m * P + P]))
            load(wo[:], w_outT.rearrange("(k p) c -> p k c", p=P))
            load(rT[:, 0:E], routerT)
            def load_expert(dst, src):
                sp.dma_start(dst, src).then_inc(s("experts_loaded"), 16)
            load_expert(W1[:].rearrange("p (e h) -> p e h", e=E), w1T.rearrange("e c h -> c e h"))
            load_expert(W3[:].rearrange("p (e h) -> p e h", e=E), w3T.rearrange("e c h -> c e h"))
            for k, (h0, hn) in enumerate(HC):
                load_expert(W2[0:hn, :, k, :], w2T[:, h0:h0 + hn, :].rearrange("e h c -> h e c"))

            def step(base):
                upto(sp, "projected", base, NT)
                sp.dma_start(XT[:], xT[bass.ds(base * 16 + P, P), :]).then_inc(s("xT_loaded"), 16)
                upto(sp, "t_ready", base, NT)
                sp.dma_start(X[:], xtok[:, bass.ds(base + NT, NT), :]).then_inc(s("x_loaded"), 16)
            step(0)
            with sp.Fori(NT, TILES - 2 * NT + 1, NT) as base:
                step(base)
            sp.wait_ge(s("zt_ready"), 2)
            sp.dma_start(xg[E * REGION:, :].rearrange("(t p) c -> p t c", p=P), ZT[:, E:, :]).then_inc(s("spare_filled"), 16)
            sp.wait_ge(s("table_ready"), 1)
            sp.wait_ge(s("scattered"), 16 * TOP * TILES)
            sp.wait_ge(s("filled_up"), 16 * E)
            sp.wait_ge(s("spare_filled"), 16)

            def fetch(t, n, par):
                row = sp.value_load(TBI[0:1, 0, t], min_val=0, max_val=E * REGION + (E - 1) * P)
                sp.wait_ge(s("gx_free"), n)
                sp.dma_start(GX[:, par, :], xg[bass.ds(row, P), :]).then_inc(s(f"gx{par}_loaded"), 16)
            with sp.Fori(0, SLOTS - 1, 2) as t:
                for par in range(2):
                    fetch(bass.ds(t + par, 1), t + par + 1, par)
            for par in range(2):
                sp.wait_ge(s(f"ye{par}_scattered"), 8 * SLOTS)
            otok = out.rearrange("(t p) c -> p t c", p=P)

            def y_load(b, base, par):
                for k in range(TOP):
                    src = yg[bass.ds(base * P + k * TOKENS, NT * P), :].rearrange("(t p) c -> p t c", p=P)
                    sp.dma_start(Y01[par][k], src).then_inc(s(f"y{par}_loaded"), 16)
            for b in range(TILES // NT):
                if b >= 2:
                    sp.wait_ge(s("added"), b - 1)
                y_load(b, b * NT, b % 2)
                if b >= 1:
                    sp.wait_ge(s("added"), b)
                    sp.dma_start(otok[:, (b - 1) * NT:b * NT, :], T2[:, (b - 1) * NT:b * NT, :]).then_inc(s("stored"), 16)
            sp.wait_ge(s("added"), TILES // NT)
            sp.dma_start(otok[:, TILES - NT:, :], T2[:, TILES - NT:, :]).then_inc(s("stored"), 16)
            sp.wait_ge(s("stored"), 16 * (TILES // NT))

        @block.tensor
        def _(pe):
            mm = nc.tensor.matmul

            def project():
                for h in range(2):
                    last = mm(pY[:, 512 * h:512 * h + 512], pw1s[:], XT[:, 512 * h:512 * h + 512], start=True, stop=True)
                last.then_inc(s("qps"), NT)
                for i in range(NT):
                    last = mm(pX[:, P * i:P * i + P], XT[:, P * i:P * i + P], pw2s[:], start=True, stop=True)
                last.then_inc(s("projected"), NT)

            def step(base, i):
                k, e, f = i - LAG, i - LAG - 1, i - 2
                if there(base, i):
                    upto(pe, "q_ready", base, NT)
                    upto(pe, "v_ready", base, NT)
                    upto(pe, "exp_ready", base, i)
                    for h in range(2):
                        q = slice(512 * h, 512 * h + 512)
                        ti = slice(P * i, P * i + P)
                        mm(pX[:, q], QH[:, ti], QH[:, q], start=True, stop=False)
                        mm(pX[:, q], QH[:, ti], QL[:, q], start=False, stop=False)
                        last = mm(pX[:, q], QL[:, ti], QH[:, q], start=False, stop=True)
                    last.then_inc(s("s_ready"), 1)
                par, half = (k // 2) % 2, k % 2
                tk = slice(P * half, P * half + P)
                if there(base, k):
                    upto(pe, "sx_ready", base, k + 1)
                    upto(pe, "bc_ready", base, k + 1)
                    upto(pe, "t_ready", base, i)
                    for m in range(3):
                        last = nc.tensor.transpose(pa[:, P * m:P * m + P], SX[:, par, m, tk], ident[:])
                    last.then_inc(s("xs_ready"), 1)
                if there(base, e):
                    upto(pe, "yg_ready", base, e + 1)
                    upto(pe, "t2_ready", base, e)
                    if i == 6:
                        upto(pe, "lg_ready", base, -4)
                    if i == 0:
                        upto(pe, "places_read", base, 0)
                    upto(pe, "cv01_evac", base, i - 1 if i % 2 else i - 2)
                    for m in range(2):
                        last = nc.tensor.transpose(pb[:, P * m:P * m + P], YG[:, P * m:P * m + P], ident[:])
                    last.then_inc(s("yT_ps"), 1)
                if there(base, k):
                    upto(pe, "ydiag_read", base, k)
                    mm(pc[:, 0:P], SX[:, par, 2, tk], CTP[:, par, tk], start=True, stop=True).then_inc(s("g_ps"), 1)
                    upto(pe, "ct3_ready", base, k + 1)
                    upto(pe, "pt_dve", base, i)
                    upto(pe, "pt_act", base, i)
                    for h2 in range(2):
                        q = slice(512 * h2, 512 * h2 + 512)
                        mm(pY[:, q], identb[:], later[:, None, :].broadcast_to([P, 4, P]), start=True, stop=False, skip_group_check=True)
                        mm(pY[:, q], NCT3[:, par, :], pick[:, half * H + 4 * h2:half * H + 4 * h2 + 4, :], start=False, stop=False, skip_group_check=True)
                    for h in range(H):
                        last = mm(pY[:, P * h:P * h + P], pick[:, half * H + h, :], CT3[:, par, :], start=False, stop=True, skip_group_check=True)
                    last.then_inc(s("d_ps"), 1)
                front = i % 2 == 0 and i < NT and there(base, f)
                if front:
                    upto(pe, "xn_ready", base, f + 2)
                    upto(pe, "ct3_ready", base, f)
                    for j in range(2):
                        last = nc.tensor.transpose(pd[:, P * j:P * j + P], XN[:, j, :], ident[:])
                    last.then_inc(s("xnT_ps"), 2)
                if there(base, e):
                    upto(pe, "yT_ready", base, e + 1)
                    for m in range(2):
                        last = mm(pb[:, 0:C], YT[:, m, :], wo[:, m, :], start=m == 0, stop=m == 1)
                    last.then_inc(s("out_ps"), 1)
                if front:
                    upto(pe, "xnT_ready", base, f + 2)
                    upto(pe, "xdt_ready", base, k + 1)
                    upto(pe, "dx_ready", base, k + 1)
                    upto(pe, "bnat_ready", base, k + 1)
                    upto(pe, "t_ready", base, i)
                    mm(pa[:, 0:DI + H], XNT[:, 0:P], wz[:], start=True, stop=True).then_inc(s("z_ps"), 1)
                    upto(pe, "gT_ready", base, k + 1)
                    mm(pc[:, 0:DI + H], XNT[:, P:2 * P], wz[:], start=True, stop=True).then_inc(s("z_ps"), 1)
                if there(base, k):
                    if front:
                        upto(pe, "xnT_ready", base, f + 2)
                    upto(pe, "xw_ready", base, k + 1)
                    upto(pe, "bnat_ready", base, k + 1)
                    upto(pe, "st_ready", base, k)
                    upto(pe, "ct3_ready", base, f if i % 2 == 0 else f + 1)
                    if k % NT != 0:
                        mm(pd[:, 0:DI], CTP[:, par, tk], ST[:], start=True, stop=True)
                    last = mm(pd[:, DI:2 * DI], BNAT[:], XW[:], start=k % NT == 0, stop=True, skip_group_check=True)
                    last.then_inc(s("state_ps"), 1)
                if there(base, i):
                    upto(pe, "expD_ready", base, k + 1)
                    upto(pe, "exp_ready", base, i + 1)
                    for j in range(NT):
                        last = nc.tensor.transpose(pY[:, P * j:P * j + P], PR[:, P * j:P * j + P], ident[:])
                    last.then_inc(s("pT_ps"), 1)
                if front:
                    upto(pe, "t2_ready", base, e + 1)
                    for m in range(2):
                        last = mm(pb[:, 256 * m:256 * m + 256], wx[:, P * m:P * m + P], XNT[:], start=True, stop=True, skip_group_check=True)
                    last.then_inc(s("xbc01_ps"), 2)
                    upto(pe, "sz_ready", base, f + 1)
                    upto(pe, "u_ready", base, f + 1)
                    mm(pa[:, 0:256], wx[:, 2 * P:3 * P], XNT[:], start=True, stop=True).then_inc(s("xbc2_ps"), 2)
                if there(base, k):
                    upto(pe, "m_ready", base, k + 1)
                    upto(pe, "xdt_ready", base, k + 1)
                    if i % 2 == 0:
                        upto(pe, "sz_ready", base, f + 2)
                        upto(pe, "u_ready", base, f + 2)
                    upto(pe, "gT_ready", base, k + 1)
                    for h in range(H):
                        last = mm(pc[:, 64 * h:64 * h + 64], M[:, h, :], XDT[:, HD * h:HD * h + 64], start=True, stop=True, skip_group_check=True)
                    last.then_inc(s("ydiag_ps"), 1)
                if front:
                    upto(pe, "ad_ready", base, f + 2)
                    if there(base, k):
                        upto(pe, "yo_ready", base, k + 1)
                        upto(pe, "st_ready", base, k + 1)
                    mm(pd[:, 0:64], tri[:], AD[:], start=True, stop=True, skip_group_check=True)
                    mm(pd[:, 64:128], ones[:], AD[:], start=True, stop=True, skip_group_check=True).then_inc(s("cum_ps"), 2)
                if there(base, i):
                    upto(pe, "pt_act", base, i + 1)
                    upto(pe, "pt_dve", base, i + 1)
                    if front:
                        upto(pe, "cv_evac", base, f + 2)
                    elif there(base, k):
                        upto(pe, "xdt_ready", base, k + 1)
                        upto(pe, "dx_ready", base, k + 1)
                        upto(pe, "bnat_ready", base, k + 1)
                    upto(pe, "t_ready", base, i)
                    for j in range(NT):
                        last = mm(pa[:, 0:C], PT[:, P * j:P * j + P], V[:, j, :], start=j == 0, stop=j == NT - 1)
                    last.then_inc(s("o_ps"), 1)
                if front:
                    upto(pe, "c3_ready", base, f + 2)
                    upto(pe, "ecum_ready", base, f + 2)
                    nc.tensor.transpose(pd[:, :].bitcast(bf16)[0:48, 0:P], C3[:].rearrange("p a b c -> p (a b c)"), identb[:]).then_inc(s("ct3_ps"), 2)
                if i in (5, 7) and there(base, -NT):
                    grp = (i - 5) // 2
                    upto(pe, "xa_ready", base, 0)
                    upto(pe, "t2_ready", base, e + 1)
                    if grp:
                        upto(pe, "lg_ready", base, -4)
                    else:
                        upto(pe, "places_read", base, 0)
                    for j in range(4):
                        last = nc.tensor.transpose(pb[:, P * j:P * j + P], XA[:, 0, 4 * grp + j, 0:C], ident[:])
                    last.then_inc(s("vT_ps"), 4)
                    upto(pe, "vT_ready", base, 4 * grp - 4)
                    for j in range(4):
                        last = mm(pb[:, 64 * j:64 * j + 64], VT[:, P * j:P * j + P], rT[:], start=True, stop=True, skip_group_check=True)
                    last.then_inc(s("logits_ps"), 4)
                if i == 7 and there(base, -NT):
                    upto(pe, "onehot_ready", base, 0)
                    for m, l in enumerate((tri, ones)):
                        last = mm(pb[:, 64 * m:64 * m + 64], l[:], OHS[:].rearrange("p a b -> p (a b)"), start=True, stop=True, skip_group_check=True)
                    last.then_inc(s("places_ps"), NT)
                if i == NT - 1 and there(base, NT):
                    if isinstance(base, int):
                        pe.wait_ge(s("xT_loaded"), 16 * (base // NT + 2))
                    else:
                        pe.wait_ge(s("xT_loaded"), base * 2 + 32)
                    upto(pe, "exp_ready", base, NT)
                    project()

            pe.wait_ge(s("setup"), 1)
            pe.wait_ge(s("xT_loaded"), 16)
            project()
            batches(pe, step)

            pe.wait_ge(s("experts_loaded"), 16 * 5)
            pe.wait_ge(s("table_ready"), 1)

            def x_T(t, par):
                pe.wait_ge(s(f"gx{par}_loaded"), t * 8 + 16)
                nc.tensor.transpose(pa[:, 0:P], GX[:, par, 0:C], ident[:]).then_inc(s("gxt_ps"), 1)

            def hidden(n, par, tile):
                expert = pe.value_load(TBI[0:1, 1, tile], min_val=0, max_val=E - 1)
                pe.wait_ge(s("gxt_ready"), n)
                for w, bank in ((W1, pX), (W3, pY)):
                    last = mm(bank[:, 512 * par:512 * par + HID], GXT[:, par, :], w[:, bass.ds(expert * HID, HID)], start=True, stop=True)
                    last.then_inc(s("h1_ps" if w is W1 else "h3_ps"), 1)
                return expert

            def result(n, par, expert):
                pe.wait_ge(s("hh_ready"), n)
                for k, (h0, hn) in enumerate(HC):
                    last = nc.tensor.transpose(pc[0:hn, P * k:P * k + P], HH[:, par, h0:h0 + hn], ident[:])
                last.then_inc(s("hT_ps"), 1)
                pe.wait_ge(s("hT_ready"), n)
                for k, (h0, hn) in enumerate(HC):
                    last = mm((pd, pb)[par][:, 0:C], HT[0:hn, par, k, :], W2[0:hn, bass.ds(expert, 1), k, :], start=k == 0, stop=k == len(HC) - 1)
                last.then_inc(s("y_ps"), 1)

            with pe.Fori(0, SLOTS - 1, 2) as t:
                x_T(t, 0)
                first = hidden(t + 1, 0, bass.ds(t, 1))
                x_T(t, 1)
                second = hidden(t + 2, 1, bass.ds(t + 1, 1))
                result(t + 1, 0, first)
                result(t + 2, 1, second)

        @block.scalar
        def _(act):
            A = nc.scalar.activation

            def take_q():
                for h in range(2):
                    q = slice(512 * h, 512 * h + 512)
                    last = A(QH[:, q], pY[:, q], ACT.Identity, bias=pcol[:, 2:3])
                last.then_inc(s("qh_ready"), NT)

            def step(base, i):
                k, e, f = i - LAG, i - LAG - 1, i - 2
                par, half = (k // 2) % 2, k % 2
                front = i % 2 == 0 and i < NT and there(base, f)
                fpar = (f // 2) % 2
                if there(base, e):
                    upto(act, "yT_ps", base, e + 1)
                    A(YT[:].rearrange("p a b -> p (a b)"), pb[:, 0:DI], ACT.Copy).then_inc(s("yT_ready"), 1)
                if there(base, k):
                    upto(act, "xs_ready", base, k + 1)
                    upto(act, "dx_ready", base, k + 1)
                    A(BNAT[:], pa[:, 2 * P:3 * P], ACT.Copy).then_inc(s("bnat_ready"), 1)
                    upto(act, "g_ps", base, k + 1)
                    upto(act, "m_ready", base, k)
                    A(GT[:], pc[:, 0:P], ACT.Copy).then_inc(s("gT_ready"), 1)
                if there(base, i):
                    upto(act, "nm_ready", base, i + 1)
                    upto(act, "pT_ps", base, i)
                    upto(act, "rg_ready", base, i)
                    A(PR[:], pX[:], ACT.Exp, bias=NM[:, i:i + 1], accum_out=RS[:, i:i + 1]).then_inc(s("exp_ready"), 1)
                if there(base, k):
                    upto(act, "d_ps", base, k + 1)
                    upto(act, "m_ready", base, k)
                    A(ED[:].rearrange("p h t -> p (h t)"), pY[:], ACT.Exp).then_inc(s("expD_ready"), 1)
                if front:
                    upto(act, "xnT_ps", base, f + 2)
                    upto(act, "xbc2_ps", base, f)
                    A(XNT[:], pd[:, 0:2 * P], ACT.Copy).then_inc(s("xnT_ready"), 2)
                    for j in range(2):
                        upto(act, "z_ps", base, f + j + 1)
                        upto(act, "sz_ready", base, f)
                        A(TZ[:, j, :], (pa, pc)[j][:, 0:DI], ACT.Tanh).then_inc(s("tz_ready"), 1)
                if there(base, i):
                    upto(act, "pT_ps", base, i + 1)
                    upto(act, "o_ps", base, i)
                    A(PT[:, 0:512], pY[:, 0:512], ACT.Copy).then_inc(s("pt_act"), 1)
                if front:
                    upto(act, "nau_ready", base, f + 2)
                    A(dts[:, 2], dts[:, 1], ACT.Exp).then_inc(s("enau_ready"), 2)
                    upto(act, "sx_ready", base, f)
                    fo = (f % NT) * P + TAPS - 1
                    upto(act, "xbc01_ps", base, f + 2)
                    for m in range(3):
                        if m == 2:
                            upto(act, "xbc2_ps", base, f + 2)
                        src = pb[:, 256 * m:256 * m + 256] if m < 2 else pa[:, 0:256]
                        A(XBC[:, m, fo:fo + 256], src, ACT.Copy)
                        last = A(CV[:, m, :], src, ACT.Identity, bias=cb[:, m:m + 1], scale=cw[:, m, 3:4])
                        if m == 1:
                            last.then_inc(s("cv01_evac"), 2)
                    last.then_inc(s("cv_evac"), 2)
                    upto(act, "conv_ready", base, f + 2)
                    A(TH[:], CV[:], ACT.Tanh).then_inc(s("th_ready"), 2)
                    upto(act, "cum1", base, f + 2)
                    A(ECUM[:, fpar], CT[:, 0:16].rearrange("p (a b) -> p a b", a=2), ACT.Exp)
                    A(ETOT[:, fpar], CT[:, 64:80].rearrange("p (a b) -> p a b", a=2), ACT.Exp).then_inc(s("ecum_ready"), 2)
                    upto(act, "dec_in", base, f + 2)
                    A(DEC[:, fpar], R1b[:], ACT.Exp).then_inc(s("dec_exp"), 2)
                    upto(act, "sx_ready", base, f + 2)
                    A(CTP[0:NS, fpar, :], SX[NS:2 * NS, fpar, 2, :], ACT.Copy).then_inc(s("bc_ready"), 2)
                if there(base, k):
                    upto(act, "yg_ready", base, k + 1)
                    upto(act, "sst_ready", base, k)
                    A(SQ[:], YG[:], ACT.Square, accum_out=SS[:]).then_inc(s("ss_ready"), 1)
                if front:
                    upto(act, "ct3_ps", base, f + 2)
                    A(CT3[0:48, fpar, :], pd[:, :].bitcast(bf16)[0:48, 0:P], ACT.Copy)
                    A(NCT3[0:48, fpar, :], pd[:, :].bitcast(bf16)[0:48, 0:P], ACT.Copy, scale=-1.0).then_inc(s("ct3_ready"), 2)
                if i == 5 and there(base, -NT):
                    upto(act, "rstd2_ready", base, 0)
                    upto(act, "xa_free", base, 0)
                    apart(act)
                    for j in range(NT):
                        last = A(XA[:, 0, j, 0:C], T2[:, bass.ds(base - NT + j, 1), :].rearrange("p a c -> p (a c)"), ACT.Identity, bias=rs2[:, 2, j:j + 1], scale=rs2[:, 1, j:j + 1])
                    last.then_inc(s("xa_ready"), NT)
                if i in (5, 7) and there(base, -NT):
                    grp = (i - 5) // 2
                    upto(act, "vT_ps", base, 4 * grp - 4)
                    upto(act, "logits_ps", base, 4 * grp - 8)
                    A(VT[:], pb[:], ACT.Copy).then_inc(s("vT_ready"), 4)
                if i == 7 and there(base, -NT):
                    upto(act, "lsub_ready", base, 0)
                    A(PB[:], LG[:], ACT.Exp).then_inc(s("pexp_ready"), NT)
                if i == NT - 1 and there(base, NT):
                    upto(act, "qps", base, 2 * NT)
                    upto(act, "s_ready", base, NT)
                    take_q()

            act.wait_ge(s("loaded"), 16 * NLOAD)
            A(hrow[:, 1, :], hrow[:, 1, :], ACT.Exp).then_inc(s("a_exp"), 1)
            act.wait_ge(s("qps"), NT)
            take_q()
            batches(act, step)

            def expert_tile(n, par):
                act.wait_ge(s("gxt_ps"), n)
                A(GXT[:, par, :], pa[:, 0:P], ACT.Copy).then_inc(s("gxt_ready"), 1)
                act.wait_ge(s("h1_ps"), n)
                A(SH[:, par, :], pX[:, 512 * par:512 * par + HID], ACT.Silu).then_inc(s("silu_ready"), 1)

            def expert_out(t, par):
                n = t + par + 1
                act.wait_ge(s("y_ps"), n)
                act.wait_ge(s(f"gx{par}_loaded"), t * 8 + 16)
                act.wait_ge(s("ye_free"), n)
                A(YE[:, par, :], (pd, pb)[par][:, 0:C], ACT.Copy, scale=GX[:, par, C:C + 1]).then_inc(s("ye_ready"), 1)

            with act.Fori(0, SLOTS - 1, 2) as t:
                for par in range(2):
                    expert_tile(t + par + 1, par)
                for par in range(2):
                    expert_out(t, par)

        @block.gpsimd
        def _(pool):
            g = nc.gpsimd
            g.memset(cw[:], 0.0)
            g.memset(cb[:], 0.0).then_inc(s("zeroed"), 1)
            for t, v in ((wx[:, DI + 2 * NS:], 0.0), (CTP[:], 0.0), (XBC[:, :, 0:TAPS - 1], 0.0), (AD[:], 0.0), (CT3[:], 0.0),
                         (NCT3[:], 0.0), (ST[:], 0.0), (XDT[:, DI:], 0.0), (ones[:], 1.0), (mhalf[:], -0.5)):
                g.memset(t, v)
            g.memset(tri[:], 1.0)
            g.memset(later[:], 0.0)
            g.memset(pick[:], 0.0)
            g.memset(ident[:], 0.0).then_inc(s("filled"), 1)
            pool.wait_ge(s("filled"), 1)
            g.affine_select(out=tri[:], in_=tri[:], compare_op=ALU.is_ge, fill=0.0, base=0, pattern=[[1, P]], channel_multiplier=-1)
            g.affine_select(out=later[:], in_=later[:], compare_op=ALU.is_ge, fill=-1e30, base=0, pattern=[[1, P]], channel_multiplier=-1)
            for j in range(3):
                g.affine_select(out=pick[:], in_=pick[:], compare_op=ALU.not_equal, fill=1.0, base=-16 * j,
                                pattern=[[-1, 16], [0, P]], channel_multiplier=1).then_inc(s("picked"), 1)
                pool.wait_ge(s("picked"), j + 1)
            g.affine_select(out=ident[:], in_=ident[:], compare_op=ALU.not_equal, fill=1.0, base=0, pattern=[[-1, P]], channel_multiplier=1).then_inc(s("filled"), 1)
            pool.wait_ge(s("filled"), 2)
            g.tensor_copy(identb[:], ident[:]).then_inc(s("consts"), 1)
            pool.sem_inc(s("xa_free"), NT)
            pool.sem_inc(s("places_read"), NT)
            g.memset(rT[:, E:], 0.0)
            g.memset(OFF[:], 0.0)
            g.memset(ZT[:], 0.0).then_inc(s("zt_ready"), 1)
            lazy = dict(allow_small_or_imprecise_dtypes=True)
            g.iota(iota8[:], [[1, E]], base=0, channel_multiplier=0, **lazy)
            g.iota(TOK[:], [[P, NT]], base=0, channel_multiplier=1, **lazy)
            g.iota(pidx[:], [[0, 1]], base=0, channel_multiplier=1, **lazy)
            g.iota(itile[:], [[1, SLOTS]], base=0, channel_multiplier=0, **lazy)
            g.iota(TB[:, 0, 0:2 * E], [[P, 2 * E]], base=PAD, channel_multiplier=1, **lazy).then_inc(s("iotas"), 1)
            pool.wait_ge(s("iotas"), 1)
            pool.wait_ge(s("zt_ready"), 1)
            g.tensor_copy(ZT[:, :, C + 1], TB[:, 0, 0:2 * E]).then_inc(s("zt_ready"), 1)
            g.tensor_scalar(ebase[:], iota8[:], float(REGION), -1.0, ALU.mult, ALU.add).then_inc(s("iotas"), 1)

            def step(base, i):
                k, e, f = i - LAG, i - LAG - 1, i - 2
                par, half = (k // 2) % 2, k % 2
                front = i % 2 == 0 and i < NT and there(base, f)
                if i == 5 and there(base, -NT):
                    upto(pool, "mv2_ready", base, 0)
                    steps = Steps(pool, "norm2_steps", base, -NT, NT, 1)
                    apart(pool)
                    steps.then(g.tensor_scalar(rs2[:, 0, :], MV2[:, :, 1], LN_EPS, 1.0, ALU.add, ALU.mult))
                    steps.then(g.tensor_tensor(rs2[:, 1, :], rs2[:, 0, :], mhalf[:, 0:1].broadcast_to([P, NT]), ALU.pow))
                    steps.then(g.tensor_tensor(rs2[:, 0, :], MV2[:, :, 0], rs2[:, 1, :], ALU.mult), True)
                    apart(pool)
                    g.tensor_scalar(rs2[:, 2, :], rs2[:, 0, :], -1.0, 1.0, ALU.mult, ALU.mult).then_inc(s("rstd2_ready"), NT)
                if there(base, e):
                    upto(pool, "ss_ready", base, e + 1)
                    upto(pool, "t2_ready", base, e)
                    apart(pool)
                    g.tensor_scalar(RY[:, 0, 0:1], SS[:], 1.0 / DI, RMS_EPS, ALU.mult, ALU.add).then_inc(s("sst_ready"), 1)
                    upto(pool, "sst_ready", base, e + 1)
                    g.tensor_tensor(RY[:, 1, 0:1], RY[:, 0, 0:1], mhalf[:, 0:1], ALU.pow).then_inc(s("ry_ready"), 1)
                if front:
                    mean, var = MV[:, f % NT:f % NT + 2, 0], MV[:, f % NT:f % NT + 2, 1]
                    upto(pool, "mv_ready", base, f + 2)
                    steps = Steps(pool, "norm_steps", base, f, 2, 8)
                    def chain(n, ins):
                        steps.then(ins, n == 7)
                    apart(pool)
                    chain(0, g.tensor_scalar(st[:, 0, :], var, LN_EPS, 1.0, ALU.add, ALU.mult))
                    chain(1, g.tensor_tensor(st[:, 1, :], st[:, 0, :], mhalf[:], ALU.pow))
                    chain(2, g.tensor_tensor(st[:, 2, :], st[:, 1, :], st[:, 1, :], ALU.mult))
                    chain(3, g.tensor_tensor(st[:, 3, :], st[:, 2, :], var, ALU.mult))
                    apart(pool)
                    chain(4, g.tensor_scalar(st[:, 4, :], st[:, 3, :], FLT_EPS, 1.0, ALU.add, ALU.mult))
                    chain(5, g.tensor_tensor(st[:, 5, :], st[:, 4, :], mhalf[:], ALU.pow))
                    chain(6, g.tensor_tensor(st[:, 6, :], st[:, 5, :], st[:, 1, :], ALU.mult))
                    apart(pool)
                    g.tensor_scalar(st[:, 8, :], st[:, 1, :], 1.0, 1.0, ALU.add, ALU.mult)
                    g.tensor_tensor(st[:, 9, :], mean, st[:, 1, :], ALU.mult)
                    chain(7, g.tensor_tensor(st[:, 7, :], mean, st[:, 6, :], ALU.mult))
                    upto(pool, "xnT_ps", base, f)
                    for j in range(2):
                        apart(pool)
                        last = g.tensor_scalar(XN[:, j, :], TA[:, f % NT + j, :], st[:, 6, j:j + 1], st[:, 7, j:j + 1], ALU.mult, ALU.subtract)
                    last.then_inc(s("xn_ready"), 2)
                    for j in range(2):
                        apart(pool)
                        last = g.tensor_scalar(TR[:, f % NT + j, :], TA[:, f % NT + j, :], st[:, 8, j:j + 1], st[:, 9, j:j + 1], ALU.mult, ALU.subtract)
                    last.then_inc(s("tr_ready"), 2)
                if there(base, k):
                    b3 = lambda t: t[:, par, half, :, None].broadcast_to([P, H, HD])
                    v3 = lambda t: t[:, 0:DI].rearrange("p (h d) -> p h d", h=H)
                    upto(pool, "xdt_ready", base, k + 1)
                    upto(pool, "dec_exp", base, k + 1)
                    upto(pool, "state_ps", base, k)
                    g.tensor_tensor(v3(XW), v3(XDT), b3(DEC), ALU.mult).then_inc(s("xw_ready"), 1)
                    if k % NT != 0:
                        upto(pool, "st_ready", base, k)
                        g.tensor_tensor(v3(STE)[0:NS], v3(ST)[0:NS], ETOT[0:NS, par, half, :, None].broadcast_to([NS, H, HD]), ALU.mult)
                        upto(pool, "yo_ready", base, k + 1)
                        upto(pool, "dx_ready", base, k + 1)
                        upto(pool, "y2_ready", base, k)
                        g.tensor_tensor(YD[:], YO[:], DX[:], ALU.add).then_inc(s("yd_ready"), 1)
                    else:
                        upto(pool, "dx_ready", base, k + 1)
                        upto(pool, "y2_ready", base, k)
                        apart(pool)
                        g.tensor_copy(YD[:], DX[:]).then_inc(s("yd_ready"), 1)
                if i == 7 and there(base, -NT):
                    upto(pool, "slots_ready", base, 0)
                    upto(pool, "xb_ready", base, 0)
                    apart(pool)
                    for j in range(NT):
                        for c_ in range(TOP):
                            g.indirect_dma_start(xg, bass.IndirectOffsetOnAxis(ap=SL[:, c_, j:j + 1], axis=0), XA[:, c_, j, :], None).then_inc(s("scattered"), 16)
                    pool.wait_ge(s("scattered"), base * (16 * TOP))
                    pool.sem_inc(s("xa_free"), NT)

            batches(pool, step)
            pool.wait_ge(s("zi_ready"), 1)
            pool.wait_ge(s("zt_ready"), 2)
            for x_ in range(E):
                g.indirect_dma_start(xg, bass.IndirectOffsetOnAxis(ap=ZI[:, x_:x_ + 1], axis=0), ZT[:, x_, :], None).then_inc(s("filled_up"), 16)

            pool.sem_inc(s("ye_free"), 2)
            pool.sem_inc(s("gx_free"), 2)

            def put(n, par):
                pool.wait_ge(s("ye_ready"), n)
                pool.wait_ge(s("dix_ready"), n)
                pool.sem_inc(s("gx_free"), 1)
                g.indirect_dma_start(yg, bass.IndirectOffsetOnAxis(ap=DIX[:, par, :], axis=0), YE[:, par, :], None).then_inc(s(f"ye{par}_scattered"), 16)
            for par in range(2):
                put(par + 1, par)
            with pool.Fori(2, SLOTS - 1, 2) as t:
                for par in range(2):
                    pool.wait_ge(s(f"ye{par}_scattered"), t * 8)
                    pool.sem_inc(s("ye_free"), 1)
                    put(t + par + 1, par)

        @block.vector
        def _(dve):
            v = nc.vector
            tt, ts, stt = v.tensor_tensor, v.tensor_scalar, v.scalar_tensor_tensor

            def take_qv(base):
                for h in range(2):
                    q = slice(512 * h, 512 * h + 512)
                    last = stt(QL[:, q], pY[:, q], pcol[:, 2:3], QH[:, q].bitcast(fp32), ALU.add, ALU.subtract)
                last.then_inc(s("q_ready"), NT)

            def take_v():
                tt(V[:], pX[:].rearrange("p (j c) -> p j c", c=C), b2b[:, None, :].broadcast_to([P, NT, C]), ALU.add).then_inc(s("v_ready"), NT)

            def route(base):
                bc = lambda a: a[:, :, None].broadcast_to([P, NT, E])
                steps = Steps(dve, "route_steps", base, -NT, NT, 8)
                then = steps.then
                upto(dve, "lg_ready", base, 0)
                then(v.tensor_reduce(r8[:, 0, :], LG[:], AX.X, ALU.max))
                tt(LG[:], LG[:], bc(r8[:, 0, :]), ALU.subtract).then_inc(s("lsub_ready"), NT)
                upto(dve, "xa_ready", base, 0)
                v.tensor_copy(XA[:, 1, :, 0:C], XA[:, 0, :, 0:C])
                v.tensor_copy(XA[:, 0, :, C + 1], TOK[:])
                ts(XA[:, 1, :, C + 1], TOK[:], float(TOKENS), None, ALU.add)
                upto(dve, "pexp_ready", base, 0)
                then(v.tensor_reduce(r8[:, 1, :], PB[:], AX.X, ALU.add))
                then(v.reciprocal(r8[:, 2, :], r8[:, 1, :]))
                then(ts(TOK[:], TOK[:], float(NT * P), None, ALU.add))
                then(tt(PB[:], PB[:], bc(r8[:, 2, :]), ALU.mult))
                apart(dve)
                for j in range(NT):
                    last = v.max(M8[:, j, :], PB[:, j, :])
                then(last)
                apart(dve)
                for j in range(NT):
                    last = v.max_index(IX[:, j, :], M8[:, j, :], PB[:, j, :])
                then(last)
                then(tt(r8[:, 3, :], M8[:, :, 0], M8[:, :, 1], ALU.add))
                then(ts(r8[:, 4, :], r8[:, 3, :], 1e-9, None, ALU.add))
                then(v.reciprocal(r8[:, 5, :], r8[:, 4, :]))
                for c_ in range(TOP):
                    last = tt(XA[:, c_, :, C], M8[:, :, c_], r8[:, 5, :], ALU.mult)
                last.then_inc(s("xb_ready"), NT)
                then(v.tensor_copy(IXF[:], IX[:, :, 0:TOP]))
                for c_ in range(TOP):
                    last = tt(OH[:, c_], iota8[:, None, :].broadcast_to([P, NT, E]), bc(IXF[:, :, c_]), ALU.is_equal)
                then(last)
                tt(OHS[:], OH[:, 0], OH[:, 1], ALU.add).then_inc(s("onehot_ready"), NT)
                upto(dve, "places_ps", base, 0)
                v.tensor_copy(PCT[:].rearrange("p m a b -> p (m a b)"), pb[:, 0:P]).then_inc(s("places_read"), NT)
                dve.wait_ge(s("places_read"), base + NT)
                for j in range(NT):
                    then(tt(OFF[:, j + 1, :], OFF[:, j, :], PCT[:, 1, j, :], ALU.add))
                then(tt(SA[:], PCT[:, 0], OFF[:, 0:NT, :], ALU.add))
                then(v.tensor_copy(OFF[:, 0, :], OFF[:, NT, :]))
                then(tt(SA[:], SA[:], ebase[:, None, :].broadcast_to([P, NT, E]), ALU.add))
                for c_ in range(TOP):
                    then(tt(PM[:], OH[:, c_], SA[:], ALU.mult))
                    then(v.tensor_reduce(SLF[:, c_, :], PM[:], AX.X, ALU.add), c_ == TOP - 1)
                upto(dve, "xa_free", base, 0)
                v.tensor_copy(SL[:], SLF[:]).then_inc(s("slots_ready"), NT)

            def step(base, i):
                k, e, f = i - LAG, i - LAG - 1, i - 2
                par, half = (k // 2) % 2, k % 2
                front = i % 2 == 0 and i < NT and there(base, f)
                fpar = (f // 2) % 2
                b3 = lambda t: t[:, par, half, :, None].broadcast_to([P, H, HD])
                v3 = lambda t: t[:, 0:DI].rearrange("p (h d) -> p h d", h=H)
                if there(base, k):
                    upto(dve, "xs_ready", base, k + 1)
                    upto(dve, "xw_ready", base, k)
                    upto(dve, "ydiag_ps", base, k)
                    tt(v3(XDT), v3(pa), b3(DT), ALU.mult).then_inc(s("xdt_ready"), 1)
                    upto(dve, "yd_ready", base, k)
                    tt(v3(DX), v3(pa), hrow[:, 2, :, None].broadcast_to([P, H, HD]), ALU.mult).then_inc(s("dx_ready"), 1)
                if there(base, i):
                    upto(dve, "s_ready", base, i + 1)
                    v.tensor_reduce(NM[:, i:i + 1], pX[:], AX.X, ALU.max, negate=True).then_inc(s("nm_ready"), 1)
                if there(base, e):
                    upto(dve, "out_ps", base, e + 1)
                    upto(dve, "ry_ready", base, e + 1)
                    upto(dve, "tr_ready", base, e + 1)
                    t2 = T2[:, bass.ds(base + e, 1), :].rearrange("p a c -> p (a c)")
                    stt(t2, pb[:, 0:C], RY[:, 1, 0:1], TR[:, e % NT, :], ALU.mult, ALU.add).then_inc(s("t2_ready"), 1)
                    upto(dve, "t2_ready", base, e + 1)
                    apart(dve)
                    v.bn_stats(BN2[:, e % NT, :], t2).then_inc(s("bn2_ready"), 1)
                    if e % NT == 0:
                        upto(dve, "rstd2_ready", base, e)
                    upto(dve, "bn2_ready", base, e + 1)
                    apart(dve)
                    v.bn_aggr(MV2[:, e % NT, :], BN2[:, e % NT, :]).then_inc(s("mv2_ready"), 1)
                if front:
                    for j in range(2):
                        bank = (pa, pc)[j]
                        upto(dve, "tz_ready", base, f + j + 1)
                        stt(SZ[:, fpar, j, :], TZ[:, j, :], 1.0, bank[:, 0:DI], ALU.add, ALU.mult).then_inc(s("sz_ready"), 1)
                        tt(dts[:, 0, j, :], bank[:, DI:DI + H], hrow[:, 0, :], ALU.add).then_inc(s("u_ready"), 1)
                    steps = Steps(dve, "softplus_steps", base, f, 2, 8)
                    def chain(n, ins):
                        steps.then(ins, n == 8)
                    upto(dve, "u_ready", base, f + 2)
                    stt(dts[:, 1], dts[:, 0], -1.0, dts[:, 0], ALU.mult, ALU.min).then_inc(s("nau_ready"), 2)
                    ts(dts[:, 3], dts[:, 0], 0.0, None, ALU.max)
                    upto(dve, "enau_ready", base, f + 2)
                    chain(0, ts(dts[:, 4], dts[:, 2], 2.0, None, ALU.add))
                    chain(9, v.reciprocal(dts[:, 9], dts[:, 4]))
                    chain(1, tt(dts[:, 5], dts[:, 2], dts[:, 9], ALU.mult))
                    chain(2, tt(dts[:, 6], dts[:, 5], dts[:, 5], ALU.mult))
                    chain(3, ts(dts[:, 7], dts[:, 6], ATANH[4], None, ALU.mult))
                    chain(4, stt(dts[:, 8], dts[:, 7], ATANH[3], dts[:, 6], ALU.add, ALU.mult))
                    chain(5, stt(dts[:, 7], dts[:, 8], ATANH[2], dts[:, 6], ALU.add, ALU.mult))
                    chain(6, stt(dts[:, 8], dts[:, 7], ATANH[1], dts[:, 6], ALU.add, ALU.mult))
                    chain(7, stt(dts[:, 7], dts[:, 8], ATANH[0], dts[:, 5], ALU.add, ALU.mult))
                    chain(8, stt(DT[:, fpar], dts[:, 7], 2.0, dts[:, 3], ALU.mult, ALU.add))
                    upto(dve, "cum_ps", base, f)
                    stt(AD[:, 0:16].rearrange("p (a b) -> p a b", a=2), DT[:, fpar], -1.0, hrow[:, 1:2, :].broadcast_to([P, 2, H]), ALU.mult, ALU.mult).then_inc(s("ad_ready"), 2)
                if there(base, k):
                    upto(dve, "expD_ready", base, k + 1)
                    upto(dve, "gT_ready", base, k + 1)
                    tt(M[:], ED[:], GT[:, None, :].broadcast_to([P, H, P]), ALU.mult).then_inc(s("m_ready"), 1)
                    upto(dve, "state_ps", base, k + 1)
                    upto(dve, "yd_ready", base, k)
                    if k % NT != 0:
                        tt(v3(YO), v3(pd), b3(ECUM), ALU.mult).then_inc(s("yo_ready"), 1)
                        upto(dve, "yd_ready", base, k + 1)
                        tt(ST[0:NS, :], STE[0:NS, :], pd[0:NS, DI:2 * DI], ALU.add).then_inc(s("st_ready"), 1)
                    else:
                        v.tensor_copy(ST[0:NS, :], pd[0:NS, DI:2 * DI]).then_inc(s("st_ready"), 1)
                        v.nop().then_inc(s("yo_ready"), 1)
                if there(base, i):
                    upto(dve, "pT_ps", base, i + 1)
                    v.tensor_copy(PT[:, 512:], pY[:, 512:]).then_inc(s("pt_dve"), 1)
                if front:
                    fo = (f % NT) * P
                    upto(dve, "cv_evac", base, f + 2)
                    for tap in range(2, -1, -1):
                        for m in range(3):
                            last = stt(CV[:, m, :], XBC[:, m, fo + tap:fo + tap + 256], cw[:, m, tap:tap + 1], CV[:, m, :], ALU.mult, ALU.add)
                        name = "conv_ready" if tap == 0 else f"conv_tap{tap}"
                        last.then_inc(s(name), 2)
                        upto(dve, name, base, f + 2)
                if there(base, k):
                    upto(dve, "ydiag_ps", base, k + 1)
                    upto(dve, "yd_ready", base, k + 1)
                    tt(v3(Y2), pc[:].rearrange("p (h w) -> p h w", h=H)[:, :, 0:HD], v3(YD), ALU.add).then_inc(s("y2_ready"), 1)
                    v.nop().then_inc(s("ydiag_read"), 1)
                    upto(dve, "y2_ready", base, k + 1)
                    upto(dve, "ss_ready", base, k)
                    tt(YG[:], Y2[:], SZ[:, par, half, :], ALU.mult).then_inc(s("yg_ready"), 1)
                if front:
                    upto(dve, "cum_ps", base, f + 2)
                    p3 = lambda a: CT[:, a:a + 16].rearrange("p (a b) -> p a b", a=2)
                    CUM = p3(0)
                    upto(dve, "ecum_ready", base, f)
                    v.tensor_copy(CT[:], pd[:, 0:P]).then_inc(s("cum1"), 2)
                    upto(dve, "cum1", base, f + 2)
                    tt(R1b[:], p3(64), CUM, ALU.subtract).then_inc(s("dec_in"), 2)
                    v.tensor_copy(C3[:, 0], CUM).then_inc(s("cum2"), 2)
                    upto(dve, "cum2", base, f + 2)
                    tt(R1[:], CUM, C3[:, 0], ALU.subtract).then_inc(s("cum3"), 2)
                    upto(dve, "cum3", base, f + 2)
                    v.tensor_copy(C3[:, 1], R1[:]).then_inc(s("cum4"), 2)
                    upto(dve, "cum4", base, f + 2)
                    tt(C3[:, 2], R1[:], C3[:, 1], ALU.subtract).then_inc(s("c3_ready"), 2)
                    upto(dve, "th_ready", base, f + 2)
                    stt(SX[:, fpar].rearrange("p a b -> p (a b)"), TH[:].rearrange("p a b -> p (a b)"), 1.0, CV[:].rearrange("p a b -> p (a b)"), ALU.add, ALU.mult).then_inc(s("sx_ready"), 2)
                if there(base, i):
                    v.reciprocal(RG[:, i:i + 1], RS[:, i:i + 1]).then_inc(s("rcp_ready"), 1)
                    upto(dve, "rcp_ready", base, i + 1)
                    ts(RG[:, i:i + 1], RG[:, i:i + 1], pcol[:, 4:5], None, ALU.mult).then_inc(s("rg_ready"), 1)
                    upto(dve, "rg_ready", base, i + 1)
                    upto(dve, "o_ps", base, i + 1)
                    if i == 0:
                        if isinstance(base, int):
                            dve.wait_ge(s("x_loaded"), 16 * (base // NT + 1))
                        else:
                            dve.wait_ge(s("x_loaded"), base * 2 + 16)
                    stt(TA[:, i, :], pa[:, 0:C], RG[:, i:i + 1], X[:, i, :], ALU.mult, ALU.add).then_inc(s("t_ready"), 1)
                    upto(dve, "t_ready", base, i + 1)
                    v.bn_stats(BN[:, i, :], TA[:, i, :]).then_inc(s("bn_ready"), 1)
                    upto(dve, "bn_ready", base, i + 1)
                    apart(dve)
                    v.bn_aggr(MV[:, i, :], BN[:, i, :]).then_inc(s("mv_ready"), 1)
                if i in (5, 7) and there(base, -NT):
                    grp = (i - 5) // 2
                    upto(dve, "logits_ps", base, 4 * grp - 4)
                    v.tensor_copy(LG[:, 4 * grp:4 * grp + 4, :], pb[:, 0:256].rearrange("p (j w) -> p j w", j=4)[:, :, 0:E]).then_inc(s("lg_ready"), 4)
                if i == 7 and there(base, -NT):
                    route(base)
                if i == NT - 1 and there(base, NT):
                    upto(dve, "projected", base, 2 * NT)
                    take_v()
                    upto(dve, "qh_ready", base, 2 * NT)
                    take_qv(base)

            dve.wait_ge(s("loaded"), 16 * NLOAD)
            dve.wait_ge(s("consts"), 1)
            dve.wait_ge(s("a_exp"), 1)
            ts(pw1s[:], pw1s[:], pcol[:, 0:1], None, ALU.mult)
            ts(pw2s[:], pw2s[:], pcol[:, 1:2], None, ALU.mult)
            ts(wz[:, 0:DI], wz[:, 0:DI], pcol[:, 3:4], 0.5, ALU.mult, ALU.mult)
            ts(wz[:, DI:], wz[:, DI:], pcol[:, 3:4], None, ALU.mult)
            ts(wx[:], wx[:], pcol[:, 3:4], None, ALU.mult)
            ts(cw[:], cw[:], 0.5, None, ALU.mult)
            ts(cb[:], cb[:], 0.5, None, ALU.mult)
            for m in range(2):
                last = ts(wo[:, m, :], wo[:, m, :], gw[:, m:m + 1], None, ALU.mult)
            last.then_inc(s("setup"), 1)
            dve.wait_ge(s("projected"), NT)
            take_v()
            dve.wait_ge(s("qh_ready"), NT)
            take_qv(0)
            batches(dve, step)

            steps = Steps(dve, "table_steps", 0, 0, 1, 64)
            then = steps.then
            runs = OFF[:, 0, :]
            dve.wait_ge(s("iotas"), 2)
            dve.wait_ge(s("route_steps"), 8 * TILES)
            dve.wait_ge(s("slots_ready"), TILES)
            then(tt(NTE[:], runs, ebase[:], ALU.add))
            then(ts(NTE[:], NTE[:], pidx[:, 0:1], 1.0, ALU.add, ALU.add))
            v.tensor_copy(ZI[:], NTE[:]).then_inc(s("zi_ready"), 1)
            dve.wait_ge(s("zi_ready"), 1)
            then(ts(NTE[:], runs, 1.0 / P, (P - 1) / P - 63.5 / P, ALU.mult, ALU.add))
            then(v.tensor_copy(NTI[:], NTE[:]))
            then(v.tensor_copy(NTE[:], NTI[:]))
            then(v.tensor_copy(CTE[:, 0:1], NTE[:, 0:1]))
            for x_ in range(1, E):
                then(tt(CTE[:, x_:x_ + 1], CTE[:, x_ - 1:x_], NTE[:, x_:x_ + 1], ALU.add))
            by = lambda a: a[:, None, :].broadcast_to([P, SLOTS, E])
            then(tt(GE[:], itile[:, :, None].broadcast_to([P, SLOTS, E]), by(CTE), ALU.is_ge))
            then(v.tensor_reduce(TB[:, 0, :], GE[:], AX.X, ALU.add))
            then(tt(GE[:], GE[:], by(NTE), ALU.mult))
            then(v.tensor_reduce(TB[:, 1, :], GE[:], AX.X, ALU.add))
            then(tt(TB[:, 1, :], itile[:], TB[:, 1, :], ALU.subtract))
            then(ts(TB[:, 1, :], TB[:, 1, :], float(P), None, ALU.mult))
            then(stt(TB[:, 2, :], TB[:, 0, :], float(REGION), TB[:, 1, :], ALU.mult, ALU.add))
            then(ts(TB[:, 0, :], TB[:, 0, :], float(E - 1), None, ALU.min))
            v.tensor_copy(TBI[:, 0, :], TB[:, 2, :])
            v.tensor_copy(TBI[:, 1, :], TB[:, 0, :]).then_inc(s("table_ready"), 1)

            def gated(n, par):
                dve.wait_ge(s("silu_ready"), n)
                dve.wait_ge(s("h3_ps"), n)
                tt(HH[:, par, :], SH[:, par, :], pY[:, 512 * par:512 * par + HID], ALU.mult).then_inc(s("hh_ready"), 1)

            def turned(n, par):
                dve.wait_ge(s("hT_ps"), n)
                v.tensor_copy(HT[:, par].rearrange("p k t -> p (k t)"), pc[:, 0:P * len(HC)]).then_inc(s("hT_ready"), 1)

            with dve.Fori(0, SLOTS - 1, 2) as t:
                for par in range(2):
                    gated(t + par + 1, par)
                for par in range(2):
                    turned(t + par + 1, par)
                for par in range(2):
                    dve.wait_ge(s(f"gx{par}_loaded"), t * 8 + 16)
                    dve.wait_ge(s("ye_free"), t + par + 1)
                    v.tensor_copy(DIX[:, par, :], GX[:, par, C + 1:C + 2]).then_inc(s("dix_ready"), 1)
            for b in range(TILES // NT):
                dve.wait_ge(s(f"y{b % 2}_loaded"), 16 * TOP * (b // 2 + 1))
                tiles = T2[:, b * NT:b * NT + NT, :]
                tt(Y01[b % 2][0], Y01[b % 2][0], Y01[b % 2][1], ALU.add).then_inc(s("y_added"), 1)
                dve.wait_ge(s("y_added"), b + 1)
                tt(tiles, tiles, Y01[b % 2][0], ALU.add).then_inc(s("added"), 1)


def kernel(**inputs):
    import numpy as _np
    import concourse.bacc as _bacc
    from concourse import mybir as _mybir
    from concourse.bass_utils import run_bass_kernel_spmd as _run

    a = {name: _np.asarray(v) for name, v in inputs.items()}
    x = a["x"]
    batch, height, width, chans = x.shape
    tokens = x.reshape(batch, height * width, chans)
    ssm = {name: a["L1_attn_" + name] for name in
           ("W_in", "conv_w", "conv_b", "dt_bias", "A_log", "Dp", "gnorm_w", "norm_w", "W_out")}
    inner, conv_dim = ssm["gnorm_w"].shape[0], ssm["conv_b"].shape[0]
    w_in = ssm["W_in"]
    laid_out = {
        "x": tokens.reshape(-1, chans),
        "xT": tokens.transpose(0, 2, 1).reshape(batch * chans, height * width),
        **{name: a["L0_conv_" + name] for name in ("dw1", "pw1", "b1", "dw2", "pw2", "b2", "gamma")},
        "w_zdt": _np.concatenate([w_in[:inner], w_in[inner + conv_dim:]], 0).T,
        "w_xbc": w_in[inner:inner + conv_dim].T,
        "conv_w": ssm["conv_w"], "conv_b": ssm["conv_b"], "dt_bias": ssm["dt_bias"], "a_log": ssm["A_log"],
        "d_skip": ssm["Dp"], "gnorm_w": ssm["gnorm_w"], "norm_w": ssm["norm_w"],
        "w_outT": ssm["W_out"].T,
        "routerT": a["L1_ffn_router_w"].T,
        "w1T": a["L1_ffn_w1"].transpose(0, 2, 1),
        "w3T": a["L1_ffn_w3"].transpose(0, 2, 1),
        "w2T": a["L1_ffn_w2"].transpose(0, 2, 1),
    }
    nc = _bacc.Bacc("TRN2", target_bir_lowering=False, num_devices=1)
    arrays, args = {}, []
    for name, v in laid_out.items():
        v = _np.ascontiguousarray(v)
        arrays[f"in_{name}_dram"] = v
        args.append(nc.dram_tensor(f"in_{name}_dram", v.shape, _mybir.dt.from_np(v.dtype), kind="ExternalInput").ap())
    out = nc.dram_tensor("out_dram", (batch * height * width, chans), _mybir.dt.from_np(x.dtype), kind="ExternalOutput").ap()
    conv_attn_ssm_moe(nc, *args, out)
    r = _run(nc, [arrays], core_ids=[0])
    return r.results[0]["out_dram"].reshape(x.shape)
```

```python
import concourse.bass as bass
from concourse import mybir
from contextlib import ExitStack


def conv_attn_ssm_moe(nc, x, xT, dw1, pw1, b1, dw2, pw2, b2, gamma, w_zdt, w_xbc, conv_w, conv_b,
                      dt_bias, a_log, d_skip, gnorm_w, norm_w, w_outT, routerT, w1T, w3T, w2T, out):
    fp32, bf16, f32r = mybir.dt.float32, mybir.dt.bfloat16, mybir.dt.float32r
    ALU, ACT, AX = mybir.AluOpType, mybir.ActivationFunctionType, mybir.AxisListType
    P = 128
    TILES = x.shape[0] // P
    NT = 8
    SEQ = NT * P
    C = x.shape[1]
    H, HD, NS = 8, 32, 32
    DI = H * HD
    TAPS = 4
    LAG = 5
    ATANH = [1.0, 0.33333157962211934, 0.20012429465084794, 0.1398064909942622, 0.14087686162896493]
    E, TOP = 8, 2
    HID = w1T.shape[2]
    HC = [(P * k, min(P, HID - P * k)) for k in range(-(-HID // P))]
    TOKENS = TILES * P
    REGION = TOKENS + P
    SLOTS = TOP * TILES + E
    ROW = C + 2
    UNUSED = E * (REGION + P)
    GROUP = 4
    PAD = TOP * TOKENS
    LN_EPS, RMS_EPS, FLT_EPS = 1e-5, 1e-5, 1.1920928955078125e-07

    ctx = ExitStack()
    with ctx:
        def sb(name, shape, dt=fp32):
            return ctx.enter_context(nc.sbuf_tensor(name, shape, dt))

        def ps(name, shape, dt=fp32):
            return ctx.enter_context(nc.psum_tensor(name, shape, dt))

        def sem(name):
            return ctx.enter_context(nc.semaphore(name))

        ident = sb("ident", [P, P])
        identb = sb("identb", [P, P], bf16)
        tri = sb("tri", [P, P])
        ones = sb("ones", [P, P])
        later = sb("later", [P, P], bf16)
        pick = sb("pick", [P, 16, P], bf16)
        mhalf = sb("mhalf", [P, 2])
        pw1s, pw2s = sb("pw1s", [P, C]), sb("pw2s", [P, C])
        pcol = sb("pcol", [P, 8])
        b2b = sb("b2b", [P, C])
        wz, wx = sb("wz", [P, DI + H]), sb("wx", [P, 3 * P])
        cw, cb = sb("cw", [P, 3, TAPS]), sb("cb", [P, 3])
        hrow = sb("hrow", [P, 3, H])
        gw = sb("gw", [P, 2])
        wo = sb("wo", [P, 2, C])
        XT, X = sb("XT", [P, SEQ]), sb("X", [P, NT, C])
        QH, QL = sb("QH", [P, SEQ], f32r), sb("QL", [P, SEQ], f32r)
        V = sb("V", [P, NT, C])
        PR, PT = sb("PR", [P, SEQ]), sb("PT", [P, SEQ])
        NM, RS, RG = sb("NM", [P, NT]), sb("RS", [P, NT]), sb("RG", [P, NT])
        TA = sb("TA", [P, NT, C])
        BN = sb("BN", [P, NT, 6])
        MV = sb("MV", [P, NT, 2])
        st = sb("st", [P, 12, 2])
        XN = sb("XN", [P, 2, C])
        TR = sb("TR", [P, NT, C])
        XNT = sb("XNT", [P, 2 * P])
        XBC = sb("XBC", [P, 3, TAPS - 1 + SEQ])
        CV, TH = sb("CV", [P, 3, 2 * P]), sb("TH", [P, 3, 2 * P])
        SX = sb("SX", [P, 2, 3, 2 * P])
        CTP = sb("CTP", [P, 2, 2 * P])
        TZ = sb("TZ", [P, 2, DI])
        SZ = sb("SZ", [P, 2, 2, DI])
        dts = sb("dts", [P, 10, 2, H])
        DT = sb("DT", [P, 2, 2, H])
        AD = sb("AD", [P, 64])
        CT = sb("CT", [P, P])
        ECUM, ETOT, DEC = (sb(n, [P, 2, 2, H]) for n in ("ECUM", "ETOT", "DEC"))
        R1 = sb("R1", [P, 2, H])
        C3 = sb("C3", [P, 3, 2, H], bf16)
        R1b = sb("R1b", [P, 2, H])
        CT3, NCT3 = sb("CT3", [P, 2, P], bf16), sb("NCT3", [P, 2, P], bf16)
        XDT = sb("XDT", [P, DI + HD])
        DX, XW, YO, YD, Y2 = (sb(n, [P, DI]) for n in ("DX", "XW", "YO", "YD", "Y2"))
        YG = sb("YG", [P, DI])
        BNAT, GT = sb("BNAT", [P, P]), sb("GT", [P, P])
        ED, M = sb("ED", [P, H, P]), sb("M", [P, H, P])
        ST, STE = sb("ST", [P, DI]), sb("STE", [P, DI])
        SQ, SS = sb("SQ", [P, DI]), sb("SS", [P, 1])
        RY = sb("RY", [P, 2, 2])
        YT = sb("YT", [P, 2, P])
        T2 = sb("T2", [P, TILES, C])
        BN2, MV2 = sb("BN2", [P, NT, 6]), sb("MV2", [P, NT, 2])
        rs2 = sb("rs2", [P, 3, NT])
        XA = sb("XA", [P, TOP, NT, ROW])
        VT = sb("VT", [P, 4 * P])
        rT = sb("rT", [P, 64])
        LG, PB, OHS, SA, PM = (sb(n, [P, NT, E]) for n in ("LG", "PB", "OHS", "SA", "PM"))
        OH = sb("OH", [P, TOP, NT, E])
        M8 = sb("M8", [P, NT, 8])
        IX = sb("IX", [P, NT, 8], mybir.dt.uint32)
        IXF = sb("IXF", [P, NT, TOP])
        r8 = sb("r8", [P, 6, NT])
        PCT = sb("PCT", [P, 2, NT, E])
        OFF = sb("OFF", [P, NT + 1, E])
        iota8, ebase = sb("iota8", [P, E]), sb("ebase", [P, E])
        TOK = sb("TOK", [P, NT])
        SLF = sb("SLF", [P, TOP, NT])
        SL = sb("SL", [P, TOP, NT], mybir.dt.uint32)
        ZT = sb("ZT", [P, 2 * E, ROW])
        ZI = sb("ZI", [P, E], mybir.dt.uint32)
        pidx = sb("pidx", [P, 1])
        NTE, CTE = sb("NTE", [P, E]), sb("CTE", [P, E])
        NTI = sb("NTI", [P, E], mybir.dt.int32)
        itile = sb("itile", [P, SLOTS])
        GE = XBC[:].rearrange("p m t -> p (m t)")[:, 0:SLOTS * E].rearrange("p (t e) -> p t e", e=E)
        TB = sb("TB", [P, 3, SLOTS])
        TBI = sb("TBI", [P, 2, SLOTS], mybir.dt.int32)
        W1, W3 = sb("W1", [P, E * HID]), sb("W3", [P, E * HID])
        W2 = sb("W2", [P, E, len(HC), C])
        GX = sb("GX", [P, GROUP, ROW])
        GXT = TA[:, 0:2, :]
        SH = XT[:, 0:2 * HID].rearrange("p (a h) -> p a h", a=2)
        HH = X[:].rearrange("p t c -> p (t c)")[:, 0:2 * HID].rearrange("p (a h) -> p a h", a=2)
        HT = V[:].rearrange("p t c -> p (t c)")[:, 0:2 * len(HC) * P].rearrange("p (a k t) -> p a k t", a=2, t=P)
        YE = sb("YE", [P, GROUP, C])
        DIX = sb("DIX", [P, GROUP, 1], mybir.dt.uint32)
        GATE = sb("GATE", [P, GROUP, 1])
        xg = nc.dram_tensor("rows_by_expert", [UNUSED + TOP * NT * P, ROW], fp32, kind="Internal").ap()
        yg = nc.dram_tensor("results_by_choice", [PAD + 2 * E * P, C], fp32, kind="Internal").ap()

        pX, pY = ps("pX", [P, 2 * 512]), ps("pY", [P, 2 * 512])
        pa, pb, pc, pd = (ps(n, [P, 512]) for n in ("pa", "pb", "pc", "pd"))

        S = {}
        Y01 = [[PR, PT], [ED, M]]
        tokens = lambda a: a[:].rearrange("p a b -> p (a b)") if a in (ED, M) else a[:]
        Y01 = [[tokens(a).rearrange("p (t c) -> p t c", c=C) for a in two] for two in Y01]

        def s(name):
            if name not in S:
                S[name] = sem(name)
            return S[name]

        def upto(eng, name, base, c):
            if not isinstance(base, int):
                eng.wait_ge(s(name), base + c)
            elif base + c > 0:
                eng.wait_ge(s(name), min(base + c, TILES))

        def apart(eng):
            eng.sem_inc(s("apart"), 1)

        class Steps:
            def __init__(self, eng, name, base, c, tiles, per_tile):
                self.eng, self.sem, self.n = eng, s(name), 0
                self.start, self.total = base * per_tile + c * per_tile, tiles * per_tile

            def then(self, ins, last=False):
                self.n += 1
                assert self.n < self.total
                if last:
                    ins.then_inc(self.sem, self.total - self.n + 1)
                    self.n = self.total
                else:
                    ins.then_inc(self.sem, 1)
                self.eng.wait_ge(self.sem, self.start + self.n)

        def there(base, c):
            return not isinstance(base, int) or 0 <= base + c < TILES

        block = ctx.enter_context(nc.Block())

        def batches(eng, step):
            for i in range(NT):
                step(0, i)
            with eng.Fori(NT, TILES - 2 * NT + 1, NT) as base:
                for i in range(NT):
                    step(base, i)
            for i in range(NT):
                step(TILES - NT, i)
            for i in range(NT):
                step(TILES, i)

        NLOAD = 5 + 5 + 2 + 3 + 3 + 2 + 1 + 1

        @block.sync
        def _(sp):
            def load(dst, src):
                sp.dma_start(dst, src).then_inc(s("loaded"), 16)
            row = lambda v, n: v.rearrange("(a n) -> a n", a=1).broadcast_to([P, n])
            sp.dma_start(XT[:], xT[0:P, :]).then_inc(s("xT_loaded"), 16)
            xtok = x.rearrange("(t p) c -> p t c", p=P)
            for h in range(2):
                half = slice(h * NT // 2, (h + 1) * NT // 2)
                sp.dma_start(X[:, half, :], xtok[:, half, :]).then_inc(s(f"x{h}_loaded"), 16)
            col = lambda v: v.rearrange("(p a) -> p a", a=1)
            for k, v in enumerate((dw1, dw2, b1, norm_w)):
                load(pcol[:, k:k + 1], col(v))
            load(pcol[:, 4:5], row(gamma, 1))
            load(pw1s[:], pw1)
            load(pw2s[:], pw2)
            load(b2b[:], row(b2, C))
            load(wz[:], w_zdt)
            load(wx[:, 0:DI + 2 * NS], w_xbc)
            sp.wait_ge(s("zeroed"), 1)
            load(cw[:, 0:2, :], conv_w[0:2 * P, :].rearrange("(m p) k -> p m k", p=P))
            load(cw[0:2 * NS, 2, :], conv_w[2 * P:, :])
            for m in range(3):
                part = conv_b[m * P:min((m + 1) * P, DI + 2 * NS)]
                load(cb[0:part.shape[0], m:m + 1], col(part))
            for k, v in enumerate((dt_bias, a_log, d_skip)):
                load(hrow[:, k, :], row(v, H))
            for m in range(2):
                load(gw[:, m:m + 1], col(gnorm_w[m * P:m * P + P]))
            load(wo[:], w_outT.rearrange("(k p) c -> p k c", p=P))
            load(rT[:, 0:E], routerT)
            def load_expert(dst, src):
                sp.dma_start(dst, src).then_inc(s("experts_loaded"), 16)
            load_expert(W1[:].rearrange("p (e h) -> p e h", e=E), w1T.rearrange("e c h -> c e h"))
            load_expert(W3[:].rearrange("p (e h) -> p e h", e=E), w3T.rearrange("e c h -> c e h"))
            for k, (h0, hn) in enumerate(HC):
                load_expert(W2[0:hn, :, k, :], w2T[:, h0:h0 + hn, :].rearrange("e h c -> h e c"))

            def step(base):
                upto(sp, "t_ready", base, NT // 2)
                sp.dma_start(X[:, 0:NT // 2, :], xtok[:, bass.ds(base + NT, NT // 2), :]).then_inc(s("x0_loaded"), 16)
                upto(sp, "projected", base, NT)
                sp.dma_start(XT[:], xT[bass.ds(base * 16 + P, P), :]).then_inc(s("xT_loaded"), 16)
                upto(sp, "t_ready", base, NT)
                sp.dma_start(X[:, NT // 2:, :], xtok[:, bass.ds(base + NT + NT // 2, NT // 2), :]).then_inc(s("x1_loaded"), 16)
            step(0)
            with sp.Fori(NT, TILES - 2 * NT + 1, NT) as base:
                step(base)
            sp.wait_ge(s("zt_ready"), 2)
            sp.dma_start(xg[E * REGION:UNUSED, :].rearrange("(t p) c -> p t c", p=P), ZT[:, E:, :]).then_inc(s("filled_up"), 16)
            sp.wait_ge(s("zi_ready"), 1)
            for x_ in range(E):
                row = sp.value_load(ZI[0:1, x_:x_ + 1], min_val=x_ * REGION, max_val=x_ * REGION + TOKENS)
                sp.dma_start(xg[bass.ds(row, P), :], ZT[:, x_, :]).then_inc(s("filled_up"), 16)
            sp.wait_ge(s("table_ready"), 1)
            sp.wait_ge(s("scattered"), 16 * TOP * (TILES + NT))
            sp.wait_ge(s("filled_up"), 16 * (E + 1))

            def fetch(t, j):
                row = sp.value_load(TBI[0:1, 0, bass.ds(t + j, 1)], min_val=0, max_val=E * REGION + (E - 1) * P)
                if not (isinstance(t, int) and t == 0):
                    sp.wait_ge(s("gxt_ps"), t + j + 1 - GROUP)
                    sp.wait_ge(s("dix_ready"), t + j + 1 - GROUP)
                sp.dma_start(GX[:, j, :], xg[bass.ds(row, P), :]).then_inc(s(f"gx{j}_loaded"), 16)
            for j in range(GROUP):
                fetch(0, j)
            with sp.Fori(GROUP, SLOTS - GROUP + 1, GROUP) as t:
                for j in range(GROUP):
                    fetch(t, j)
            for j in range(GROUP):
                sp.wait_ge(s(f"ye{j}_scattered"), 16 // GROUP * SLOTS)
            otok = out.rearrange("(t p) c -> p t c", p=P)

            def y_load(b, base, par):
                for k in range(TOP):
                    src = yg[bass.ds(base * P + k * TOKENS, NT * P), :].rearrange("(t p) c -> p t c", p=P)
                    sp.dma_start(Y01[par][k], src).then_inc(s(f"y{par}_loaded"), 16)
            for b in range(TILES // NT):
                if b >= 2:
                    sp.wait_ge(s("added"), b - 1)
                y_load(b, b * NT, b % 2)
                if b >= 1:
                    sp.wait_ge(s("added"), b)
                    sp.dma_start(otok[:, (b - 1) * NT:b * NT, :], T2[:, (b - 1) * NT:b * NT, :]).then_inc(s("stored"), 16)
            sp.wait_ge(s("added"), TILES // NT)
            sp.dma_start(otok[:, TILES - NT:, :], T2[:, TILES - NT:, :]).then_inc(s("stored"), 16)
            sp.wait_ge(s("stored"), 16 * (TILES // NT))

        @block.tensor
        def _(pe):
            mm = nc.tensor.matmul

            def project_q():
                for h in range(2):
                    last = mm(pY[:, 512 * h:512 * h + 512], pw1s[:], XT[:, 512 * h:512 * h + 512], start=True, stop=True)
                last.then_inc(s("qps"), NT)

            def project_v():
                for j in range(NT):
                    last = mm(pX[:, P * j:P * j + P], XT[:, P * j:P * j + P], pw2s[:], start=True, stop=True)
                last.then_inc(s("projected"), NT)

            def step(base, i):
                o, k, e = i - 1, i - LAG, i - LAG - 1
                fa, fb = i - 3, i - 4
                front_a, front_b = i % 2 == 1 and there(base, fa), i % 2 == 0 and there(base, fb)
                par, half = (k // 2) % 2, k % 2
                tk = slice(P * half, P * half + P)
                if there(base, o):
                    if i == 0 and there(base, 0):
                        upto(pe, "q_ready", base, NT)
                    upto(pe, "exp_ready", base, o + 1)
                    upto(pe, "expD_ready", base, k)
                    for j in range(NT):
                        last = nc.tensor.transpose(pY[:, P * j:P * j + P], PR[:, P * j:P * j + P], ident[:])
                    last.then_inc(s("pT_ps"), 1)
                if front_b:
                    upto(pe, "xbc01_evac", base, fb + 2)
                    upto(pe, "y2_ready", base, k)
                    mm(pc[:, 0:DI + H], XNT[:, 0:P], wz[:], start=True, stop=True).then_inc(s("z_ps"), 1)
                    upto(pe, "st_ready", base, k)
                    upto(pe, "yo_ready", base, k)
                    mm(pd[:, 0:DI + H], XNT[:, P:2 * P], wz[:], start=True, stop=True).then_inc(s("z_ps"), 1)
                if there(base, i):
                    upto(pe, "q_ready", base, NT)
                    upto(pe, "exp_ready", base, i)
                    if i == 1:
                        upto(pe, "v_ready", base, NT)
                    for h in range(2):
                        q = slice(512 * h, 512 * h + 512)
                        ti = slice(P * i, P * i + P)
                        mm(pX[:, q], QH[:, ti], QH[:, q], start=True, stop=False)
                        mm(pX[:, q], QH[:, ti], QL[:, q], start=False, stop=False)
                        last = mm(pX[:, q], QL[:, ti], QH[:, q], start=False, stop=True)
                    last.then_inc(s("s_ready"), 1)
                if there(base, k):
                    upto(pe, "bc_ready", base, k + 1)
                    upto(pe, "t_ready", base, o)
                    for m in range(3):
                        last = nc.tensor.transpose(pa[:, P * m:P * m + P], SX[:, par, m, tk], ident[:])
                    mm(pa[:, 3 * P:4 * P], SX[:, par, 2, tk], CTP[:, par, tk], start=True, stop=True, skip_group_check=True).then_inc(s("xs_ready"), 1)
                if front_a:
                    upto(pe, "xn_ready", base, fa + 2)
                    upto(pe, "y2_ready", base, k)
                    for j in range(2):
                        last = nc.tensor.transpose(pc[:, P * j:P * j + P], XN[:, j, :], ident[:])
                    last.then_inc(s("xnT_ps"), 2)
                if there(base, e):
                    upto(pe, "yg_ready", base, e + 1)
                    upto(pe, "t2_ready", base, e)
                    if i % 2 == 0:
                        upto(pe, "cv_evac", base, i - 2)
                    else:
                        upto(pe, "ct3_ready", base, i - 3)
                    if i == 7:
                        upto(pe, "lg_ready", base, 0)
                    if i == 0:
                        upto(pe, "places_read", base, 0)
                    for m in range(2):
                        last = nc.tensor.transpose(pb[:, P * m:P * m + P], YG[:, P * m:P * m + P], ident[:])
                    last.then_inc(s("yT_ps"), 1)
                if there(base, k):
                    upto(pe, "ct3_ready", base, k + 1)
                    upto(pe, "pt_dve", base, o + 1)
                    upto(pe, "pt_act", base, o + 1)
                    for h2 in range(2):
                        q = slice(512 * h2, 512 * h2 + 512)
                        mm(pY[:, q], identb[:], later[:, None, :].broadcast_to([P, 4, P]), start=True, stop=False, skip_group_check=True)
                        mm(pY[:, q], NCT3[:, par, :], pick[:, half * H + 4 * h2:half * H + 4 * h2 + 4, :], start=False, stop=False, skip_group_check=True)
                    for h in range(H):
                        last = mm(pY[:, P * h:P * h + P], pick[:, half * H + h, :], CT3[:, par, :], start=False, stop=True, skip_group_check=True)
                    last.then_inc(s("d_ps"), 1)
                if front_a:
                    upto(pe, "xnT_ready", base, fa + 2)
                    for m in range(2):
                        last = mm(pc[:, 256 * m:256 * m + 256], wx[:, P * m:P * m + P], XNT[:], start=True, stop=True, skip_group_check=True)
                    last.then_inc(s("xbc01_ps"), 2)
                if there(base, e):
                    upto(pe, "yT_ready", base, e + 1)
                    for m in range(2):
                        last = mm(pb[:, 0:C], YT[:, m, :], wo[:, m, :], start=m == 0, stop=m == 1)
                    last.then_inc(s("out_ps"), 1)
                if there(base, o):
                    upto(pe, "pt_act", base, o + 1)
                    upto(pe, "pt_dve", base, o + 1)
                    upto(pe, "dx_ready", base, k + 1)
                    upto(pe, "gT_ready", base, k + 1)
                    upto(pe, "t_ready", base, o)
                    if o >= 0:
                        upto(pe, "v_ready", base, NT)
                    for j in range(NT):
                        last = mm(pa[:, 0:C], PT[:, P * j:P * j + P], V[:, j, :], start=j == 0, stop=j == NT - 1)
                    last.then_inc(s("o_ps"), 1)
                if front_a:
                    upto(pe, "t2_ready", base, e + 1)
                    mm(pb[:, 0:256], wx[:, 2 * P:3 * P], XNT[:], start=True, stop=True).then_inc(s("xbc2_ps"), 2)
                if there(base, k):
                    upto(pe, "xw_ready", base, k + 1)
                    upto(pe, "bnat_ready", base, k + 1)
                    upto(pe, "st_ready", base, k)
                    upto(pe, "yo_ready", base, k)
                    if front_b:
                        upto(pe, "u_ready", base, fb + 2)
                    if k % NT != 0:
                        mm(pd[:, 0:DI], CTP[:, par, tk], ST[:], start=True, stop=True)
                    last = mm(pd[:, DI:2 * DI], BNAT[:], XW[:], start=k % NT == 0, stop=True, skip_group_check=True)
                    last.then_inc(s("state_ps"), 1)
                if front_b:
                    upto(pe, "ad_ready", base, fb + 2)
                    upto(pe, "t2_ready", base, e + 1)
                    mm(pb[:, 0:64], tri[:], AD[:], start=True, stop=True, skip_group_check=True)
                    mm(pb[:, 64:128], ones[:], AD[:], start=True, stop=True, skip_group_check=True).then_inc(s("cum_ps"), 2)
                if there(base, k):
                    upto(pe, "m_ready", base, k + 1)
                    upto(pe, "xdt_ready", base, k + 1)
                    upto(pe, "y2_ready", base, k)
                    if front_b:
                        upto(pe, "u_ready", base, fb + 2)
                    if front_a:
                        upto(pe, "xbc01_evac", base, fa + 2)
                    for h in range(H):
                        last = mm(pc[:, 64 * h:64 * h + 64], M[:, h, :], XDT[:, HD * h:HD * h + 64], start=True, stop=True, skip_group_check=True)
                    last.then_inc(s("ydiag_ps"), 1)
                if front_b:
                    upto(pe, "c3_ready", base, fb + 2)
                    upto(pe, "ecum_ready", base, fb + 2)
                    nc.tensor.transpose(pb[:, :].bitcast(bf16)[0:48, 0:P], C3[:].rearrange("p a b c -> p (a b c)"), identb[:]).then_inc(s("ct3_ps"), 2)
                if i == 0 and there(base, 0):
                    upto(pe, "exp_ready", base, 1)
                    project_v()
                if i == 6 and there(base, -NT):
                    upto(pe, "xa_ready", base, 0)
                    upto(pe, "ct3_ready", base, fb + 2)
                    upto(pe, "t2_ready", base, e + 1)
                    for grp in range(2):
                        if grp:
                            upto(pe, "lg_ready", base, -4)
                        for j in range(4):
                            last = nc.tensor.transpose(pb[:, P * j:P * j + P], XA[:, 0, 4 * grp + j, 0:C], ident[:])
                        last.then_inc(s("vT_ps"), 4)
                        upto(pe, "vT_ready", base, 4 * grp - 4)
                        for j in range(4):
                            last = mm(pb[:, 64 * j:64 * j + 64], VT[:, P * j:P * j + P], rT[:], start=True, stop=True, skip_group_check=True)
                        last.then_inc(s("logits_ps"), 4)
                if i == 7 and there(base, -NT):
                    upto(pe, "onehot_ready", base, 0)
                    upto(pe, "cv_evac", base, fa + 2)
                    upto(pe, "t2_ready", base, e + 1)
                    for m, l in enumerate((tri, ones)):
                        last = mm(pb[:, 64 * m:64 * m + 64], l[:], OHS[:].rearrange("p a b -> p (a b)"), start=True, stop=True, skip_group_check=True)
                    last.then_inc(s("places_ps"), NT)
                if i == NT - 1 and there(base, NT):
                    if isinstance(base, int):
                        pe.wait_ge(s("xT_loaded"), 16 * (base // NT + 2))
                    else:
                        pe.wait_ge(s("xT_loaded"), base * 2 + 32)
                    upto(pe, "expD_ready", base, k + 1)
                    upto(pe, "pt_act", base, o + 1)
                    upto(pe, "pt_dve", base, o + 1)
                    project_q()

            pe.wait_ge(s("setup"), 1)
            pe.wait_ge(s("xT_loaded"), 16)
            project_q()
            batches(pe, step)

            pe.wait_ge(s("experts_loaded"), 16 * 5)
            pe.wait_ge(s("table_ready"), 1)

            def x_T(t, j):
                j, t = j % GROUP, t + j // GROUP * GROUP
                pe.wait_ge(s(f"gx{j}_loaded"), t * 4 + 16)
                nc.tensor.transpose(pa[:, 0:P], GX[:, j, 0:C], ident[:]).then_inc(s("gxt_ps"), 1)

            def expert_of(t, j):
                return pe.value_load(TBI[0:1, 1, bass.ds(t + j, 1)], min_val=0, max_val=E - 1)

            def hidden(n, par, expert):
                pe.wait_ge(s("gxt_ready"), n)
                for w, bank in ((W1, pX), (W3, pY)):
                    last = mm(bank[:, 512 * par:512 * par + HID], GXT[:, par, :], w[:, bass.ds(expert * HID, HID)], start=True, stop=True)
                    last.then_inc(s("h1_ps" if w is W1 else "h3_ps"), 1)

            def hidden_T(n, par):
                pe.wait_ge(s("hh_ready"), n)
                for k, (h0, hn) in enumerate(HC):
                    last = nc.tensor.transpose(pc[0:hn, P * k:P * k + P], HH[:, par, h0:h0 + hn], ident[:])
                last.then_inc(s("hT_ps"), 1)

            def result(n, par, expert):
                pe.wait_ge(s("hT_ready"), n)
                if not isinstance(n, int) or n > 2:
                    pe.wait_ge(s("ye_ready"), n - 2)
                for k, (h0, hn) in enumerate(HC):
                    last = mm((pd, pb)[par][:, 0:C], HT[0:hn, par, k, :], W2[0:hn, bass.ds(expert, 1), k, :], start=k == 0, stop=k == len(HC) - 1)
                last.then_inc(s("y_ps"), 1)

            def group(t):
                experts = [expert_of(t, j) for j in range(GROUP)]
                before = None if isinstance(t, int) and t == 0 else expert_of(t, -1)
                for j in range(GROUP):
                    hidden(t + j + 1, j % 2, experts[j])
                    if not (isinstance(t, int) and t + j == SLOTS - 1):
                        x_T(t, j + 1)
                    if j or before is not None:
                        result(t + j, (j - 1) % 2, experts[j - 1] if j else before)
                    hidden_T(t + j + 1, j % 2)
            x_T(0, 0)
            group(0)
            with pe.Fori(GROUP, SLOTS - 2 * GROUP + 1, GROUP) as t:
                group(t)
            group(SLOTS - GROUP)
            result(SLOTS, (SLOTS - 1) % 2, expert_of(SLOTS - 1, 0))

        @block.scalar
        def _(act):
            A = nc.scalar.activation

            def take_q():
                for h in range(2):
                    q = slice(512 * h, 512 * h + 512)
                    last = A(QH[:, q], pY[:, q], ACT.Identity, bias=pcol[:, 2:3])
                last.then_inc(s("qh_ready"), NT)

            def step(base, i):
                o, k, e = i - 1, i - LAG, i - LAG - 1
                fa, fb = i - 3, i - 4
                front_a, front_b = i % 2 == 1 and there(base, fa), i % 2 == 0 and there(base, fb)
                fpar = (fb // 2) % 2
                if there(base, o):
                    upto(act, "pT_ps", base, o + 1)
                    upto(act, "o_ps", base, o)
                    A(PT[:, 0:512], pY[:, 0:512], ACT.Copy).then_inc(s("pt_act"), 1)
                if front_b:
                    for j in range(2):
                        upto(act, "z_ps", base, fb + j + 1)
                        upto(act, "sz_ready", base, fb)
                        A(TZ[:, j, :], (pc, pd)[j][:, 0:DI], ACT.Tanh).then_inc(s("tz_ready"), 1)
                if there(base, e):
                    upto(act, "yT_ps", base, e + 1)
                    A(YT[:].rearrange("p a b -> p (a b)"), pb[:, 0:DI], ACT.Copy).then_inc(s("yT_ready"), 1)
                if front_a:
                    upto(act, "xnT_ps", base, fa + 2)
                    A(XNT[:], pc[:, 0:2 * P], ACT.Copy).then_inc(s("xnT_ready"), 2)
                if there(base, i):
                    upto(act, "nm_ready", base, i + 1)
                    upto(act, "pT_ps", base, i)
                    upto(act, "rg_ready", base, i - 1)
                    A(PR[:], pX[:], ACT.Exp, bias=NM[:, i:i + 1], accum_out=RS[:, i:i + 1]).then_inc(s("exp_ready"), 1)
                if there(base, k):
                    upto(act, "dx_ready", base, k + 1)
                    upto(act, "state_ps", base, k)
                    A(BNAT[:], pa[:, 2 * P:3 * P], ACT.Copy).then_inc(s("bnat_ready"), 1)
                    upto(act, "m_ready", base, k)
                    A(GT[:], pa[:, 3 * P:4 * P], ACT.Copy).then_inc(s("gT_ready"), 1)
                if front_a:
                    fo = (fa % NT) * P + TAPS - 1
                    upto(act, "xbc01_ps", base, fa + 2)
                    A(XBC[:, 0:2, fo:fo + 256], pc[:].rearrange("p (m t) -> p m t", m=2), ACT.Copy).then_inc(s("xbc01_evac"), 2)
                if there(base, k):
                    upto(act, "d_ps", base, k + 1)
                    A(ED[:].rearrange("p h t -> p (h t)"), pY[:], ACT.Exp).then_inc(s("expD_ready"), 1)
                if front_b:
                    upto(act, "nau_ready", base, fb + 2)
                    A(dts[:, 2], dts[:, 1], ACT.Exp).then_inc(s("enau_ready"), 2)
                    upto(act, "conv_ready", base, fb + 2)
                    A(TH[:], CV[:], ACT.Tanh).then_inc(s("th_ready"), 2)
                if front_a:
                    upto(act, "xbc01_evac", base, fa + 2)
                    upto(act, "sx_ready", base, fa)
                    for m in range(2):
                        A(CV[:, m, :], XBC[:, m, fo:fo + 256], ACT.Identity, bias=cb[:, m:m + 1], scale=cw[:, m, 3:4])
                    upto(act, "xbc2_ps", base, fa + 2)
                    A(XBC[:, 2, fo:fo + 256], pb[:, 0:256], ACT.Copy)
                    A(CV[:, 2, :], pb[:, 0:256], ACT.Identity, bias=cb[:, 2:3], scale=cw[:, 2, 3:4]).then_inc(s("cv_evac"), 2)
                if front_b:
                    upto(act, "cum1", base, fb + 2)
                    A(ECUM[:, fpar], CT[:, 0:16].rearrange("p (a b) -> p a b", a=2), ACT.Exp)
                    A(ETOT[:, fpar], CT[:, 64:80].rearrange("p (a b) -> p a b", a=2), ACT.Exp).then_inc(s("ecum_ready"), 2)
                    upto(act, "dec_in", base, fb + 2)
                    A(DEC[:, fpar], R1b[:], ACT.Exp).then_inc(s("dec_exp"), 2)
                    upto(act, "ct3_ps", base, fb + 2)
                    A(CT3[0:48, fpar, :], pb[:, :].bitcast(bf16)[0:48, 0:P], ACT.Copy)
                    A(NCT3[0:48, fpar, :], pb[:, :].bitcast(bf16)[0:48, 0:P], ACT.Copy, scale=-1.0).then_inc(s("ct3_ready"), 2)
                    upto(act, "sx_ready", base, fb + 2)
                    A(CTP[0:NS, fpar, :], SX[NS:2 * NS, fpar, 2, :], ACT.Copy).then_inc(s("bc_ready"), 2)
                if there(base, k):
                    upto(act, "yg_ready", base, k + 1)
                    upto(act, "sst_ready", base, k)
                    A(SQ[:], YG[:], ACT.Square, accum_out=SS[:]).then_inc(s("ss_ready"), 1)
                if i == 6 and there(base, -NT):
                    upto(act, "rstd2_ready", base, 0)
                    act.wait_ge(s("scattered"), base * (16 * TOP))
                    for j in range(NT):
                        last = A(XA[:, 0, j, 0:C], T2[:, bass.ds(base - NT + j, 1), :].rearrange("p a c -> p (a c)"), ACT.Identity, bias=rs2[:, 2, j:j + 1], scale=rs2[:, 1, j:j + 1])
                    last.then_inc(s("xa_ready"), NT)
                    for grp in range(2):
                        upto(act, "vT_ps", base, 4 * grp - 4)
                        A(VT[:], pb[:], ACT.Copy).then_inc(s("vT_ready"), 4)
                    upto(act, "lsub_ready", base, 0)
                    A(PB[:], LG[:], ACT.Exp).then_inc(s("pexp_ready"), NT)
                if i == NT - 1 and there(base, NT):
                    upto(act, "qps", base, 2 * NT)
                    upto(act, "s_ready", base, NT)
                    take_q()

            act.wait_ge(s("loaded"), 16 * NLOAD)
            A(hrow[:, 1, :], hrow[:, 1, :], ACT.Exp).then_inc(s("a_exp"), 1)
            act.wait_ge(s("qps"), NT)
            take_q()
            batches(act, step)

            def rows_T(n, par):
                act.wait_ge(s("gxt_ps"), n)
                A(GXT[:, par, :], pa[:, 0:P], ACT.Copy).then_inc(s("gxt_ready"), 1)

            def silu(n, par):
                act.wait_ge(s("h1_ps"), n)
                A(SH[:, par, :], pX[:, 512 * par:512 * par + HID], ACT.Silu).then_inc(s("silu_ready"), 1)

            def gate(t, j):
                n = t + j + 1
                act.wait_ge(s("y_ps"), n)
                act.wait_ge(s("dix_ready"), n)
                if not (isinstance(t, int) and t == 0):
                    act.wait_ge(s(f"ye{j}_scattered"), t * 4)
                A(YE[:, j, :], (pd, pb)[j % 2][:, 0:C], ACT.Copy, scale=GATE[:, j, 0:1]).then_inc(s("ye_ready"), 1)

            def group(t):
                for j in range(GROUP):
                    silu(t + j + 1, j % 2)
                    if not (isinstance(t, int) and t + j == SLOTS - 1):
                        rows_T(t + j + 2, (j + 1) % 2)
                    if j:
                        gate(t, j - 1)
                    elif not (isinstance(t, int) and t == 0):
                        gate(t - GROUP, GROUP - 1)
            A(SS[:], SS[:], ACT.Silu)
            rows_T(1, 0)
            group(0)
            with act.Fori(GROUP, SLOTS - 2 * GROUP + 1, GROUP) as t:
                group(t)
            group(SLOTS - GROUP)
            gate(SLOTS - GROUP, GROUP - 1)

        @block.gpsimd
        def _(pool):
            g = nc.gpsimd
            g.memset(cw[:], 0.0)
            g.memset(cb[:], 0.0).then_inc(s("zeroed"), 1)
            for t, v in ((wx[:, DI + 2 * NS:], 0.0), (CTP[:], 0.0), (XBC[:, :, 0:TAPS - 1], 0.0), (AD[:], 0.0), (CT3[:], 0.0),
                         (NCT3[:], 0.0), (ST[:], 0.0), (XDT[:, DI:], 0.0), (ones[:], 1.0), (mhalf[:], -0.5)):
                g.memset(t, v)
            g.memset(tri[:], 1.0)
            g.memset(later[:], 0.0)
            g.memset(pick[:], 0.0)
            g.memset(ident[:], 0.0).then_inc(s("filled"), 1)
            pool.wait_ge(s("filled"), 1)
            g.affine_select(out=tri[:], in_=tri[:], compare_op=ALU.is_ge, fill=0.0, base=0, pattern=[[1, P]], channel_multiplier=-1)
            g.affine_select(out=later[:], in_=later[:], compare_op=ALU.is_ge, fill=-1e30, base=0, pattern=[[1, P]], channel_multiplier=-1)
            for j in range(3):
                g.affine_select(out=pick[:], in_=pick[:], compare_op=ALU.not_equal, fill=1.0, base=-16 * j,
                                pattern=[[-1, 16], [0, P]], channel_multiplier=1).then_inc(s("picked"), 1)
                pool.wait_ge(s("picked"), j + 1)
            g.affine_select(out=ident[:], in_=ident[:], compare_op=ALU.not_equal, fill=1.0, base=0, pattern=[[-1, P]], channel_multiplier=1).then_inc(s("filled"), 1)
            pool.wait_ge(s("filled"), 2)
            g.tensor_copy(identb[:], ident[:]).then_inc(s("consts"), 1)
            pool.sem_inc(s("places_read"), NT)
            g.memset(rT[:, E:], 0.0)
            g.memset(OFF[:], 0.0)
            g.memset(ZT[:], 0.0).then_inc(s("zt_ready"), 1)
            lazy = dict(allow_small_or_imprecise_dtypes=True)
            g.memset(XA[:], 0.0)
            g.iota(SL[:].rearrange("p c j -> p (c j)"), [[P, TOP * NT]], base=UNUSED, channel_multiplier=1)
            g.iota(iota8[:], [[1, E]], base=0, channel_multiplier=0, **lazy)
            g.iota(TOK[:], [[P, NT]], base=0, channel_multiplier=1, **lazy)
            g.iota(pidx[:], [[0, 1]], base=0, channel_multiplier=1, **lazy)
            g.iota(itile[:], [[1, SLOTS]], base=0, channel_multiplier=0, **lazy)
            g.iota(TB[:, 0, 0:2 * E], [[P, 2 * E]], base=PAD, channel_multiplier=1, **lazy).then_inc(s("iotas"), 1)
            pool.wait_ge(s("iotas"), 1)
            pool.wait_ge(s("zt_ready"), 1)
            g.tensor_copy(ZT[:, :, C + 1], TB[:, 0, 0:2 * E]).then_inc(s("zt_ready"), 1)
            g.tensor_scalar(ebase[:], iota8[:], float(REGION), -1.0, ALU.mult, ALU.add).then_inc(s("iotas"), 1)

            def step(base, i):
                o, k, e = i - 1, i - LAG, i - LAG - 1
                fn = i - 2
                par, half = (k // 2) % 2, k % 2
                if i == 6 and there(base, -NT):
                    upto(pool, "mv2_ready", base, 0)
                    steps = Steps(pool, "norm2_steps", base, -NT, NT, 1)
                    apart(pool)
                    steps.then(g.tensor_scalar(rs2[:, 0, :], MV2[:, :, 1], LN_EPS, 1.0, ALU.add, ALU.mult))
                    steps.then(g.tensor_tensor(rs2[:, 1, :], rs2[:, 0, :], mhalf[:, 0:1].broadcast_to([P, NT]), ALU.pow))
                    steps.then(g.tensor_tensor(rs2[:, 0, :], MV2[:, :, 0], rs2[:, 1, :], ALU.mult), True)
                    apart(pool)
                    g.tensor_scalar(rs2[:, 2, :], rs2[:, 0, :], -1.0, 1.0, ALU.mult, ALU.mult).then_inc(s("rstd2_ready"), NT)
                if there(base, e):
                    upto(pool, "ss_ready", base, e + 1)
                    upto(pool, "t2_ready", base, e)
                    apart(pool)
                    g.tensor_scalar(RY[:, 0, 0:1], SS[:], 1.0 / DI, RMS_EPS, ALU.mult, ALU.add).then_inc(s("sst_ready"), 1)
                    upto(pool, "sst_ready", base, e + 1)
                    g.tensor_tensor(RY[:, 1, 0:1], RY[:, 0, 0:1], mhalf[:, 0:1], ALU.pow).then_inc(s("ry_ready"), 1)
                if there(base, k):
                    b3 = lambda t: t[:, par, half, :, None].broadcast_to([P, H, HD])
                    v3 = lambda t: t[:, 0:DI].rearrange("p (h d) -> p h d", h=H)
                    if k % NT != 0:
                        upto(pool, "st_ready", base, k)
                        g.tensor_tensor(v3(STE)[0:NS], v3(ST)[0:NS], ETOT[0:NS, par, half, :, None].broadcast_to([NS, H, HD]), ALU.mult).then_inc(s("ste_ready"), 1)
                    else:
                        pool.sem_inc(s("ste_ready"), 1)
                    upto(pool, "xdt_ready", base, k + 1)
                    upto(pool, "dec_exp", base, k + 1)
                    upto(pool, "state_ps", base, k)
                    g.tensor_tensor(v3(XW), v3(XDT), b3(DEC), ALU.mult).then_inc(s("xw_ready"), 1)
                if i < 6 and there(base, -2 * NT):
                    if i == 0:
                        upto(pool, "slots_ready", base, -NT)
                        upto(pool, "xb_ready", base, -NT)
                        apart(pool)
                    for j in range(3 * i, min(3 * i + 3, TOP * NT)):
                        scatter_rows(j)
                if there(base, k):
                    upto(pool, "dx_ready", base, k + 1)
                    upto(pool, "y2_ready", base, k)
                    if k % NT != 0:
                        upto(pool, "yo_ready", base, k + 1)
                        g.tensor_tensor(YD[:], YO[:], DX[:], ALU.add).then_inc(s("yd_ready"), 1)
                    else:
                        apart(pool)
                        g.tensor_copy(YD[:], DX[:]).then_inc(s("yd_ready"), 1)
                if i % 2 == 0 and there(base, fn):
                    mean, var = MV[:, fn % NT:fn % NT + 2, 0], MV[:, fn % NT:fn % NT + 2, 1]
                    upto(pool, "mv_ready", base, fn + 2)
                    steps = Steps(pool, "norm_steps", base, fn, 2, 8)
                    def chain(n, ins):
                        steps.then(ins, n == 7)
                    apart(pool)
                    chain(0, g.tensor_scalar(st[:, 0, :], var, LN_EPS, 1.0, ALU.add, ALU.mult))
                    chain(1, g.tensor_tensor(st[:, 1, :], st[:, 0, :], mhalf[:], ALU.pow))
                    chain(2, g.tensor_tensor(st[:, 2, :], st[:, 1, :], st[:, 1, :], ALU.mult))
                    chain(3, g.tensor_tensor(st[:, 3, :], st[:, 2, :], var, ALU.mult))
                    apart(pool)
                    chain(4, g.tensor_scalar(st[:, 4, :], st[:, 3, :], FLT_EPS, 1.0, ALU.add, ALU.mult))
                    chain(5, g.tensor_tensor(st[:, 5, :], st[:, 4, :], mhalf[:], ALU.pow))
                    chain(6, g.tensor_tensor(st[:, 6, :], st[:, 5, :], st[:, 1, :], ALU.mult))
                    apart(pool)
                    g.tensor_scalar(st[:, 8, :], st[:, 1, :], 1.0, 1.0, ALU.add, ALU.mult)
                    g.tensor_tensor(st[:, 9, :], mean, st[:, 1, :], ALU.mult)
                    chain(7, g.tensor_tensor(st[:, 7, :], mean, st[:, 6, :], ALU.mult))
                    upto(pool, "xnT_ps", base, fn)
                    for j in range(2):
                        apart(pool)
                        last = g.tensor_scalar(XN[:, j, :], TA[:, fn % NT + j, :], st[:, 6, j:j + 1], st[:, 7, j:j + 1], ALU.mult, ALU.subtract)
                    last.then_inc(s("xn_ready"), 2)
                    for j in range(2):
                        apart(pool)
                        last = g.tensor_scalar(TR[:, fn % NT + j, :], TA[:, fn % NT + j, :], st[:, 8, j:j + 1], st[:, 9, j:j + 1], ALU.mult, ALU.subtract)
                    last.then_inc(s("tr_ready"), 2)

            def scatter_rows(j):
                g.indirect_dma_start(xg, bass.IndirectOffsetOnAxis(ap=SL[:, j // NT, j % NT:j % NT + 1], axis=0), XA[:, j // NT, j % NT, :], None).then_inc(s("scattered"), 16)

            batches(pool, step)
            pool.wait_ge(s("slots_ready"), TILES)
            pool.wait_ge(s("xb_ready"), TILES)
            for j in range(TOP * NT):
                scatter_rows(j)

            def put(t, j):
                pool.wait_ge(s("ye_ready"), t + j + 1)
                apart(pool)
                g.indirect_dma_start(yg, bass.IndirectOffsetOnAxis(ap=DIX[:, j, :], axis=0), YE[:, j, :], None).then_inc(s(f"ye{j}_scattered"), 16)
            with pool.Fori(0, SLOTS - GROUP + 1, GROUP) as t:
                for j in range(GROUP):
                    put(t, j)

        @block.vector
        def _(dve):
            v = nc.vector
            tt, ts, stt = v.tensor_tensor, v.tensor_scalar, v.scalar_tensor_tensor

            def take_qv(base):
                for h in range(2):
                    q = slice(512 * h, 512 * h + 512)
                    last = stt(QL[:, q], pY[:, q], pcol[:, 2:3], QH[:, q].bitcast(fp32), ALU.add, ALU.subtract)
                last.then_inc(s("q_ready"), NT)

            def take_v():
                tt(V[:], pX[:].rearrange("p (j c) -> p j c", c=C), b2b[:, None, :].broadcast_to([P, NT, C]), ALU.add).then_inc(s("v_ready"), NT)

            def route_a(base):
                bc = lambda a: a[:, :, None].broadcast_to([P, NT, E])
                steps = Steps(dve, "route_a_steps", base, -NT, NT, 4)
                then = steps.then
                v.tensor_copy(XA[:, 1, :, 0:C], XA[:, 0, :, 0:C])
                v.tensor_copy(XA[:, 0, :, C + 1], TOK[:])
                ts(XA[:, 1, :, C + 1], TOK[:], float(TOKENS), None, ALU.add)
                upto(dve, "pexp_ready", base, 0)
                then(v.tensor_reduce(r8[:, 1, :], PB[:], AX.X, ALU.add))
                then(v.reciprocal(r8[:, 2, :], r8[:, 1, :]))
                then(ts(TOK[:], TOK[:], float(NT * P), None, ALU.add))
                then(tt(PB[:], PB[:], bc(r8[:, 2, :]), ALU.mult))
                apart(dve)
                for j in range(NT):
                    last = v.max(M8[:, j, :], PB[:, j, :])
                then(last)
                apart(dve)
                for j in range(NT):
                    last = v.max_index(IX[:, j, :], M8[:, j, :], PB[:, j, :])
                then(last)
                then(tt(r8[:, 3, :], M8[:, :, 0], M8[:, :, 1], ALU.add))
                then(ts(r8[:, 4, :], r8[:, 3, :], 1e-9, None, ALU.add))
                then(v.reciprocal(r8[:, 5, :], r8[:, 4, :]))
                for c_ in range(TOP):
                    last = tt(XA[:, c_, :, C], M8[:, :, c_], r8[:, 5, :], ALU.mult)
                last.then_inc(s("xb_ready"), NT)
                then(v.tensor_copy(IXF[:], IX[:, :, 0:TOP]))
                for c_ in range(TOP):
                    last = tt(OH[:, c_], iota8[:, None, :].broadcast_to([P, NT, E]), bc(IXF[:, :, c_]), ALU.is_equal)
                then(last, True)
                tt(OHS[:], OH[:, 0], OH[:, 1], ALU.add).then_inc(s("onehot_ready"), NT)

            def route_b(base):
                steps = Steps(dve, "route_b_steps", base, -NT, NT, 4)
                then = steps.then
                upto(dve, "places_ps", base, 0)
                v.tensor_copy(PCT[:].rearrange("p m a b -> p (m a b)"), pb[:, 0:P]).then_inc(s("places_read"), NT)
                dve.wait_ge(s("places_read"), base + NT)
                for j in range(NT):
                    then(tt(OFF[:, j + 1, :], OFF[:, j, :], PCT[:, 1, j, :], ALU.add))
                then(tt(SA[:], PCT[:, 0], OFF[:, 0:NT, :], ALU.add))
                then(v.tensor_copy(OFF[:, 0, :], OFF[:, NT, :]))
                then(tt(SA[:], SA[:], ebase[:, None, :].broadcast_to([P, NT, E]), ALU.add))
                for c_ in range(TOP):
                    then(tt(PM[:], OH[:, c_], SA[:], ALU.mult))
                    then(v.tensor_reduce(SLF[:, c_, :], PM[:], AX.X, ALU.add), c_ == TOP - 1)
                v.tensor_copy(SL[:], SLF[:]).then_inc(s("slots_ready"), NT)

            def step(base, i):
                o, k, e = i - 1, i - LAG, i - LAG - 1
                fa, fb = i - 3, i - 4
                front_a, front_b = i % 2 == 1 and there(base, fa), i % 2 == 0 and there(base, fb)
                par, half = (k // 2) % 2, k % 2
                fpar = (fb // 2) % 2
                b3 = lambda t: t[:, par, half, :, None].broadcast_to([P, H, HD])
                v3 = lambda t: t[:, 0:DI].rearrange("p (h d) -> p h d", h=H)

                def conv(first, tap):
                    fo = (first % NT) * P
                    for m in range(3):
                        last = stt(CV[:, m, :], XBC[:, m, fo + tap:fo + tap + 256], cw[:, m, tap:tap + 1], CV[:, m, :], ALU.mult, ALU.add)
                    return last

                if there(base, o):
                    upto(dve, "pT_ps", base, o + 1)
                    upto(dve, "o_ps", base, o)
                    v.tensor_copy(PT[:, 512:], pY[:, 512:]).then_inc(s("pt_dve"), 1)
                if front_b:
                    conv(fb, 0).then_inc(s("conv_ready"), 2)
                    for j in range(2):
                        bank = (pc, pd)[j]
                        upto(dve, "tz_ready", base, fb + j + 1)
                        stt(SZ[:, fpar, j, :], TZ[:, j, :], 1.0, bank[:, 0:DI], ALU.add, ALU.mult).then_inc(s("sz_ready"), 1)
                        tt(dts[:, 0, j, :], bank[:, DI:DI + H], hrow[:, 0, :], ALU.add).then_inc(s("u_ready"), 1)
                    upto(dve, "u_ready", base, fb + 2)
                    stt(dts[:, 1], dts[:, 0], -1.0, dts[:, 0], ALU.mult, ALU.min).then_inc(s("nau_ready"), 2)
                    ts(dts[:, 3], dts[:, 0], 0.0, None, ALU.max)
                if there(base, i):
                    upto(dve, "s_ready", base, i + 1)
                    v.tensor_reduce(NM[:, i:i + 1], pX[:], AX.X, ALU.max, negate=True).then_inc(s("nm_ready"), 1)
                if there(base, k):
                    upto(dve, "xs_ready", base, k + 1)
                    upto(dve, "xw_ready", base, k)
                    upto(dve, "ydiag_ps", base, k)
                    tt(v3(XDT), v3(pa), b3(DT), ALU.mult).then_inc(s("xdt_ready"), 1)
                    upto(dve, "yd_ready", base, k)
                    tt(v3(DX), v3(pa), hrow[:, 2, :, None].broadcast_to([P, H, HD]), ALU.mult).then_inc(s("dx_ready"), 1)
                if there(base, e):
                    upto(dve, "out_ps", base, e + 1)
                    upto(dve, "ry_ready", base, e + 1)
                    upto(dve, "tr_ready", base, e + 1)
                    t2 = T2[:, bass.ds(base + e, 1), :].rearrange("p a c -> p (a c)")
                    stt(t2, pb[:, 0:C], RY[:, 1, 0:1], TR[:, e % NT, :], ALU.mult, ALU.add).then_inc(s("t2_ready"), 1)
                    upto(dve, "t2_ready", base, e + 1)
                    apart(dve)
                    v.bn_stats(BN2[:, e % NT, :], t2).then_inc(s("bn2_ready"), 1)
                if front_b:
                    steps = Steps(dve, "softplus_steps", base, fb, 2, 8)
                    def chain(n, ins):
                        steps.then(ins, n == 8)
                    upto(dve, "enau_ready", base, fb + 2)
                    chain(0, ts(dts[:, 4], dts[:, 2], 2.0, None, ALU.add))
                    chain(9, v.reciprocal(dts[:, 9], dts[:, 4]))
                    chain(1, tt(dts[:, 5], dts[:, 2], dts[:, 9], ALU.mult))
                    chain(2, tt(dts[:, 6], dts[:, 5], dts[:, 5], ALU.mult))
                    chain(3, ts(dts[:, 7], dts[:, 6], ATANH[4], None, ALU.mult))
                    chain(4, stt(dts[:, 8], dts[:, 7], ATANH[3], dts[:, 6], ALU.add, ALU.mult))
                    chain(5, stt(dts[:, 7], dts[:, 8], ATANH[2], dts[:, 6], ALU.add, ALU.mult))
                    chain(6, stt(dts[:, 8], dts[:, 7], ATANH[1], dts[:, 6], ALU.add, ALU.mult))
                    chain(7, stt(dts[:, 7], dts[:, 8], ATANH[0], dts[:, 5], ALU.add, ALU.mult))
                    chain(8, stt(DT[:, fpar], dts[:, 7], 2.0, dts[:, 3], ALU.mult, ALU.add))
                    upto(dve, "cum_ps", base, fb)
                    stt(AD[:, 0:16].rearrange("p (a b) -> p a b", a=2), DT[:, fpar], -1.0, hrow[:, 1:2, :].broadcast_to([P, 2, H]), ALU.mult, ALU.mult).then_inc(s("ad_ready"), 2)
                if there(base, k):
                    upto(dve, "expD_ready", base, k + 1)
                    upto(dve, "gT_ready", base, k + 1)
                    upto(dve, "ydiag_ps", base, k)
                    tt(M[:], ED[:], GT[:, None, :].broadcast_to([P, H, P]), ALU.mult).then_inc(s("m_ready"), 1)
                if there(base, e):
                    if e % NT == 0:
                        upto(dve, "rstd2_ready", base, e)
                    upto(dve, "bn2_ready", base, e + 1)
                    apart(dve)
                    v.bn_aggr(MV2[:, e % NT, :], BN2[:, e % NT, :]).then_inc(s("mv2_ready"), 1)
                if there(base, o):
                    v.reciprocal(RG[:, o % NT:o % NT + 1], RS[:, o % NT:o % NT + 1]).then_inc(s("rcp_ready"), 1)
                if there(base, k):
                    upto(dve, "state_ps", base, k + 1)
                    upto(dve, "yd_ready", base, k)
                    if k % NT != 0:
                        tt(v3(YO), v3(pd), b3(ECUM), ALU.mult).then_inc(s("yo_ready"), 1)
                        upto(dve, "ste_ready", base, k + 1)
                        tt(ST[0:NS, :], STE[0:NS, :], pd[0:NS, DI:2 * DI], ALU.add).then_inc(s("st_ready"), 1)
                    else:
                        v.tensor_copy(ST[0:NS, :], pd[0:NS, DI:2 * DI]).then_inc(s("st_ready"), 1)
                        v.nop().then_inc(s("yo_ready"), 1)
                if front_b:
                    upto(dve, "cum_ps", base, fb + 2)
                    p3 = lambda a: CT[:, a:a + 16].rearrange("p (a b) -> p a b", a=2)
                    CUM = p3(0)
                    upto(dve, "ecum_ready", base, fb)
                    v.tensor_copy(CT[:], pb[:, 0:P]).then_inc(s("cum1"), 2)
                if there(base, o):
                    upto(dve, "rcp_ready", base, o + 1)
                    ts(RG[:, o % NT:o % NT + 1], RG[:, o % NT:o % NT + 1], pcol[:, 4:5], None, ALU.mult).then_inc(s("rg_ready"), 1)
                if front_b:
                    upto(dve, "cum1", base, fb + 2)
                    upto(dve, "dec_exp", base, fb)
                    tt(R1b[:], p3(64), CUM, ALU.subtract).then_inc(s("dec_in"), 2)
                    upto(dve, "ct3_ps", base, fb)
                    v.tensor_copy(C3[:, 0], CUM).then_inc(s("cum2"), 2)
                if there(base, o):
                    upto(dve, "rg_ready", base, o + 1)
                    upto(dve, "o_ps", base, o + 1)
                    if o % 4 == 0:
                        if isinstance(base, int):
                            dve.wait_ge(s(f"x{o // 4}_loaded"), 16 * (base // NT + 1))
                        else:
                            dve.wait_ge(s(f"x{o // 4}_loaded"), base * 2 + 16)
                    stt(TA[:, o % NT, :], pa[:, 0:C], RG[:, o % NT:o % NT + 1], X[:, o % NT, :], ALU.mult, ALU.add).then_inc(s("t_ready"), 1)
                if front_b:
                    upto(dve, "cum2", base, fb + 2)
                    tt(R1[:], CUM, C3[:, 0], ALU.subtract).then_inc(s("cum3"), 2)
                if there(base, o):
                    upto(dve, "t_ready", base, o + 1)
                    v.bn_stats(BN[:, o % NT, :], TA[:, o % NT, :]).then_inc(s("bn_ready"), 1)
                if front_b:
                    upto(dve, "cum3", base, fb + 2)
                    v.tensor_copy(C3[:, 1], R1[:]).then_inc(s("cum4"), 2)
                if there(base, o):
                    upto(dve, "bn_ready", base, o + 1)
                    apart(dve)
                    v.bn_aggr(MV[:, o % NT, :], BN[:, o % NT, :]).then_inc(s("mv_ready"), 1)
                if front_b:
                    upto(dve, "cum4", base, fb + 2)
                    tt(C3[:, 2], R1[:], C3[:, 1], ALU.subtract).then_inc(s("c3_ready"), 2)
                if there(base, k):
                    upto(dve, "ydiag_ps", base, k + 1)
                    upto(dve, "yd_ready", base, k + 1)
                    tt(v3(Y2), pc[:].rearrange("p (h w) -> p h w", h=H)[:, :, 0:HD], v3(YD), ALU.add).then_inc(s("y2_ready"), 1)
                if front_b:
                    upto(dve, "th_ready", base, fb + 2)
                    stt(SX[:, fpar].rearrange("p a b -> p (a b)"), TH[:].rearrange("p a b -> p (a b)"), 1.0, CV[:].rearrange("p a b -> p (a b)"), ALU.add, ALU.mult).then_inc(s("sx_ready"), 2)
                if there(base, k):
                    upto(dve, "y2_ready", base, k + 1)
                    upto(dve, "ss_ready", base, k)
                    upto(dve, "yT_ps", base, k)
                    tt(YG[:], Y2[:], SZ[:, par, half, :], ALU.mult).then_inc(s("yg_ready"), 1)
                if front_a:
                    upto(dve, "cv_evac", base, fa + 2)
                    conv(fa, 2).then_inc(s("conv_tap2"), 2)
                    upto(dve, "conv_tap2", base, fa + 2)
                    conv(fa, 1).then_inc(s("conv_tap1"), 2)
                    upto(dve, "conv_tap1", base, fa + 2)
                if i == 0 and there(base, 0):
                    upto(dve, "projected", base, NT)
                    take_v()
                if i == 6 and there(base, -NT):
                    for grp in range(2):
                        upto(dve, "logits_ps", base, 4 * grp - 4)
                        v.tensor_copy(LG[:, 4 * grp:4 * grp + 4, :], pb[:, 0:256].rearrange("p (j w) -> p j w", j=4)[:, :, 0:E]).then_inc(s("lg_ready"), 4)
                    upto(dve, "lg_ready", base, 0)
                    v.tensor_reduce(r8[:, 0, :], LG[:], AX.X, ALU.max).then_inc(s("lmax_ready"), NT)
                    upto(dve, "lmax_ready", base, 0)
                    tt(LG[:], LG[:], r8[:, 0, :, None].broadcast_to([P, NT, E]), ALU.subtract).then_inc(s("lsub_ready"), NT)
                if i == 7 and there(base, -NT):
                    route_a(base)
                    route_b(base)
                if i == NT - 1 and there(base, NT):
                    upto(dve, "qh_ready", base, 2 * NT)
                    take_qv(base)

            dve.wait_ge(s("loaded"), 16 * NLOAD)
            dve.wait_ge(s("consts"), 1)
            dve.wait_ge(s("a_exp"), 1)
            ts(pw1s[:], pw1s[:], pcol[:, 0:1], None, ALU.mult)
            ts(pw2s[:], pw2s[:], pcol[:, 1:2], None, ALU.mult)
            ts(wz[:, 0:DI], wz[:, 0:DI], pcol[:, 3:4], 0.5, ALU.mult, ALU.mult)
            ts(wz[:, DI:], wz[:, DI:], pcol[:, 3:4], None, ALU.mult)
            ts(wx[:], wx[:], pcol[:, 3:4], None, ALU.mult)
            ts(cw[:], cw[:], 0.5, None, ALU.mult)
            ts(cb[:], cb[:], 0.5, None, ALU.mult)
            for m in range(2):
                last = ts(wo[:, m, :], wo[:, m, :], gw[:, m:m + 1], None, ALU.mult)
            last.then_inc(s("setup"), 1)
            dve.wait_ge(s("qh_ready"), NT)
            take_qv(0)
            batches(dve, step)

            steps = Steps(dve, "table_steps", 0, 0, 1, 64)
            then = steps.then
            runs = OFF[:, 0, :]
            dve.wait_ge(s("iotas"), 2)
            dve.wait_ge(s("route_b_steps"), 4 * TILES)
            dve.wait_ge(s("slots_ready"), TILES)
            then(tt(NTE[:], runs, ebase[:], ALU.add))
            then(ts(NTE[:], NTE[:], pidx[:, 0:1], 1.0, ALU.add, ALU.add))
            v.tensor_copy(ZI[:], NTE[:]).then_inc(s("zi_ready"), 1)
            dve.wait_ge(s("zi_ready"), 1)
            then(ts(NTE[:], runs, 1.0 / P, (P - 1) / P - 63.5 / P, ALU.mult, ALU.add))
            then(v.tensor_copy(NTI[:], NTE[:]))
            then(v.tensor_copy(NTE[:], NTI[:]))
            then(v.tensor_copy(CTE[:, 0:1], NTE[:, 0:1]))
            for x_ in range(1, E):
                then(tt(CTE[:, x_:x_ + 1], CTE[:, x_ - 1:x_], NTE[:, x_:x_ + 1], ALU.add))
            by = lambda a: a[:, None, :].broadcast_to([P, SLOTS, E])
            then(tt(GE[:], itile[:, :, None].broadcast_to([P, SLOTS, E]), by(CTE), ALU.is_ge))
            then(v.tensor_reduce(TB[:, 0, :], GE[:], AX.X, ALU.add))
            then(tt(GE[:], GE[:], by(NTE), ALU.mult))
            then(v.tensor_reduce(TB[:, 1, :], GE[:], AX.X, ALU.add))
            then(tt(TB[:, 1, :], itile[:], TB[:, 1, :], ALU.subtract))
            then(ts(TB[:, 1, :], TB[:, 1, :], float(P), None, ALU.mult))
            then(stt(TB[:, 2, :], TB[:, 0, :], float(REGION), TB[:, 1, :], ALU.mult, ALU.add))
            then(ts(TB[:, 0, :], TB[:, 0, :], float(E - 1), None, ALU.min))
            v.tensor_copy(TBI[:, 0, :], TB[:, 2, :])
            v.tensor_copy(TBI[:, 1, :], TB[:, 0, :]).then_inc(s("table_ready"), 1)

            def gated(n, par):
                dve.wait_ge(s("silu_ready"), n)
                dve.wait_ge(s("h3_ps"), n)
                tt(HH[:, par, :], SH[:, par, :], pY[:, 512 * par:512 * par + HID], ALU.mult).then_inc(s("hh_ready"), 1)

            def turned(n, par):
                dve.wait_ge(s("hT_ps"), n)
                v.tensor_copy(HT[:, par].rearrange("p k t -> p (k t)"), pc[:, 0:P * len(HC)]).then_inc(s("hT_ready"), 1)

            def take_gates(t, j):
                j, t = j % GROUP, t + j // GROUP * GROUP
                dve.wait_ge(s(f"gx{j}_loaded"), t * 4 + 16)
                if not (isinstance(t, int) and t == 0):
                    dve.wait_ge(s(f"ye{j}_scattered"), t * 4)
                v.tensor_copy(DIX[:, j, :], GX[:, j, C + 1:C + 2])
                v.tensor_copy(GATE[:, j, :], GX[:, j, C:C + 1]).then_inc(s("dix_ready"), 1)

            def group(t):
                for j in range(GROUP):
                    gated(t + j + 1, j % 2)
                    turned(t + j + 1, j % 2)
                    if not (isinstance(t, int) and t + j == SLOTS - 1):
                        take_gates(t, j + 1)
            take_gates(0, 0)
            with dve.Fori(0, SLOTS - 2 * GROUP + 1, GROUP) as t:
                group(t)
            group(SLOTS - GROUP)
            for b in range(TILES // NT):
                dve.wait_ge(s(f"y{b % 2}_loaded"), 16 * TOP * (b // 2 + 1))
                tiles = T2[:, b * NT:b * NT + NT, :]
                tt(Y01[b % 2][0], Y01[b % 2][0], Y01[b % 2][1], ALU.add).then_inc(s("y_added"), 1)
                dve.wait_ge(s("y_added"), b + 1)
                tt(tiles, tiles, Y01[b % 2][0], ALU.add).then_inc(s("added"), 1)


def kernel(**inputs):
    import numpy as _np
    import concourse.bacc as _bacc
    from concourse import mybir as _mybir
    from concourse.bass_utils import run_bass_kernel_spmd as _run

    a = {name: _np.asarray(v) for name, v in inputs.items()}
    x = a["x"]
    batch, height, width, chans = x.shape
    tokens = x.reshape(batch, height * width, chans)
    ssm = {name: a["L1_attn_" + name] for name in
           ("W_in", "conv_w", "conv_b", "dt_bias", "A_log", "Dp", "gnorm_w", "norm_w", "W_out")}
    inner, conv_dim = ssm["gnorm_w"].shape[0], ssm["conv_b"].shape[0]
    w_in = ssm["W_in"]
    laid_out = {
        "x": tokens.reshape(-1, chans),
        "xT": tokens.transpose(0, 2, 1).reshape(batch * chans, height * width),
        **{name: a["L0_conv_" + name] for name in ("dw1", "pw1", "b1", "dw2", "pw2", "b2", "gamma")},
        "w_zdt": _np.concatenate([w_in[:inner], w_in[inner + conv_dim:]], 0).T,
        "w_xbc": w_in[inner:inner + conv_dim].T,
        "conv_w": ssm["conv_w"], "conv_b": ssm["conv_b"], "dt_bias": ssm["dt_bias"], "a_log": ssm["A_log"],
        "d_skip": ssm["Dp"], "gnorm_w": ssm["gnorm_w"], "norm_w": ssm["norm_w"],
        "w_outT": ssm["W_out"].T,
        "routerT": a["L1_ffn_router_w"].T,
        "w1T": a["L1_ffn_w1"].transpose(0, 2, 1),
        "w3T": a["L1_ffn_w3"].transpose(0, 2, 1),
        "w2T": a["L1_ffn_w2"].transpose(0, 2, 1),
    }
    nc = _bacc.Bacc("TRN2", target_bir_lowering=False, num_devices=1)
    arrays, args = {}, []
    for name, v in laid_out.items():
        v = _np.ascontiguousarray(v)
        arrays[f"in_{name}_dram"] = v
        args.append(nc.dram_tensor(f"in_{name}_dram", v.shape, _mybir.dt.from_np(v.dtype), kind="ExternalInput").ap())
    out = nc.dram_tensor("out_dram", (batch * height * width, chans), _mybir.dt.from_np(x.dtype), kind="ExternalOutput").ap()
    conv_attn_ssm_moe(nc, *args, out)
    r = _run(nc, [arrays], core_ids=[0])
    return r.results[0]["out_dram"].reshape(x.shape)
```

```python
import concourse.bass as bass
from concourse import mybir
from contextlib import ExitStack


def conv_attn_ssm_moe(nc, x, xT, dw1, pw1, b1, dw2, pw2, b2, gamma, w_zdt, w_xbc, conv_w, conv_b,
                      dt_bias, a_log, d_skip, gnorm_w, norm_w, w_outT, routerT, w1T, w3T, w2T, out):
    fp32, bf16, f32r = mybir.dt.float32, mybir.dt.bfloat16, mybir.dt.float32r
    ALU, ACT, AX = mybir.AluOpType, mybir.ActivationFunctionType, mybir.AxisListType
    P = 128
    TILES = x.shape[0] // P
    NT = 8
    SEQ = NT * P
    C = x.shape[1]
    H, HD, NS = 8, 32, 32
    DI = H * HD
    TAPS = 4
    LAG = 5
    ATANH = [1.0, 0.33333157962211934, 0.20012429465084794, 0.1398064909942622, 0.14087686162896493]
    E, TOP = 8, 2
    HID = w1T.shape[2]
    HC = [(P * k, min(P, HID - P * k)) for k in range(-(-HID // P))]
    TOKENS = TILES * P
    REGION = TOKENS + P
    SLOTS = TOP * TILES + E
    ROW = C + 2
    GROUP = 4
    DIGITS = GROUP + 2
    PAD = TOP * TOKENS
    LN_EPS, RMS_EPS, FLT_EPS = 1e-5, 1e-5, 1.1920928955078125e-07

    ctx = ExitStack()
    with ctx:
        def sb(name, shape, dt=fp32):
            return ctx.enter_context(nc.sbuf_tensor(name, shape, dt))

        def ps(name, shape, dt=fp32):
            return ctx.enter_context(nc.psum_tensor(name, shape, dt))

        def sem(name):
            return ctx.enter_context(nc.semaphore(name))

        ident = sb("ident", [P, P])
        identb = sb("identb", [P, P], bf16)
        tri = sb("tri", [P, P])
        ones = sb("ones", [P, P])
        later = sb("later", [P, P], bf16)
        pick = sb("pick", [P, 16, P], bf16)
        mhalf = sb("mhalf", [P, 2])
        pw1s, pw2s = sb("pw1s", [P, C]), sb("pw2s", [P, C])
        pcol = sb("pcol", [P, 8])
        b2b = sb("b2b", [P, C])
        wz, wx = sb("wz", [P, DI + H]), sb("wx", [P, 3 * P])
        cw, cb = sb("cw", [P, 3, TAPS]), sb("cb", [P, 3])
        hrow = sb("hrow", [P, 3, H])
        gw = sb("gw", [P, 2])
        wo = sb("wo", [P, 2, C])
        diagD = sb("diagD", [P, 2, P])
        XT, X = sb("XT", [P, SEQ]), sb("X", [P, NT, C])
        QH, QL = sb("QH", [P, SEQ], f32r), sb("QL", [P, SEQ], f32r)
        V = sb("V", [P, NT, C])
        PR, PT = sb("PR", [P, SEQ]), sb("PT", [P, SEQ])
        NM, RS, RG = sb("NM", [P, NT]), sb("RS", [P, NT]), sb("RG", [P, NT])
        TA = sb("TA", [P, NT, C])
        BN = sb("BN", [P, NT, 6])
        MV = sb("MV", [P, NT, 2])
        st = sb("st", [P, 7, 4])
        XN = sb("XN", [P, 2, C])
        TR = sb("TR", [P, NT, C])
        XNT = sb("XNT", [P, 2 * P])
        XBC = sb("XBC", [P, 3, TAPS - 1 + SEQ])
        CV, TH = sb("CV", [P, 3, 2 * P]), sb("TH", [P, 3, 2 * P])
        SX = sb("SX", [P, 2, 3, 2 * P])
        CTP = sb("CTP", [P, 2, 2 * P])
        TZ = sb("TZ", [P, 2, DI])
        SZ = sb("SZ", [P, 2, 2, DI])
        dts = sb("dts", [P, 10, 2, H])
        DT = sb("DT", [P, 2, 2, H])
        AD = sb("AD", [P, 64])
        CT = sb("CT", [P, P])
        ECUM, ETOT, DEC = (sb(n, [P, 2, 2, H]) for n in ("ECUM", "ETOT", "DEC"))
        R1 = sb("R1", [P, 2, H])
        C3 = sb("C3", [P, 3, 2, H], bf16)
        R1b = sb("R1b", [P, 2, H])
        CT3, NCT3 = sb("CT3", [P, 2, P], bf16), sb("NCT3", [P, 2, P], bf16)
        XDT = sb("XDT", [P, 2, DI + HD])
        XW, YO, Y2 = (sb(n, [P, DI]) for n in ("XW", "YO", "Y2"))
        YG = sb("YG", [P, DI])
        BNAT, GT = sb("BNAT", [P, P]), sb("GT", [P, P])
        ED, M = sb("ED", [P, H, P]), sb("M", [P, H, P])
        ST, STE = sb("ST", [P, DI]), sb("STE", [P, DI])
        SQ, SS = sb("SQ", [P, DI]), sb("SS", [P, 1])
        RY = sb("RY", [P, 2, 2])
        YT = sb("YT", [P, 2, P])
        T2 = sb("T2", [P, TILES, C])
        BN2, MV2 = sb("BN2", [P, NT, 6]), sb("MV2", [P, NT, 2])
        rs2 = sb("rs2", [P, 3, NT])
        XA = sb("XA", [P, TOP, NT, ROW])
        VT = sb("VT", [P, 4 * P])
        rT = sb("rT", [P, 64])
        LG, PB, OHS, SA, PM = (sb(n, [P, NT, E]) for n in ("LG", "PB", "OHS", "SA", "PM"))
        OH = sb("OH", [P, TOP, NT, E])
        M8 = sb("M8", [P, NT, 8])
        IX = sb("IX", [P, NT, 8], mybir.dt.uint32)
        IXF = sb("IXF", [P, NT, TOP])
        r8 = sb("r8", [P, 6, NT])
        PCT = sb("PCT", [P, 2, NT, E])
        OFF = sb("OFF", [P, NT + 1, E])
        iota8, ebase = sb("iota8", [P, E]), sb("ebase", [P, E])
        TOK = sb("TOK", [P, NT])
        SLF = sb("SLF", [P, TOP, NT])
        SL = sb("SL", [P, TOP, NT], mybir.dt.uint32)
        ZT = sb("ZT", [P, 2 * E, ROW])
        ZI = sb("ZI", [P, E], mybir.dt.uint32)
        pidx = sb("pidx", [P, 1])
        NTE, CTE = sb("NTE", [P, E]), sb("CTE", [P, E])
        NTI = sb("NTI", [P, E], mybir.dt.int32)
        itile = sb("itile", [P, SLOTS])
        GE = SX[:].rearrange("p a m t -> p (a m t)")[:, 0:SLOTS * E].rearrange("p (t e) -> p t e", e=E)
        TB = sb("TB", [P, 3, SLOTS])
        EXPERT = sb("EXPERT", [P, SLOTS + DIGITS])
        DIGS = sb("DIGS", [P, SLOTS + 1])
        TBI = sb("TBI", [P, 2, SLOTS + 1], mybir.dt.int32)
        W1, W3 = sb("W1", [P, E * HID]), sb("W3", [P, E * HID])
        W2 = sb("W2", [P, E, len(HC), C])
        GX = sb("GX", [P, GROUP, ROW])
        GXT = TA[:, 0:2, :]
        SH = XT[:, 0:2 * HID].rearrange("p (a h) -> p a h", a=2)
        HH = X[:].rearrange("p t c -> p (t c)")[:, 0:2 * HID].rearrange("p (a h) -> p a h", a=2)
        HT = V[:].rearrange("p t c -> p (t c)")[:, 0:2 * len(HC) * P].rearrange("p (a k t) -> p a k t", a=2, t=P)
        YE = sb("YE", [P, GROUP, C])
        DIX = sb("DIX", [P, GROUP, 1], mybir.dt.uint32)
        GATE = sb("GATE", [P, GROUP, 1])
        xg = nc.dram_tensor("rows_by_expert", [E * REGION + E * P, ROW], fp32, kind="Internal").ap()
        yg = nc.dram_tensor("results_by_choice", [PAD + 2 * E * P, C], fp32, kind="Internal").ap()

        pX, pY = ps("pX", [P, 2 * 512]), ps("pY", [P, 2 * 512])
        pa, pb, pc, pd = (ps(n, [P, 512]) for n in ("pa", "pb", "pc", "pd"))

        S = {}
        wide = lambda a, k: a[:, k * SEQ:(k + 1) * SEQ]
        heads = lambda a: a[:].rearrange("p h t -> p (h t)")
        Y01 = [[PR[:], PT[:]], [heads(ED), heads(M)], [wide(W1, 0), wide(W1, 1)], [wide(W3, 0), wide(W3, 1)]]
        Y01 = [[a.rearrange("p (t c) -> p t c", c=C) for a in two] for two in Y01]

        def s(name):
            if name not in S:
                S[name] = sem(name)
            return S[name]

        def upto(eng, name, base, c):
            if not isinstance(base, int):
                eng.wait_ge(s(name), base + c)
            elif base + c > 0:
                eng.wait_ge(s(name), min(base + c, TILES))

        def apart(eng):
            eng.sem_inc(s("apart"), 1)

        class Steps:
            def __init__(self, eng, name, base, c, tiles, per_tile):
                self.eng, self.sem, self.n = eng, s(name), 0
                self.start, self.total = base * per_tile + c * per_tile, tiles * per_tile

            def then(self, ins, last=False):
                self.n += 1
                assert self.n < self.total
                if last:
                    ins.then_inc(self.sem, self.total - self.n + 1)
                    self.n = self.total
                else:
                    ins.then_inc(self.sem, 1)
                self.eng.wait_ge(self.sem, self.start + self.n)

        def there(base, c):
            return not isinstance(base, int) or 0 <= base + c < TILES

        block = ctx.enter_context(nc.Block())

        def batches(eng, step):
            for i in range(2 * NT):
                step(i // NT * NT, i % NT)
            with eng.Fori(2 * NT, TILES - 2 * NT + 1, NT) as base:
                for i in range(NT):
                    step(base, i)
            for i in range(3 * NT - 1):
                step(TILES - NT + i // NT * NT, i % NT)

        NLOAD = 2 + 3 + 2 + 3 + 3 + 2 + 1 + 1

        @block.sync
        def _(sp):
            def load(dst, src):
                sp.dma_start(dst, src).then_inc(s("loaded"), 16)
            row = lambda v, n: v.rearrange("(a n) -> a n", a=1).broadcast_to([P, n])
            sp.dma_start(XT[:], xT[0:P, :]).then_inc(s("xT_loaded"), 16)
            xtok = x.rearrange("(t p) c -> p t c", p=P)
            for h in range(2):
                half = slice(h * NT // 2, (h + 1) * NT // 2)
                sp.dma_start(X[:, half, :], xtok[:, half, :]).then_inc(s(f"x{h}_loaded"), 16)
            col = lambda v: v.rearrange("(p a) -> p a", a=1)
            load(pcol[:, 3:4], col(norm_w))
            load(pcol[:, 4:5], row(gamma, 1))
            load(b2b[:], row(b2, C))
            load(wz[:], w_zdt)
            load(wx[:, 0:DI + 2 * NS], w_xbc)
            sp.wait_ge(s("zeroed"), 1)
            load(cw[:, 0:2, :], conv_w[0:2 * P, :].rearrange("(m p) k -> p m k", p=P))
            load(cw[0:2 * NS, 2, :], conv_w[2 * P:, :])
            for m in range(3):
                part = conv_b[m * P:min((m + 1) * P, DI + 2 * NS)]
                load(cb[0:part.shape[0], m:m + 1], col(part))
            for k, v in enumerate((dt_bias, a_log, d_skip)):
                load(hrow[:, k, :], row(v, H))
            for m in range(2):
                load(gw[:, m:m + 1], col(gnorm_w[m * P:m * P + P]))
            load(wo[:], w_outT.rearrange("(k p) c -> p k c", p=P))
            load(rT[:, 0:E], routerT)
            def load_expert(dst, src):
                sp.dma_start(dst, src).then_inc(s("experts_loaded"), 16)
            load_expert(W1[:].rearrange("p (e h) -> p e h", e=E), w1T.rearrange("e c h -> c e h"))
            load_expert(W3[:].rearrange("p (e h) -> p e h", e=E), w3T.rearrange("e c h -> c e h"))
            for k, (h0, hn) in enumerate(HC):
                load_expert(W2[0:hn, :, k, :], w2T[:, h0:h0 + hn, :].rearrange("e h c -> h e c"))

            def step(base):
                upto(sp, "t_ready", base, NT // 2)
                sp.dma_start(X[:, 0:NT // 2, :], xtok[:, bass.ds(base + NT, NT // 2), :]).then_inc(s("x0_loaded"), 16)
                upto(sp, "projected", base, NT)
                sp.dma_start(XT[:], xT[bass.ds(base * 16 + P, P), :]).then_inc(s("xT_loaded"), 16)
                upto(sp, "t_ready", base, NT)
                sp.dma_start(X[:, NT // 2:, :], xtok[:, bass.ds(base + NT + NT // 2, NT // 2), :]).then_inc(s("x1_loaded"), 16)
            step(0)
            with sp.Fori(NT, TILES - 2 * NT + 1, NT) as base:
                step(base)
            sp.wait_ge(s("zt_ready"), 2)
            sp.dma_start(xg[E * REGION:, :].rearrange("(t p) c -> p t c", p=P), ZT[:, E:, :]).then_inc(s("filled_up"), 16)
            sp.wait_ge(s("zi_ready"), 1)
            for x_ in range(E):
                row = sp.value_load(ZI[0:1, x_:x_ + 1], min_val=x_ * REGION, max_val=x_ * REGION + TOKENS)
                sp.dma_start(xg[bass.ds(row, P), :], ZT[:, x_, :]).then_inc(s("filled_up"), 16)
            sp.wait_ge(s("table_ready"), 1)
            sp.wait_ge(s("scattered"), 16 * TOP * TILES)
            sp.wait_ge(s("filled_up"), 16 * (E + 1))

            def fetch(t, j):
                row = sp.value_load(TBI[0:1, 0, bass.ds(t + j, 1)], min_val=0, max_val=E * REGION + (E - 1) * P)
                if not (isinstance(t, int) and t == 0):
                    sp.wait_ge(s("gxt_ps"), t + j + 1 - GROUP)
                    sp.wait_ge(s("dix_ready"), t + j + 1 - GROUP)
                sp.dma_start(GX[:, j, :], xg[bass.ds(row, P), :]).then_inc(s(f"gx{j}_loaded"), 16)
            for j in range(GROUP):
                fetch(0, j)
            with sp.Fori(GROUP, SLOTS - GROUP + 1, GROUP) as t:
                for j in range(GROUP):
                    fetch(t, j)
            for j in range(GROUP):
                sp.wait_ge(s(f"ye{j}_scattered"), 16 // GROUP * SLOTS)
            def y_load(b):
                for c_ in range(TOP):
                    src = yg[bass.ds(b * NT * P + c_ * TOKENS, NT * P), :].rearrange("(t p) c -> p t c", p=P)
                    sp.dma_start(Y01[b % len(Y01)][c_], src).then_inc(s(f"y{b % len(Y01)}_loaded"), 16)
            for b in range(TILES // NT):
                if b >= len(Y01):
                    sp.wait_ge(s("added"), b + 1 - len(Y01))
                y_load(b)

        @block.tensor
        def _(pe):
            mm = nc.tensor.matmul

            def project_q():
                for h in range(2):
                    last = mm(pX[:, 512 * h:512 * h + 512], pw1s[:], XT[:, 512 * h:512 * h + 512], start=True, stop=True)
                last.then_inc(s("qps"), NT)

            def project_v():
                for j in range(NT):
                    last = mm(pX[:, P * j:P * j + P], XT[:, P * j:P * j + P], pw2s[:], start=True, stop=True)
                last.then_inc(s("projected"), NT)

            def rows_of_x(base, grp):
                upto(pe, "xa_ready", base, 4 * grp - 4)
                upto(pe, "st_ready", base, 2)
                upto(pe, "yo_ready", base, 2)
                if grp:
                    upto(pe, "lg_ready", base, -4)
                for j in range(4):
                    last = nc.tensor.transpose(pd[:, P * j:P * j + P], XA[:, 0, 4 * grp + j, 0:C], ident[:])
                last.then_inc(s("vT_ps"), 4)

            def logits(base, grp):
                upto(pe, "vT_ready", base, 4 * grp - 4)
                for j in range(4):
                    last = mm(pd[:, 64 * j:64 * j + 64], VT[:, P * j:P * j + P], rT[:], start=True, stop=True, skip_group_check=True)
                last.then_inc(s("logits_ps"), 4)

            def step(base, i):
                o, k, e = i - 1, i - LAG, i - LAG - 1
                fa, fb = i - 3, i - 4
                front_a, front_b = i % 2 == 1 and there(base, fa), i % 2 == 0 and there(base, fb)
                decays = i % 2 == 1 and there(base, k)
                par, half = (k // 2) % 2, k % 2
                tk = slice(P * half, P * half + P)
                if there(base, o):
                    upto(pe, "exp_ready", base, o + 1)
                    upto(pe, "expD_ready", base, k)
                    if front_b:
                        upto(pe, "xbc2_evac", base, fb + 2)
                    for j in range(NT):
                        last = nc.tensor.transpose(pY[:, P * j:P * j + P], PR[:, P * j:P * j + P], ident[:])
                    last.then_inc(s("pT_ps"), 1)
                if there(base, i):
                    upto(pe, "q_ready", base, NT)
                    upto(pe, "exp_ready", base, i)
                    if i == 1:
                        upto(pe, "v_copied", base, NT)
                    for h in range(2):
                        q = slice(512 * h, 512 * h + 512)
                        ti = slice(P * i, P * i + P)
                        mm(pX[:, q], QH[:, ti], QH[:, q], start=True, stop=False)
                        mm(pX[:, q], QH[:, ti], QL[:, q], start=False, stop=False)
                        last = mm(pX[:, q], QL[:, ti], QH[:, q], start=False, stop=True)
                    last.then_inc(s("s_ready"), 1)
                if front_b:
                    upto(pe, "xnT_ready", base, fb + 2)
                    upto(pe, "t2_ready", base, e)
                    mm(pb[:, 0:DI + H], XNT[:, 0:P], wz[:], start=True, stop=True).then_inc(s("z_ps"), 1)
                    upto(pe, "st_ready", base, k)
                    upto(pe, "yo_ready", base, k)
                    mm(pd[:, 0:DI + H], XNT[:, P:2 * P], wz[:], start=True, stop=True).then_inc(s("z_ps"), 1)
                if there(base, e):
                    upto(pe, "m_ready", base, e + 1)
                    upto(pe, "xdt_ready", base, e + 1)
                    if front_b:
                        upto(pe, "xbc01_evac", base, fb + 2)
                    if decays:
                        upto(pe, "cum1", base, k + 2)
                    if i == 3:
                        upto(pe, "places_read", base, -NT)
                    for h in range(H):
                        mm(pc[:, 64 * h:64 * h + 64], M[:, h, :], XDT[:, e % 2, HD * h:HD * h + 64], start=h == 0, stop=False, skip_group_check=True)
                    y_heads = pc[:].rearrange("p (h w) -> p h w", h=H)
                    for m in range(2):
                        last = mm(y_heads[:, 4 * m:4 * m + 4, 0:HD], SX[:, (e // 2) % 2, m, P * (e % 2):P * (e % 2) + P], diagD[:, m, :], start=False, stop=True, skip_group_check=True)
                    last.then_inc(s("ydiag_ps"), 1)
                if decays:
                    upto(pe, "c3_ready", base, k + 2)
                    upto(pe, "t2_ready", base, e)
                    nc.tensor.transpose(pb[:, :].bitcast(bf16)[0:48, 0:P], C3[:].rearrange("p a b c -> p (a b c)"), identb[:]).then_inc(s("ct3_ps"), 2)
                if there(base, k):
                    upto(pe, "bc_ready", base, k + 1)
                    upto(pe, "t_ready", base, o)
                    for m in range(3):
                        last = nc.tensor.transpose(pa[:, P * m:P * m + P], SX[:, par, m, tk], ident[:])
                    mm(pa[:, 3 * P:4 * P], SX[:, par, 2, tk], CTP[:, par, tk], start=True, stop=True, skip_group_check=True).then_inc(s("xs_ready"), 1)
                if i == 7 and there(base, -NT):
                    rows_of_x(base, 0)
                if there(base, k):
                    upto(pe, "ct3_ready", base, k + 1)
                    upto(pe, "pt_act", base, o + 1)
                    if front_b:
                        upto(pe, "xbc2_evac", base, fb + 2)
                    for h2 in range(2):
                        q = slice(512 * h2, 512 * h2 + 512)
                        mm(pY[:, q], identb[:], later[:, None, :].broadcast_to([P, 4, P]), start=True, stop=False, skip_group_check=True)
                        mm(pY[:, q], NCT3[:, par, :], pick[:, half * H + 4 * h2:half * H + 4 * h2 + 4, :], start=False, stop=False, skip_group_check=True)
                    for h in range(H):
                        last = mm(pY[:, P * h:P * h + P], pick[:, half * H + h, :], CT3[:, par, :], start=False, stop=True, skip_group_check=True)
                    last.then_inc(s("d_ps"), 1)
                if there(base, e):
                    upto(pe, "yg_ready", base, e + 1)
                    upto(pe, "t2_ready", base, e)
                    if front_b:
                        upto(pe, "u_ready", base, fb + 1)
                    if decays:
                        upto(pe, "ct3_ready", base, k + 2)
                    for m in range(2):
                        last = nc.tensor.transpose(pb[:, P * m:P * m + P], YG[:, P * m:P * m + P], ident[:])
                    last.then_inc(s("yT_ps"), 1)
                if isinstance(base, int) and base == 0 and i == 3:
                    pe.wait_ge(s("setup"), 1)
                if front_a:
                    upto(pe, "xn_ready", base, fa + 2)
                    upto(pe, "y2_ready", base, e + 1)
                    for j in range(2):
                        last = nc.tensor.transpose(pc[:, P * j:P * j + P], XN[:, j, :], ident[:])
                    last.then_inc(s("xnT_ps"), 2)
                if i == 7 and there(base, -NT):
                    logits(base, 0)
                if there(base, o):
                    upto(pe, "pt_act", base, o + 1)
                    upto(pe, "xdt_ready", base, k + 1)
                    upto(pe, "t_ready", base, o)
                    if o >= 0:
                        upto(pe, "v_ready", base, NT)
                    for j in range(NT):
                        last = mm(pa[:, 0:C], PT[:, P * j:P * j + P], V[:, j, :], start=j == 0, stop=j == NT - 1)
                    last.then_inc(s("o_ps"), 1)
                if there(base, e):
                    upto(pe, "yT_ready", base, e + 1)
                    for m in range(2):
                        last = mm(pb[:, 0:C], YT[:, m, :], wo[:, m, :], start=m == 0, stop=m == 1)
                    last.then_inc(s("out_ps"), 1)
                if i == 7 and there(base, -NT):
                    rows_of_x(base, 1)
                if i == 0 and there(base, 0):
                    upto(pe, "exp_ready", base, 1)
                    project_v()
                if i == NT - 1 and there(base, NT):
                    if isinstance(base, int):
                        pe.wait_ge(s("xT_loaded"), 16 * (base // NT + 2))
                    else:
                        pe.wait_ge(s("xT_loaded"), base * 2 + 32)
                    upto(pe, "exp_ready", base, NT)
                    project_q()
                if i == 7 and there(base, -NT):
                    logits(base, 1)
                if front_a:
                    upto(pe, "xnT_ready", base, fa + 2)
                    for m in range(2):
                        last = mm(pc[:, 256 * m:256 * m + 256], wx[:, P * m:P * m + P], XNT[:], start=True, stop=True, skip_group_check=True)
                    last.then_inc(s("xbc01_ps"), 2)
                    upto(pe, "expD_ready", base, k + 1)
                    upto(pe, "pt_act", base, o + 1)
                    mm(pY[:, 0:256], wx[:, 2 * P:3 * P], XNT[:], start=True, stop=True).then_inc(s("xbc2_ps"), 2)
                if there(base, k):
                    upto(pe, "xw_ready", base, k + 1)
                    upto(pe, "bnat_ready", base, k + 1)
                    upto(pe, "st_ready", base, k)
                    upto(pe, "yo_ready", base, k)
                    if front_b:
                        upto(pe, "u_ready", base, fb + 2)
                    if i == 7 and there(base, -NT):
                        upto(pe, "lg_ready", base, 0)
                    if k % NT != 0:
                        mm(pd[:, 0:DI], CTP[:, par, tk], ST[:], start=True, stop=True)
                    last = mm(pd[:, DI:2 * DI], BNAT[:], XW[:], start=k % NT == 0, stop=True, skip_group_check=True)
                    last.then_inc(s("state_ps"), 1)
                if i == 2 and there(base, -2 * NT):
                    upto(pe, "onehot_ready", base, -NT)
                    upto(pe, "y2_ready", base, e + 1)
                    for m, l in enumerate((tri, ones)):
                        last = mm(pc[:, 128 + 64 * m:192 + 64 * m], l[:], OHS[:].rearrange("p a b -> p (a b)"), start=True, stop=True, skip_group_check=True)
                    last.then_inc(s("places_ps"), NT)
                if front_b:
                    upto(pe, "ad_ready", base, fb + 2)
                    upto(pe, "y2_ready", base, e + 1)
                    mm(pc[:, 0:64], tri[:], AD[:], start=True, stop=True, skip_group_check=True)
                    mm(pc[:, 64:128], ones[:], AD[:], start=True, stop=True, skip_group_check=True).then_inc(s("cum_ps"), 2)

            pe.wait_ge(s("q_setup"), 1)
            pe.wait_ge(s("xT_loaded"), 16)
            project_q()
            pe.wait_ge(s("consts"), 1)
            batches(pe, step)

            pe.wait_ge(s("experts_loaded"), 16 * 5)
            pe.wait_ge(s("table_ready"), 1)

            def x_T(t, j):
                j, t = j % GROUP, t + j // GROUP * GROUP
                pe.wait_ge(s(f"gx{j}_loaded"), t * 4 + 16)
                nc.tensor.transpose(pa[:, 0:P], GX[:, j, 0:C], ident[:]).then_inc(s("gxt_ps"), 1)

            def experts_of(t):
                packed = pe.value_load(TBI[0:1, 1, bass.ds(t, 1)], min_val=0, max_val=E ** DIGITS - 1)
                return [packed // E ** j % E for j in range(DIGITS)]

            def hidden(n, par, expert, between):
                pe.wait_ge(s("gxt_ready"), n)
                cols = bass.ds(expert * HID, HID)
                mm(pX[:, 512 * par:512 * par + HID], GXT[:, par, :], W1[:, cols], start=True, stop=True).then_inc(s("h1_ps"), 1)
                between()
                mm(pY[:, 512 * par:512 * par + HID], GXT[:, par, :], W3[:, cols], start=True, stop=True).then_inc(s("h3_ps"), 1)

            def hidden_T(n, par):
                pe.wait_ge(s("hh_ready"), n)
                if not (isinstance(n, int) and n == 1):
                    pe.wait_ge(s("hT_ready"), n - 1)
                for k, (h0, hn) in enumerate(HC):
                    last = nc.tensor.transpose(pc[0:hn, P * k:P * k + P], HH[:, par, h0:h0 + hn], ident[:])
                last.then_inc(s("hT_ps"), 1)

            def result(n, par, expert):
                pe.wait_ge(s("hT_ready"), n)
                if not isinstance(n, int) or n > 2:
                    pe.wait_ge(s("ye_ready"), n - 2)
                for k, (h0, hn) in enumerate(HC):
                    last = mm((pd, pb)[par][:, 0:C], HT[0:hn, par, k, :], W2[0:hn, bass.ds(expert, 1), k, :], start=k == 0, stop=k == len(HC) - 1)
                last.then_inc(s("y_ps"), 1)

            def group(t):
                experts = experts_of(t)
                for j in range(GROUP):
                    def between():
                        if not (isinstance(t, int) and t + j == SLOTS - 1):
                            x_T(t, j + 1)
                        if not (isinstance(t, int) and t + j == 0):
                            hidden_T(t + j, (j - 1) % 2)
                    hidden(t + j + 1, j % 2, experts[2 + j], between)
                    if not (isinstance(t, int) and t + j < 2):
                        result(t + j - 1, j % 2, experts[j])
            x_T(0, 0)
            group(0)
            with pe.Fori(GROUP, SLOTS - 2 * GROUP + 1, GROUP) as t:
                group(t)
            group(SLOTS - GROUP)
            experts = experts_of(SLOTS)
            result(SLOTS - 1, 0, experts[0])
            hidden_T(SLOTS, 1)
            result(SLOTS, 1, experts[1])

        @block.scalar
        def _(act):
            A = nc.scalar.activation
            for dst, src in ((pcol[:, 0:1], dw1.rearrange("(p a) -> p a", a=1)), (pw1s[:], pw1), (pcol[:, 2:3], b1.rearrange("(p a) -> p a", a=1)),
                             (pcol[:, 1:2], dw2.rearrange("(p a) -> p a", a=1)), (pw2s[:], pw2)):
                act.dma_start(dst, src).then_inc(s("q_loaded"), 16)

            def take_q():
                for h in range(2):
                    q = slice(512 * h, 512 * h + 512)
                    last = A(QH[:, q], pX[:, q], ACT.Identity, bias=pcol[:, 2:3])
                last.then_inc(s("qh_ready"), NT)

            def step(base, i):
                o, k, e = i - 1, i - LAG, i - LAG - 1
                fa, fb = i - 3, i - 4
                front_a, front_b = i % 2 == 1 and there(base, fa), i % 2 == 0 and there(base, fb)
                decays = i % 2 == 1 and there(base, k)
                fpar, kpar = (fb // 2) % 2, (k // 2) % 2
                if decays:
                    upto(act, "cum1", base, k + 2)
                    A(ECUM[:, kpar], CT[:, 0:16].rearrange("p (a b) -> p a b", a=2), ACT.Exp)
                    A(ETOT[:, kpar], CT[:, 64:80].rearrange("p (a b) -> p a b", a=2), ACT.Exp).then_inc(s("ecum_ready"), 2)
                    upto(act, "sx_ready", base, k + 2)
                    A(CTP[0:NS, kpar, :], SX[NS:2 * NS, kpar, 2, :], ACT.Copy).then_inc(s("bc_ready"), 2)
                    upto(act, "dec_in", base, k + 2)
                    A(DEC[:, kpar], R1b[:], ACT.Exp).then_inc(s("dec_exp"), 2)
                if there(base, o):
                    upto(act, "pT_ps", base, o + 1)
                    upto(act, "o_ps", base, o)
                    A(PT[:], pY[:], ACT.Copy).then_inc(s("pt_act"), 1)
                if decays:
                    upto(act, "ct3_ps", base, k + 2)
                    A(CT3[0:48, kpar, :], pb[:, :].bitcast(bf16)[0:48, 0:P], ACT.Copy)
                    A(NCT3[0:48, kpar, :], pb[:, :].bitcast(bf16)[0:48, 0:P], ACT.Copy, scale=-1.0).then_inc(s("ct3_ready"), 2)
                if front_a:
                    upto(act, "norm_ready", base, fa + 2)
                    upto(act, "xnT_ps", base, fa)
                    for j in range(2):
                        last = A(XN[:, j, :], TA[:, fa % NT + j, :], ACT.Identity, bias=st[:, 5, 2 + j:3 + j], scale=st[:, 4, 2 + j:3 + j])
                    last.then_inc(s("xn_ready"), 2)
                if front_b:
                    for j in range(2):
                        upto(act, "z_ps", base, fb + j + 1)
                        upto(act, "sz_ready", base, fb)
                        A(TZ[:, j, :], (pb, pd)[j][:, 0:DI], ACT.Tanh).then_inc(s("tz_ready"), 1)
                    upto(act, "nau_ready", base, fb + 2)
                    A(dts[:, 2], dts[:, 1], ACT.Exp).then_inc(s("enau_ready"), 2)
                if i == 7 and there(base, -NT):
                    rows_of_x(base, 0)
                if there(base, k):
                    upto(act, "xs_ready", base, k + 1)
                    upto(act, "state_ps", base, k)
                    A(BNAT[:], pa[:, 2 * P:3 * P], ACT.Copy).then_inc(s("bnat_ready"), 1)
                    upto(act, "m_ready", base, k)
                    A(GT[:], pa[:, 3 * P:4 * P], ACT.Copy).then_inc(s("gT_ready"), 1)
                if there(base, i):
                    upto(act, "nm_ready", base, i + 1)
                    upto(act, "pT_ps", base, i)
                    upto(act, "rg_ready", base, i - 1)
                    A(PR[:], pX[:], ACT.Exp, bias=NM[:, i:i + 1], accum_out=RS[:, i:i + 1]).then_inc(s("exp_ready"), 1)
                if there(base, e):
                    upto(act, "yg_ready", base, e + 1)
                    upto(act, "sst_ready", base, e)
                    A(SQ[:], YG[:], ACT.Square, accum_out=SS[:]).then_inc(s("ss_ready"), 1)
                    upto(act, "yT_ps", base, e + 1)
                    A(YT[:].rearrange("p a b -> p (a b)"), pb[:, 0:DI], ACT.Copy).then_inc(s("yT_ready"), 1)
                if front_a:
                    upto(act, "xnT_ps", base, fa + 2)
                    A(XNT[:], pc[:, 0:2 * P], ACT.Copy).then_inc(s("xnT_ready"), 2)
                if there(base, k):
                    upto(act, "d_ps", base, k + 1)
                    A(ED[:].rearrange("p h t -> p (h t)"), pY[:], ACT.Exp).then_inc(s("expD_ready"), 1)
                if front_a:
                    for j in range(2):
                        last = A(TR[:, fa % NT + j, :], TA[:, fa % NT + j, :], ACT.Identity, bias=st[:, 5, j:j + 1], scale=st[:, 6, j:j + 1])
                    last.then_inc(s("tr_ready"), 2)
                if i == 7 and there(base, -NT):
                    rows_of_x(base, 1)
                    upto(act, "xa_ready", base, 0)
                    A(XA[:, 1, :, 0:C], XA[:, 0, :, 0:C], ACT.Copy).then_inc(s("xa_copied"), NT)
                if i == NT - 1 and there(base, NT):
                    upto(act, "qps", base, 2 * NT)
                    upto(act, "s_ready", base, NT)
                    take_q()
                if front_a:
                    fo = (fa % NT) * P + TAPS - 1
                    upto(act, "xbc01_ps", base, fa + 2)
                    A(XBC[:, 0:2, fo:fo + 256], pc[:].rearrange("p (m t) -> p m t", m=2), ACT.Copy).then_inc(s("xbc01_evac"), 2)
                    upto(act, "xbc2_ps", base, fa + 2)
                    A(XBC[:, 2, fo:fo + 256], pY[:, 0:256], ACT.Copy).then_inc(s("xbc2_evac"), 2)
                    upto(act, "xbc2_evac", base, fa + 2)
                    upto(act, "sx_ready", base, fa)
                    for m in range(3):
                        last = A(CV[:, m, :], XBC[:, m, fo:fo + 256], ACT.Identity, bias=cb[:, m:m + 1], scale=cw[:, m, 3:4])
                        if m == 1:
                            last.then_inc(s("cv01_evac"), 2)
                    last.then_inc(s("cv_evac"), 2)
                if i == 6 and there(base, -NT):
                    upto(act, "rstd2_ready", base, 0)
                    if not (isinstance(base, int) and base == NT):
                        act.wait_ge(s("scattered"), base * (16 * TOP) - 16 * TOP * NT)
                    for j in range(NT):
                        last = A(XA[:, 0, j, 0:C], T2[:, bass.ds(base - NT + j, 1), :].rearrange("p a c -> p (a c)"), ACT.Identity, bias=rs2[:, 2, j:j + 1], scale=rs2[:, 1, j:j + 1])
                        if j % 4 == 3:
                            last.then_inc(s("xa_ready"), 4)
                if i == 0 and there(base, 0):
                    upto(act, "projected", base, NT)
                    upto(act, "o_ps", base, 0)
                    A(V[:].rearrange("p j c -> p (j c)"), pX[:], ACT.Copy).then_inc(s("v_copied"), NT)
                if front_b:
                    upto(act, "conv_ready", base, fb + 2)
                    upto(act, "sx_ready", base, fb)
                    A(TH[:], CV[:], ACT.Tanh).then_inc(s("th_ready"), 2)
                if i == 0 and there(base, -2 * NT):
                    upto(act, "lsub_ready", base, -NT)
                    A(PB[:], LG[:], ACT.Exp).then_inc(s("pexp_ready"), NT)

            def rows_of_x(base, grp):
                upto(act, "vT_ps", base, 4 * grp - 4)
                A(VT[:], pd[:], ACT.Copy).then_inc(s("vT_ready"), 4)

            act.wait_ge(s("qps"), NT)
            take_q()
            act.wait_ge(s("loaded"), 16 * NLOAD)
            A(hrow[:, 1, :], hrow[:, 1, :], ACT.Exp).then_inc(s("a_exp"), 1)
            batches(act, step)

            def rows_T(n, par):
                act.wait_ge(s("gxt_ps"), n)
                A(GXT[:, par, :], pa[:, 0:P], ACT.Copy).then_inc(s("gxt_ready"), 1)

            def silu(n, par):
                act.wait_ge(s("h1_ps"), n)
                A(SH[:, par, :], pX[:, 512 * par:512 * par + HID], ACT.Silu).then_inc(s("silu_ready"), 1)

            def gate(t, j):
                n = t + j + 1
                act.wait_ge(s("y_ps"), n)
                act.wait_ge(s("dix_ready"), n)
                if not (isinstance(t, int) and t == 0):
                    act.wait_ge(s(f"ye{j}_scattered"), t * 4)
                A(YE[:, j, :], (pd, pb)[j % 2][:, 0:C], ACT.Copy, scale=GATE[:, j, 0:1]).then_inc(s("ye_ready"), 1)

            def group(t):
                for j in range(GROUP):
                    if not (isinstance(t, int) and t + j == SLOTS - 1):
                        rows_T(t + j + 2, (j + 1) % 2)
                    silu(t + j + 1, j % 2)
                    if j >= 2:
                        gate(t, j - 2)
                    elif not (isinstance(t, int) and t == 0):
                        gate(t - GROUP, GROUP + j - 2)
            A(SS[:], SS[:], ACT.Silu)
            rows_T(1, 0)
            group(0)
            with act.Fori(GROUP, SLOTS - 2 * GROUP + 1, GROUP) as t:
                group(t)
            group(SLOTS - GROUP)
            for j in (2, 1):
                gate(SLOTS - GROUP, GROUP - j)
            for b in range(TILES // NT):
                tiles = slice(b * NT, b * NT + NT)
                act.wait_ge(s("added"), b + 1)
                act.dma_start(out.rearrange("(t p) c -> p t c", p=P)[:, tiles, :], T2[:, tiles, :]).then_inc(s("stored"), 16)
            act.wait_ge(s("stored"), 16 * (TILES // NT))

        @block.gpsimd
        def _(pool):
            g = nc.gpsimd
            g.memset(ident[:], 0.0).then_inc(s("filled"), 1)
            g.memset(cw[:], 0.0)
            g.memset(cb[:], 0.0).then_inc(s("zeroed"), 1)
            for t, v in ((wx[:, DI + 2 * NS:], 0.0), (CTP[:], 0.0), (XBC[:, :, 0:TAPS - 1], 0.0), (AD[:], 0.0), (CT3[:], 0.0),
                         (NCT3[:], 0.0), (ST[:], 0.0), (XDT[:, :, DI:], 0.0), (ones[:], 1.0), (mhalf[:], -0.5)):
                g.memset(t, v)
            g.memset(tri[:], 1.0)
            g.memset(later[:], 0.0)
            g.memset(pick[:], 0.0).then_inc(s("filled"), 1)
            pool.wait_ge(s("filled"), 2)
            g.affine_select(out=tri[:], in_=tri[:], compare_op=ALU.is_ge, fill=0.0, base=0, pattern=[[1, P]], channel_multiplier=-1)
            g.affine_select(out=later[:], in_=later[:], compare_op=ALU.is_ge, fill=-1e30, base=0, pattern=[[1, P]], channel_multiplier=-1)
            for j in range(3):
                g.affine_select(out=pick[:], in_=pick[:], compare_op=ALU.not_equal, fill=1.0, base=-16 * j,
                                pattern=[[-1, 16], [0, P]], channel_multiplier=1).then_inc(s("picked"), 1)
                pool.wait_ge(s("picked"), j + 1)
            g.affine_select(out=ident[:], in_=ident[:], compare_op=ALU.not_equal, fill=1.0, base=0, pattern=[[-1, P]], channel_multiplier=1).then_inc(s("filled"), 1)
            pool.wait_ge(s("filled"), 3)
            g.tensor_copy(identb[:], ident[:]).then_inc(s("consts"), 1)
            g.memset(rT[:, E:], 0.0)
            g.memset(OFF[:], 0.0)
            g.memset(EXPERT[:], 0.0).then_inc(s("iotas"), 1)
            g.memset(ZT[:], 0.0).then_inc(s("zt_ready"), 1)
            lazy = dict(allow_small_or_imprecise_dtypes=True)
            g.iota(iota8[:], [[1, E]], base=0, channel_multiplier=0, **lazy)
            g.iota(TOK[:], [[P, NT]], base=0, channel_multiplier=1, **lazy)
            g.iota(pidx[:], [[0, 1]], base=0, channel_multiplier=1, **lazy)
            g.iota(itile[:], [[1, SLOTS]], base=0, channel_multiplier=0, **lazy)
            g.iota(TB[:, 0, 0:2 * E], [[P, 2 * E]], base=PAD, channel_multiplier=1, **lazy).then_inc(s("iotas"), 1)
            pool.wait_ge(s("iotas"), 2)
            pool.wait_ge(s("zt_ready"), 1)
            g.tensor_copy(ZT[:, :, C + 1], TB[:, 0, 0:2 * E]).then_inc(s("zt_ready"), 1)
            g.tensor_scalar(ebase[:], iota8[:], float(REGION), -1.0, ALU.mult, ALU.add).then_inc(s("iotas"), 1)

            def norm_for_experts(base):
                upto(pool, "mv2_ready", base, 0)
                steps = Steps(pool, "norm2_steps", base, -NT, NT, 1)
                apart(pool)
                steps.then(g.tensor_scalar(rs2[:, 0, :], MV2[:, :, 1], LN_EPS, 1.0, ALU.add, ALU.mult))
                steps.then(g.tensor_tensor(rs2[:, 1, :], rs2[:, 0, :], mhalf[:, 0:1].broadcast_to([P, NT]), ALU.pow))
                steps.then(g.tensor_tensor(rs2[:, 0, :], MV2[:, :, 0], rs2[:, 1, :], ALU.mult), True)
                apart(pool)
                g.tensor_scalar(rs2[:, 2, :], rs2[:, 0, :], -1.0, 1.0, ALU.mult, ALU.mult).then_inc(s("rstd2_ready"), NT)

            def step(base, i):
                o, k, e = i - 1, i - LAG, i - LAG - 1
                fn = i - 2
                par, half = (k // 2) % 2, k % 2
                if there(base, k):
                    b3 = lambda t: t[:, par, half, :, None].broadcast_to([P, H, HD])
                    v3 = lambda t: t[:, 0:DI].rearrange("p (h d) -> p h d", h=H)
                    if k % NT != 0:
                        upto(pool, "st_ready", base, k)
                        upto(pool, "ecum_ready", base, k + 1)
                        g.tensor_tensor(v3(STE)[0:NS], v3(ST)[0:NS], ETOT[0:NS, par, half, :, None].broadcast_to([NS, H, HD]), ALU.mult).then_inc(s("ste_ready"), 1)
                    else:
                        pool.sem_inc(s("ste_ready"), 1)
                if there(base, e):
                    upto(pool, "y2_ready", base, e + 1)
                    upto(pool, "sz_ready", base, e + 1)
                    upto(pool, "ss_ready", base, e)
                    upto(pool, "yT_ps", base, e)
                    g.tensor_tensor(YG[:], Y2[:], SZ[:, (e // 2) % 2, e % 2, :], ALU.mult).then_inc(s("yg_ready"), 1)
                if there(base, k):
                    upto(pool, "xdt_ready", base, k + 1)
                    upto(pool, "dec_exp", base, k + 1)
                    upto(pool, "state_ps", base, k)
                    g.tensor_tensor(v3(XW), v3(XDT[:, k % 2, :]), b3(DEC), ALU.mult).then_inc(s("xw_ready"), 1)
                if there(base, e):
                    upto(pool, "ss_ready", base, e + 1)
                    upto(pool, "t2_ready", base, e)
                    apart(pool)
                    g.tensor_scalar(RY[:, 0, 0:1], SS[:], 1.0 / DI, RMS_EPS, ALU.mult, ALU.add).then_inc(s("sst_ready"), 1)
                    upto(pool, "sst_ready", base, e + 1)
                    g.tensor_tensor(RY[:, 1, 0:1], RY[:, 0, 0:1], mhalf[:, 0:1], ALU.pow).then_inc(s("ry_ready"), 1)
                last_norm = isinstance(base, int) and base == TILES
                if i == 5 and last_norm:
                    norm_for_experts(base)
                if 3 <= i <= 5 and there(base, -2 * NT):
                    if i == 3:
                        upto(pool, "slots_ready", base, -NT)
                        upto(pool, "xb_ready", base, -NT)
                        upto(pool, "xa_copied", base, -NT)
                        apart(pool)
                    for j in range((0, 6, 10)[i - 3], (6, 10, 16)[i - 3]):
                        scatter_rows(j)
                if i == 5 and there(base, -NT) and not last_norm:
                    norm_for_experts(base)
                if i % 2 == 0 and there(base, fn):
                    mean, var = MV[:, fn % NT:fn % NT + 2, 0], MV[:, fn % NT:fn % NT + 2, 1]
                    upto(pool, "mv_ready", base, fn + 2)
                    steps = Steps(pool, "norm_steps", base, fn, 2, 2)
                    upto(pool, "tr_ready", base, fn)
                    apart(pool)
                    g.tensor_scalar(st[:, 0, 0:2], var, 1.0, LN_EPS, ALU.mult, ALU.add)
                    g.tensor_scalar(st[:, 2, 0:2], mean, -1.0, 0.0, ALU.mult, ALU.add)
                    steps.then(g.tensor_scalar(st[:, 0, 2:4], var, 1.0 + FLT_EPS, LN_EPS * FLT_EPS, ALU.mult, ALU.add))
                    steps.then(g.tensor_tensor(st[:, 4, 0:4], st[:, 0, 0:4], mhalf[:, 0:1].broadcast_to([P, 4]), ALU.pow), True)
                    apart(pool)
                    g.tensor_scalar(st[:, 6, 0:2], st[:, 4, 0:2], 1.0, 1.0, ALU.mult, ALU.add)
                    g.tensor_tensor(st[:, 5, 0:4].rearrange("p (a b) -> p a b", a=2), st[:, 4, 0:4].rearrange("p (a b) -> p a b", a=2),
                                    st[:, 2, None, 0:2].broadcast_to([P, 2, 2]), ALU.mult).then_inc(s("norm_ready"), 2)
                if i == 0 and there(base, 0):
                    upto(pool, "v_copied", base, NT)
                    g.tensor_tensor(V[:], V[:], b2b[:, None, :].broadcast_to([P, NT, C]), ALU.add).then_inc(s("v_ready"), NT)

            def scatter_rows(j):
                g.indirect_dma_start(xg, bass.IndirectOffsetOnAxis(ap=SL[:, j // NT, j % NT:j % NT + 1], axis=0), XA[:, j // NT, j % NT, :], None).then_inc(s("scattered"), 16)

            pool.wait_ge(s("loaded"), 16 * NLOAD)
            batches(pool, step)

            def put(t, j):
                pool.wait_ge(s("ye_ready"), t + j + 1)
                apart(pool)
                g.indirect_dma_start(yg, bass.IndirectOffsetOnAxis(ap=DIX[:, j, :], axis=0), YE[:, j, :], None).then_inc(s(f"ye{j}_scattered"), 16)
            with pool.Fori(0, SLOTS - GROUP + 1, GROUP) as t:
                for j in range(GROUP):
                    put(t, j)

        @block.vector
        def _(dve):
            v = nc.vector
            tt, ts, stt = v.tensor_tensor, v.tensor_scalar, v.scalar_tensor_tensor

            def take_ql():
                for h in range(2):
                    q = slice(512 * h, 512 * h + 512)
                    last = stt(QL[:, q], pX[:, q], pcol[:, 2:3], QH[:, q].bitcast(fp32), ALU.add, ALU.subtract)
                last.then_inc(s("q_ready"), NT)

            def route_a(base):
                bc = lambda a: a[:, :, None].broadcast_to([P, NT, E])
                steps = Steps(dve, "route_a_steps", base, -2 * NT, NT, 4)
                then = steps.then
                v.tensor_copy(XA[:, 0, :, C + 1], TOK[:])
                ts(XA[:, 1, :, C + 1], TOK[:], float(TOKENS), None, ALU.add)
                upto(dve, "pexp_ready", base, -NT)
                then(v.tensor_reduce(r8[:, 1, :], PB[:], AX.X, ALU.add))
                then(v.reciprocal(r8[:, 2, :], r8[:, 1, :]))
                then(ts(TOK[:], TOK[:], float(NT * P), None, ALU.add))
                then(tt(PB[:], PB[:], bc(r8[:, 2, :]), ALU.mult))
                apart(dve)
                for j in range(NT):
                    last = v.max(M8[:, j, :], PB[:, j, :])
                then(last)
                apart(dve)
                for j in range(NT):
                    last = v.max_index(IX[:, j, :], M8[:, j, :], PB[:, j, :])
                then(last)
                then(tt(r8[:, 3, :], M8[:, :, 0], M8[:, :, 1], ALU.add))
                then(ts(r8[:, 4, :], r8[:, 3, :], 1e-9, None, ALU.add))
                then(v.reciprocal(r8[:, 5, :], r8[:, 4, :]))
                for c_ in range(TOP):
                    last = tt(XA[:, c_, :, C], M8[:, :, c_], r8[:, 5, :], ALU.mult)
                last.then_inc(s("xb_ready"), NT)
                then(v.tensor_copy(IXF[:], IX[:, :, 0:TOP]))
                for c_ in range(TOP):
                    last = tt(OH[:, c_], iota8[:, None, :].broadcast_to([P, NT, E]), bc(IXF[:, :, c_]), ALU.is_equal)
                then(last, True)
                tt(OHS[:], OH[:, 0], OH[:, 1], ALU.add).then_inc(s("onehot_ready"), NT)

            def route_b(base):
                steps = Steps(dve, "route_b_steps", base, -2 * NT, NT, 4)
                then = steps.then
                upto(dve, "places_read", base, -NT)
                for j in range(NT):
                    then(tt(OFF[:, j + 1, :], OFF[:, j, :], PCT[:, 1, j, :], ALU.add))
                then(tt(SA[:], PCT[:, 0], OFF[:, 0:NT, :], ALU.add))
                then(v.tensor_copy(OFF[:, 0, :], OFF[:, NT, :]))
                then(tt(SA[:], SA[:], ebase[:, None, :].broadcast_to([P, NT, E]), ALU.add))
                for c_ in range(TOP):
                    then(tt(PM[:], OH[:, c_], SA[:], ALU.mult))
                    then(v.tensor_reduce(SLF[:, c_, :], PM[:], AX.X, ALU.add), c_ == TOP - 1)
                v.tensor_copy(SL[:], SLF[:]).then_inc(s("slots_ready"), NT)

            def step(base, i):
                o, k, e = i - 1, i - LAG, i - LAG - 1
                fa, fb = i - 3, i - 4
                front_a, front_b = i % 2 == 1 and there(base, fa), i % 2 == 0 and there(base, fb)
                decays = i % 2 == 1 and there(base, k)
                par, half = (k // 2) % 2, k % 2
                fpar = (fb // 2) % 2
                b3 = lambda t: t[:, par, half, :, None].broadcast_to([P, H, HD])
                v3 = lambda t: t[:, 0:DI].rearrange("p (h d) -> p h d", h=H)
                p3 = lambda a: CT[:, a:a + 16].rearrange("p (a b) -> p a b", a=2)
                CUM = p3(0)

                def conv(tap, m):
                    fo = (fb % NT) * P
                    return stt(CV[:, m, :], XBC[:, m, fo + tap:fo + tap + 256], cw[:, m, tap:tap + 1], CV[:, m, :], ALU.mult, ALU.add)

                if decays:
                    upto(dve, "th_ready", base, k + 2)
                    stt(SX[:, par].rearrange("p a b -> p (a b)"), TH[:].rearrange("p a b -> p (a b)"), 1.0, CV[:].rearrange("p a b -> p (a b)"), ALU.add, ALU.mult).then_inc(s("sx_ready"), 2)
                    upto(dve, "cum1", base, k + 2)
                    upto(dve, "ct3_ps", base, k)
                    v.tensor_copy(C3[:, 0], CUM).then_inc(s("cum2"), 2)
                    tt(R1b[:], p3(64), CUM, ALU.subtract).then_inc(s("dec_in"), 2)
                    upto(dve, "cum2", base, k + 2)
                    tt(R1[:], CUM, C3[:, 0], ALU.subtract).then_inc(s("cum3"), 2)
                    upto(dve, "cum3", base, k + 2)
                    v.tensor_copy(C3[:, 1], R1[:]).then_inc(s("cum4"), 2)
                    upto(dve, "cum4", base, k + 2)
                    tt(C3[:, 2], R1[:], C3[:, 1], ALU.subtract).then_inc(s("c3_ready"), 2)
                if front_b:
                    upto(dve, "cv01_evac", base, fb + 2)
                    conv(2, 0)
                    conv(2, 1)
                    upto(dve, "cv_evac", base, fb + 2)
                    last = conv(2, 2)
                    last.then_inc(s("conv_tap2"), 2)
                if there(base, i):
                    upto(dve, "s_ready", base, i + 1)
                    v.tensor_reduce(NM[:, i:i + 1], pX[:], AX.X, ALU.max, negate=True).then_inc(s("nm_ready"), 1)
                if front_b:
                    for j in range(2):
                        bank = (pb, pd)[j]
                        upto(dve, "tz_ready", base, fb + j + 1)
                        stt(SZ[:, fpar, j, :], TZ[:, j, :], 1.0, bank[:, 0:DI], ALU.add, ALU.mult).then_inc(s("sz_ready"), 1)
                        tt(dts[:, 0, j, :], bank[:, DI:DI + H], hrow[:, 0, :], ALU.add).then_inc(s("u_ready"), 1)
                    upto(dve, "u_ready", base, fb + 2)
                    stt(dts[:, 1], dts[:, 0], -1.0, dts[:, 0], ALU.mult, ALU.min).then_inc(s("nau_ready"), 2)
                    ts(dts[:, 3], dts[:, 0], 0.0, None, ALU.max)
                    upto(dve, "conv_tap2", base, fb + 2)
                    steps = Steps(dve, "softplus_steps", base, fb, 2, 8)
                    upto(dve, "enau_ready", base, fb + 2)
                    ts(dts[:, 4], dts[:, 2], 2.0, None, ALU.add).then_inc(s("e2_ready"), 2)
                if there(base, e):
                    upto(dve, "ydiag_ps", base, e + 1)
                    upto(dve, "yg_ready", base, e)
                    y_heads = pc[:].rearrange("p (h w) -> p h w", h=H)[:, :, 0:HD]
                    if e % NT != 0:
                        upto(dve, "yo_ready", base, e + 1)
                        last = tt(v3(Y2), y_heads, v3(YO), ALU.add)
                    else:
                        last = v.tensor_copy(v3(Y2), y_heads)
                    last.then_inc(s("y2_ready"), 1)
                if front_b:
                    upto(dve, "e2_ready", base, fb + 2)
                    steps.then(v.reciprocal(dts[:, 9], dts[:, 4]))
                    steps.then(tt(dts[:, 5], dts[:, 2], dts[:, 9], ALU.mult))
                if there(base, k):
                    upto(dve, "gT_ready", base, k + 1)
                    upto(dve, "xw_ready", base, k - 1)
                    upto(dve, "ydiag_ps", base, k - 1)
                    tt(v3(XDT[:, k % 2, :]), v3(pa), b3(DT), ALU.mult).then_inc(s("xdt_ready"), 1)
                if front_b:
                    steps.then(tt(dts[:, 6], dts[:, 5], dts[:, 5], ALU.mult))
                if i == 7 and there(base, -NT):
                    take_logits(base, 0)
                if i == 1 and there(base, -2 * NT):
                    route_a(base)
                if i == 3 and there(base, -2 * NT):
                    route_b(base)
                if front_b:
                    steps.then(ts(dts[:, 7], dts[:, 6], ATANH[4], None, ALU.mult))
                    conv(1, 0)
                    steps.then(stt(dts[:, 8], dts[:, 7], ATANH[3], dts[:, 6], ALU.add, ALU.mult))
                    conv(1, 1)
                    steps.then(stt(dts[:, 7], dts[:, 8], ATANH[2], dts[:, 6], ALU.add, ALU.mult))
                    conv(1, 2).then_inc(s("conv_tap1"), 2)
                    steps.then(stt(dts[:, 8], dts[:, 7], ATANH[1], dts[:, 6], ALU.add, ALU.mult))
                    steps.then(stt(dts[:, 7], dts[:, 8], ATANH[0], dts[:, 5], ALU.add, ALU.mult))
                if there(base, o):
                    v.reciprocal(RG[:, o % NT:o % NT + 1], RS[:, o % NT:o % NT + 1]).then_inc(s("rcp_ready"), 1)
                if front_b:
                    steps.then(stt(DT[:, fpar], dts[:, 7], 2.0, dts[:, 3], ALU.mult, ALU.add), True)
                if there(base, o):
                    upto(dve, "rcp_ready", base, o + 1)
                    ts(RG[:, o % NT:o % NT + 1], RG[:, o % NT:o % NT + 1], pcol[:, 4:5], None, ALU.mult).then_inc(s("rg_ready"), 1)
                if front_b:
                    upto(dve, "cum_ps", base, fb)
                    stt(AD[:, 0:16].rearrange("p (a b) -> p a b", a=2), DT[:, fpar], -1.0, hrow[:, 1:2, :].broadcast_to([P, 2, H]), ALU.mult, ALU.mult).then_inc(s("ad_ready"), 2)
                if there(base, k):
                    upto(dve, "expD_ready", base, k + 1)
                    upto(dve, "gT_ready", base, k + 1)
                    upto(dve, "ydiag_ps", base, k)
                    tt(M[:], ED[:], GT[:, None, :].broadcast_to([P, H, P]), ALU.mult).then_inc(s("m_ready"), 1)
                if there(base, o):
                    upto(dve, "rg_ready", base, o + 1)
                    upto(dve, "o_ps", base, o + 1)
                    if o % 4 == 0:
                        if isinstance(base, int):
                            dve.wait_ge(s(f"x{o // 4}_loaded"), 16 * (base // NT + 1))
                        else:
                            dve.wait_ge(s(f"x{o // 4}_loaded"), base * 2 + 16)
                    stt(TA[:, o % NT, :], pa[:, 0:C], RG[:, o % NT:o % NT + 1], X[:, o % NT, :], ALU.mult, ALU.add).then_inc(s("t_ready"), 1)
                if there(base, e):
                    upto(dve, "out_ps", base, e + 1)
                    upto(dve, "ry_ready", base, e + 1)
                    upto(dve, "tr_ready", base, e + 1)
                    t2 = T2[:, bass.ds(base + e, 1), :].rearrange("p a c -> p (a c)")
                    stt(t2, pb[:, 0:C], RY[:, 1, 0:1], TR[:, e % NT, :], ALU.mult, ALU.add).then_inc(s("t2_ready"), 1)
                if there(base, o):
                    upto(dve, "t_ready", base, o + 1)
                    v.bn_stats(BN[:, o % NT, :], TA[:, o % NT, :]).then_inc(s("bn_ready"), 1)
                if front_b:
                    upto(dve, "conv_tap1", base, fb + 2)
                    for m in range(3):
                        last = conv(0, m)
                    last.then_inc(s("conv_ready"), 2)
                if there(base, e):
                    upto(dve, "t2_ready", base, e + 1)
                    apart(dve)
                    v.bn_stats(BN2[:, e % NT, :], t2).then_inc(s("bn2_ready"), 1)
                if there(base, o):
                    upto(dve, "bn_ready", base, o + 1)
                    apart(dve)
                    v.bn_aggr(MV[:, o % NT, :], BN[:, o % NT, :]).then_inc(s("mv_ready"), 1)
                if i == 7 and there(base, -NT):
                    take_logits(base, 1)
                if i == NT - 1 and there(base, NT):
                    upto(dve, "qh_ready", base, 2 * NT)
                    take_ql()
                if front_b:
                    upto(dve, "cum_ps", base, fb + 2)
                    upto(dve, "dec_exp", base, fb)
                    v.tensor_copy(CT[:], pc[:, 0:P]).then_inc(s("cum1"), 2)
                if i == 2 and there(base, -2 * NT):
                    upto(dve, "places_ps", base, -NT)
                    v.tensor_copy(PCT[:].rearrange("p m a b -> p (m a b)"), pc[:, P:2 * P]).then_inc(s("places_read"), NT)
                if there(base, k) and k % NT != 0:
                    upto(dve, "state_ps", base, k + 1)
                    upto(dve, "y2_ready", base, k)
                    tt(v3(YO), v3(pd), b3(ECUM), ALU.mult).then_inc(s("yo_ready"), 1)
                if there(base, e):
                    if e % NT == 0:
                        upto(dve, "rstd2_ready", base, e)
                    upto(dve, "bn2_ready", base, e + 1)
                    apart(dve)
                    v.bn_aggr(MV2[:, e % NT, :], BN2[:, e % NT, :]).then_inc(s("mv2_ready"), 1)
                if there(base, k):
                    if k % NT != 0:
                        upto(dve, "ste_ready", base, k + 1)
                        tt(ST[0:NS, :], STE[0:NS, :], pd[0:NS, DI:2 * DI], ALU.add).then_inc(s("st_ready"), 1)
                    else:
                        upto(dve, "state_ps", base, k + 1)
                        v.tensor_copy(ST[0:NS, :], pd[0:NS, DI:2 * DI]).then_inc(s("st_ready"), 1)
                        v.nop().then_inc(s("yo_ready"), 1)
                if i == 7 and there(base, -NT):
                    upto(dve, "lg_ready", base, 0)
                    v.tensor_reduce(r8[:, 0, :], LG[:], AX.X, ALU.max).then_inc(s("lmax_ready"), NT)
                    upto(dve, "lmax_ready", base, 0)
                    tt(LG[:], LG[:], r8[:, 0, :, None].broadcast_to([P, NT, E]), ALU.subtract).then_inc(s("lsub_ready"), NT)

            def take_logits(base, grp):
                upto(dve, "logits_ps", base, 4 * grp - 4)
                v.tensor_copy(LG[:, 4 * grp:4 * grp + 4, :], pd[:, 0:256].rearrange("p (j w) -> p j w", j=4)[:, :, 0:E]).then_inc(s("lg_ready"), 4)

            dve.wait_ge(s("q_loaded"), 16 * 5)
            ts(pw1s[:], pw1s[:], pcol[:, 0:1], None, ALU.mult)
            ts(pw2s[:], pw2s[:], pcol[:, 1:2], None, ALU.mult).then_inc(s("q_setup"), 1)
            dve.wait_ge(s("qh_ready"), NT)
            take_ql()
            dve.wait_ge(s("loaded"), 16 * NLOAD)
            dve.wait_ge(s("consts"), 1)
            dve.wait_ge(s("a_exp"), 1)
            ts(wz[:, 0:DI], wz[:, 0:DI], pcol[:, 3:4], 0.5, ALU.mult, ALU.mult)
            ts(wz[:, DI:], wz[:, DI:], pcol[:, 3:4], None, ALU.mult)
            ts(wx[:], wx[:], pcol[:, 3:4], None, ALU.mult)
            ts(cw[:], cw[:], 0.5, None, ALU.mult)
            ts(cb[:], cb[:], 0.5, None, ALU.mult)
            for m in range(2):
                last = ts(wo[:, m, :], wo[:, m, :], gw[:, m:m + 1], None, ALU.mult)
            for m in range(2):
                last = tt(diagD[:, m, :].rearrange("p (h d) -> p h d", d=HD), ident[:].rearrange("p (h d) -> p h d", d=HD),
                          hrow[:, 2, 4 * m:4 * m + 4, None].broadcast_to([P, 4, HD]), ALU.mult)
            last.then_inc(s("setup"), 1)
            batches(dve, step)

            steps = Steps(dve, "table_steps", 0, 0, 1, 64)
            then = steps.then
            runs = OFF[:, 0, :]
            dve.wait_ge(s("iotas"), 3)
            dve.wait_ge(s("route_b_steps"), 4 * TILES)
            dve.wait_ge(s("slots_ready"), TILES)
            then(tt(NTE[:], runs, ebase[:], ALU.add))
            then(ts(NTE[:], NTE[:], pidx[:, 0:1], 1.0, ALU.add, ALU.add))
            v.tensor_copy(ZI[:], NTE[:]).then_inc(s("zi_ready"), 1)
            dve.wait_ge(s("zi_ready"), 1)
            then(ts(NTE[:], runs, 1.0 / P, (P - 1) / P - 63.5 / P, ALU.mult, ALU.add))
            then(v.tensor_copy(NTI[:], NTE[:]))
            then(v.tensor_copy(NTE[:], NTI[:]))
            then(v.tensor_copy(CTE[:, 0:1], NTE[:, 0:1]))
            for x_ in range(1, E):
                then(tt(CTE[:, x_:x_ + 1], CTE[:, x_ - 1:x_], NTE[:, x_:x_ + 1], ALU.add))
            by = lambda a: a[:, None, :].broadcast_to([P, SLOTS, E])
            then(tt(GE[:], itile[:, :, None].broadcast_to([P, SLOTS, E]), by(CTE), ALU.is_ge))
            then(v.tensor_reduce(TB[:, 0, :], GE[:], AX.X, ALU.add))
            then(tt(GE[:], GE[:], by(NTE), ALU.mult))
            then(v.tensor_reduce(TB[:, 1, :], GE[:], AX.X, ALU.add))
            then(tt(TB[:, 1, :], itile[:], TB[:, 1, :], ALU.subtract))
            then(ts(TB[:, 1, :], TB[:, 1, :], float(P), None, ALU.mult))
            then(stt(TB[:, 2, :], TB[:, 0, :], float(REGION), TB[:, 1, :], ALU.mult, ALU.add))
            then(ts(EXPERT[:, 2:2 + SLOTS], TB[:, 0, :], float(E - 1), None, ALU.min))
            then(v.tensor_copy(DIGS[:], EXPERT[:, DIGITS - 1:DIGITS + SLOTS]))
            for j in range(DIGITS - 2, -1, -1):
                then(stt(DIGS[:], DIGS[:], float(E), EXPERT[:, j:j + SLOTS + 1], ALU.mult, ALU.add))
            v.tensor_copy(TBI[:, 0, 0:SLOTS], TB[:, 2, :])
            v.tensor_copy(TBI[:, 1, :], DIGS[:]).then_inc(s("table_ready"), 1)

            def gated(n, par):
                dve.wait_ge(s("silu_ready"), n)
                dve.wait_ge(s("h3_ps"), n)
                tt(HH[:, par, :], SH[:, par, :], pY[:, 512 * par:512 * par + HID], ALU.mult).then_inc(s("hh_ready"), 1)

            def turned(n, par):
                dve.wait_ge(s("hT_ps"), n)
                v.tensor_copy(HT[:, par].rearrange("p k t -> p (k t)"), pc[:, 0:P * len(HC)]).then_inc(s("hT_ready"), 1)

            def take_gates(t, j):
                dve.wait_ge(s(f"gx{j}_loaded"), t * 4 + 16)
                if not (isinstance(t, int) and t == 0):
                    dve.wait_ge(s(f"ye{j}_scattered"), t * 4)
                v.tensor_copy(DIX[:, j, :], GX[:, j, C + 1:C + 2])
                v.tensor_copy(GATE[:, j, :], GX[:, j, C:C + 1]).then_inc(s("dix_ready"), 1)

            def group(t):
                for j in range(GROUP):
                    if not (isinstance(t, int) and t + j == 0):
                        turned(t + j, (j - 1) % 2)
                    gated(t + j + 1, j % 2)
                    take_gates(t, j)
            group(0)
            with dve.Fori(GROUP, SLOTS - 2 * GROUP + 1, GROUP) as t:
                group(t)
            group(SLOTS - GROUP)
            turned(SLOTS, 1)
            for b in range(TILES // NT):
                dve.wait_ge(s(f"y{b % len(Y01)}_loaded"), 16 * TOP * (b // len(Y01) + 1))
                tiles = T2[:, b * NT:b * NT + NT, :]
                tt(Y01[b % len(Y01)][0], Y01[b % len(Y01)][0], Y01[b % len(Y01)][1], ALU.add).then_inc(s("y_added"), 1)
                dve.wait_ge(s("y_added"), b + 1)
                tt(tiles, tiles, Y01[b % len(Y01)][0], ALU.add).then_inc(s("added"), 1)


def kernel(**inputs):
    import numpy as _np
    import concourse.bacc as _bacc
    from concourse import mybir as _mybir
    from concourse.bass_utils import run_bass_kernel_spmd as _run

    a = {name: _np.asarray(v) for name, v in inputs.items()}
    x = a["x"]
    batch, height, width, chans = x.shape
    tokens = x.reshape(batch, height * width, chans)
    ssm = {name: a["L1_attn_" + name] for name in
           ("W_in", "conv_w", "conv_b", "dt_bias", "A_log", "Dp", "gnorm_w", "norm_w", "W_out")}
    inner, conv_dim = ssm["gnorm_w"].shape[0], ssm["conv_b"].shape[0]
    w_in = ssm["W_in"]
    laid_out = {
        "x": tokens.reshape(-1, chans),
        "xT": tokens.transpose(0, 2, 1).reshape(batch * chans, height * width),
        **{name: a["L0_conv_" + name] for name in ("dw1", "pw1", "b1", "dw2", "pw2", "b2", "gamma")},
        "w_zdt": _np.concatenate([w_in[:inner], w_in[inner + conv_dim:]], 0).T,
        "w_xbc": w_in[inner:inner + conv_dim].T,
        "conv_w": ssm["conv_w"], "conv_b": ssm["conv_b"], "dt_bias": ssm["dt_bias"], "a_log": ssm["A_log"],
        "d_skip": ssm["Dp"], "gnorm_w": ssm["gnorm_w"], "norm_w": ssm["norm_w"],
        "w_outT": ssm["W_out"].T,
        "routerT": a["L1_ffn_router_w"].T,
        "w1T": a["L1_ffn_w1"].transpose(0, 2, 1),
        "w3T": a["L1_ffn_w3"].transpose(0, 2, 1),
        "w2T": a["L1_ffn_w2"].transpose(0, 2, 1),
    }
    nc = _bacc.Bacc("TRN2", target_bir_lowering=False, num_devices=1)
    arrays, args = {}, []
    for name, v in laid_out.items():
        v = _np.ascontiguousarray(v)
        arrays[f"in_{name}_dram"] = v
        args.append(nc.dram_tensor(f"in_{name}_dram", v.shape, _mybir.dt.from_np(v.dtype), kind="ExternalInput").ap())
    out = nc.dram_tensor("out_dram", (batch * height * width, chans), _mybir.dt.from_np(x.dtype), kind="ExternalOutput").ap()
    conv_attn_ssm_moe(nc, *args, out)
    r = _run(nc, [arrays], core_ids=[0])
    return r.results[0]["out_dram"].reshape(x.shape)
```
